# Optimizing a Trainium2 kernel written in Bass

```python
import numpy as np
import jax
import jax.numpy as jnp

def _softmax(x, axis=-1):
    return jax.nn.softmax(x, axis=axis)

def _gelu(x):
    return jax.nn.gelu(x, approximate=True)

def _silu(x):
    return jax.nn.silu(x)

def _sigmoid(x):
    return jax.nn.sigmoid(x)

def _layernorm(x, axis=-1, eps=1e-05):
    m = jnp.mean(x, axis=axis, keepdims=True)
    v = jnp.var(x, axis=axis, keepdims=True)
    return (x - m) / jnp.sqrt(v + eps)

def _scatter_add(tgt, idx, src, axis=0):
    return tgt.at[idx].add(src)

def _segment_sum(src, seg, n):
    return jax.ops.segment_sum(src, seg, n)
kernel_name = 'mk_decoder_postln_d2_seqx_r4_71c440'

def setup_inputs(seed: int=0):
    np.random.seed(seed)
    _w = jnp.asarray

    def _rec_inputs():
        import jax
        import jax.numpy as jnp
        _rk = jax.random.key(seed)
        x = -0.000125 + 0.9999 * jax.random.normal(jax.random.fold_in(_rk, 1), (8, 256, 256), jnp.float32)
        _lenS = 256 - jax.random.randint(jax.random.fold_in(_rk, 7), (8,), 0, max(1, 256 // 4) + 1, jnp.int32)
        _lenS2 = 77 - jax.random.randint(jax.random.fold_in(_rk, 8), (8,), 0, max(1, 77 // 4) + 1, jnp.int32)
        _ctx_768P = jax.random.normal(jax.random.fold_in(_rk, 11), (8, 16, 192), jnp.float32)
        _ctx_768c = jax.random.dirichlet(jax.random.fold_in(_rk, 511), 0.3 * jnp.ones((16,), jnp.float32), (8, 77))
        _ctx_768t = jnp.einsum('bsk,bkd->bsd', _ctx_768c, _ctx_768P)
        _ctx_768t = _ctx_768t * jax.lax.rsqrt(jnp.mean(jnp.square(_ctx_768t)) + 1e-12) * 0.953939
        ctx_768 = -5.15168e-05 + 0.999825 * (_ctx_768t + 0.3 * jax.random.normal(jax.random.fold_in(_rk, 611), (8, 77, 192), jnp.float32))
        return (x, ctx_768)
    x, ctx_768 = _rec_inputs()

    def _L0_attn_setup():
        import jax, jax.numpy as jnp
        import numpy as np
        B, T, D = (8, 1024, 256)
        key = jax.random.key(seed)
        k1, k2, k3, k4, k5 = jax.random.split(key, 5)
        s = 1.0 / np.sqrt(D)
        return {'seq': jax.random.normal(k1, (B, T, D), dtype=jnp.float32), 'W_delta': jax.random.uniform(k2, (D, D), jnp.float32, -s, s), 'b_delta': jax.random.uniform(k3, (D,), jnp.float32, -s, s), 'W_value': jax.random.uniform(k4, (D, D), jnp.float32, -s, s), 'b_value': jax.random.uniform(k5, (D,), jnp.float32, -s, s)}
    _L0_attn_all = _L0_attn_setup()
    _L0_attn_in = {k: v for k, v in _L0_attn_all.items() if k in ('W_delta', 'b_delta', 'W_value', 'b_value')}
    del _L0_attn_all

    def _L0_xattn_setup():
        import jax, jax.numpy as jnp
        import numpy as np
        Q_DIM, K_DIM, V_DIM, OUT_DIM = (256, 192, 192, 256)
        key = jax.random.key(seed)
        ks = jax.random.split(key, 9)
        s = lambda d: 1.0 / np.sqrt(d)
        return {'query': jax.random.normal(ks[0], (16, 512, Q_DIM), jnp.float32), 'key': jax.random.normal(ks[1], (16, 512, K_DIM), jnp.float32), 'value': jax.random.normal(ks[2], (16, 512, V_DIM), jnp.float32), 'Wq': jax.random.uniform(ks[3], (OUT_DIM, Q_DIM), jnp.float32, -s(Q_DIM), s(Q_DIM)), 'bq': jax.random.uniform(ks[4], (OUT_DIM,), jnp.float32, -s(Q_DIM), s(Q_DIM)), 'Wk': jax.random.uniform(ks[5], (OUT_DIM, K_DIM), jnp.float32, -s(K_DIM), s(K_DIM)), 'bk': jax.random.uniform(ks[6], (OUT_DIM,), jnp.float32, -s(K_DIM), s(K_DIM)), 'Wv': jax.random.uniform(ks[7], (OUT_DIM, V_DIM), jnp.float32, -s(V_DIM), s(V_DIM)), 'bv': jax.random.uniform(ks[8], (OUT_DIM,), jnp.float32, -s(V_DIM), s(V_DIM))}
    _L0_xattn_all = _L0_xattn_setup()
    _L0_xattn_in = {k: v for k, v in _L0_xattn_all.items() if k in ('Wq', 'bq', 'Wk', 'bk', 'Wv', 'bv')}
    del _L0_xattn_all

    def _L0_ffn_setup():
        import math
        import jax, jax.numpy as jnp
        import numpy as np
        B, T, H = (4, 512, 256)
        E, K, F = (8, 2, 512)
        CAP_FACTOR = 1.25

        def _moe_forward(x, Wg, W_in, W_out):
            b, t, h = x.shape
            xf = x.reshape(-1, h)
            S = xf.shape[0]
            C = int(math.ceil(K * S / E * CAP_FACTOR))
            logits = xf @ Wg
            probs = jax.nn.softmax(logits, axis=-1)
            top_vals, top_idx = jax.lax.top_k(probs, K)
            flat_idx = top_idx.T.reshape(-1)
            onehot = jax.nn.one_hot(flat_idx, E, dtype=jnp.int32)
            cum = jnp.cumsum(onehot, axis=0) - 1
            loc = jnp.take_along_axis(cum, flat_idx[:, None], axis=1)[:, 0]
            loc = loc.reshape(K, S).T
            keep = loc < C
            gates = top_vals * keep.astype(top_vals.dtype)
            denom = jnp.maximum(gates.sum(-1, keepdims=True), 1e-09)
            gates = gates / denom
            loc_c = jnp.where(keep, loc, C)
            e_flat = top_idx.reshape(-1)
            l_flat = loc_c.reshape(-1)
            xk = jnp.broadcast_to(xf[:, None, :], (S, K, h)).reshape(-1, h)
            xk = jnp.where(keep.reshape(-1, 1), xk, 0.0)
            buf = jnp.zeros((E, C + 1, h), x.dtype).at[e_flat, l_flat].set(xk)
            inp = buf[:, :C]
            hid = jnp.einsum('ech,ehf->ecf', inp, W_in)
            a, g = jnp.split(hid, 2, axis=-1)
            hid = jax.nn.gelu(a, approximate=False) * g
            out_e = jnp.einsum('ecf,efh->ech', hid, W_out)
            out_pad = jnp.concatenate([out_e, jnp.zeros((E, 1, h), out_e.dtype)], axis=1)
            gathered = out_pad[e_flat, l_flat].reshape(S, K, h)
            y = (gathered * gates[..., None]).sum(axis=1)
            return y.reshape(b, t, h)
        key = jax.random.key(seed)
        k1, k2, k3, k4 = jax.random.split(key, 4)
        x = jax.random.normal(k1, (B, T, H), dtype=jnp.float32)
        Wg = jax.random.normal(k2, (H, E), dtype=jnp.float32) * 0.02
        W_in = jax.random.normal(k3, (E, H, 2 * F), dtype=jnp.float32) * (1.0 / math.sqrt(H))
        W_out = jax.random.normal(k4, (E, F, H), dtype=jnp.float32) * (1.0 / math.sqrt(F))
        return {'x': x, 'Wg': Wg, 'W_in': W_in, 'W_out': W_out}
    _L0_ffn_all = _L0_ffn_setup()
    _L0_ffn_in = {k: v for k, v in _L0_ffn_all.items() if k in ('Wg', 'W_in', 'W_out')}
    del _L0_ffn_all

    def _L1_attn_setup():
        import jax, jax.numpy as jnp
        import numpy as np
        import math
        EMBED_DIM = 256
        NUM_HEADS = 16
        HEAD_DIM = EMBED_DIM // NUM_HEADS
        T, N = (256, 8)
        key = jax.random.key(seed)
        k1, k2, k3, k4 = jax.random.split(key, 4)
        scale = 0.02
        x = jax.random.normal(k1, (T, N, EMBED_DIM), dtype=jnp.float32)
        q_weight = jax.random.normal(k2, (EMBED_DIM, NUM_HEADS, HEAD_DIM), dtype=jnp.float32) * scale
        v_weight = jax.random.normal(k3, (EMBED_DIM, NUM_HEADS, HEAD_DIM), dtype=jnp.float32) * scale
        out_w = jax.random.normal(k4, (EMBED_DIM, EMBED_DIM), dtype=jnp.float32) * scale
        out_b = jnp.zeros((EMBED_DIM,), dtype=jnp.float32)
        return {'x': x, 'q_weight': q_weight, 'v_weight': v_weight, 'out_w': out_w, 'out_b': out_b}
    _L1_attn_all = _L1_attn_setup()
    _L1_attn_in = {k: v for k, v in _L1_attn_all.items() if k in ('q_weight', 'v_weight', 'out_w', 'out_b')}
    del _L1_attn_all

    def _L1_xattn_setup():
        import jax, jax.numpy as jnp
        import numpy as np
        IMG_DIM, TXT_DIM, HID = (256, 192, 256)
        B, LQ, LK = (8, 512, 512)
        key = jax.random.key(seed)
        ks = jax.random.split(key, 8)
        s_img = 1.0 / np.sqrt(IMG_DIM)
        s_txt = 1.0 / np.sqrt(TXT_DIM)
        return {'image_features': jax.random.normal(ks[0], (B, LQ, IMG_DIM), jnp.float32), 'text_features': jax.random.normal(ks[1], (B, LK, TXT_DIM), jnp.float32), 'Wq': jax.random.uniform(ks[2], (IMG_DIM, HID), jnp.float32, -s_img, s_img), 'bq': jax.random.uniform(ks[3], (HID,), jnp.float32, -s_img, s_img), 'Wk': jax.random.uniform(ks[4], (TXT_DIM, HID), jnp.float32, -s_txt, s_txt), 'bk': jax.random.uniform(ks[5], (HID,), jnp.float32, -s_txt, s_txt), 'Wv': jax.random.uniform(ks[6], (TXT_DIM, HID), jnp.float32, -s_txt, s_txt), 'bv': jax.random.uniform(ks[7], (HID,), jnp.float32, -s_txt, s_txt)}
    _L1_xattn_all = _L1_xattn_setup()
    _L1_xattn_in = {k: v for k, v in _L1_xattn_all.items() if k in ('Wq', 'bq', 'Wk', 'bk', 'Wv', 'bv')}
    del _L1_xattn_all

    def _L1_ffn_setup():
        import jax, jax.numpy as jnp
        import numpy as np
        CHUNK = 128
        NUM_BITS = 6
        key = jax.random.key(seed)
        k1, k2, k3 = jax.random.split(key, 3)
        B, L, D, E = (4, 1024, 256, 64)
        x = jax.random.normal(k1, (B, L, D), dtype=jnp.float32)
        expert_weights = jax.random.normal(k2, (E, D, D), dtype=jnp.float32) * 0.02
        hyperplanes = jax.random.normal(k3, (D, NUM_BITS), dtype=jnp.float32)
        return {'x': x, 'expert_weights': expert_weights, 'hyperplanes': hyperplanes}
    _L1_ffn_all = _L1_ffn_setup()
    _L1_ffn_in = {k: v for k, v in _L1_ffn_all.items() if k in ('expert_weights', 'hyperplanes')}
    del _L1_ffn_all
    return {'x': x, 'ctx_768': ctx_768, 'L0_attn_W_delta': _L0_attn_in['W_delta'], 'L0_attn_b_delta': _L0_attn_in['b_delta'], 'L0_attn_W_value': _L0_attn_in['W_value'], 'L0_attn_b_value': _L0_attn_in['b_value'], 'L0_xattn_Wq': _L0_xattn_in['Wq'], 'L0_xattn_bq': _L0_xattn_in['bq'], 'L0_xattn_Wk': _L0_xattn_in['Wk'], 'L0_xattn_bk': _L0_xattn_in['bk'], 'L0_xattn_Wv': _L0_xattn_in['Wv'], 'L0_xattn_bv': _L0_xattn_in['bv'], 'L0_ffn_Wg': _L0_ffn_in['Wg'], 'L0_ffn_W_in': _L0_ffn_in['W_in'], 'L0_ffn_W_out': _L0_ffn_in['W_out'], 'L1_attn_q_weight': _L1_attn_in['q_weight'], 'L1_attn_v_weight': _L1_attn_in['v_weight'], 'L1_attn_out_w': _L1_attn_in['out_w'], 'L1_attn_out_b': _L1_attn_in['out_b'], 'L1_xattn_Wq': _L1_xattn_in['Wq'], 'L1_xattn_bq': _L1_xattn_in['bq'], 'L1_xattn_Wk': _L1_xattn_in['Wk'], 'L1_xattn_bk': _L1_xattn_in['bk'], 'L1_xattn_Wv': _L1_xattn_in['Wv'], 'L1_xattn_bv': _L1_xattn_in['bv'], 'L1_ffn_expert_weights': _L1_ffn_in['expert_weights'], 'L1_ffn_hyperplanes': _L1_ffn_in['hyperplanes']}

def reference(x, ctx_768, L0_attn_W_delta, L0_attn_b_delta, L0_attn_W_value, L0_attn_b_value, L0_xattn_Wq, L0_xattn_bq, L0_xattn_Wk, L0_xattn_bk, L0_xattn_Wv, L0_xattn_bv, L0_ffn_Wg, L0_ffn_W_in, L0_ffn_W_out, L1_attn_q_weight, L1_attn_v_weight, L1_attn_out_w, L1_attn_out_b, L1_xattn_Wq, L1_xattn_bq, L1_xattn_Wk, L1_xattn_bk, L1_xattn_Wv, L1_xattn_bv, L1_ffn_expert_weights, L1_ffn_hyperplanes):
    import jax
    import jax.numpy as jnp

    def _L0_attn_ref(seq, W_delta, b_delta, W_value, b_value):
        import jax, jax.numpy as jnp
        import numpy as np
        B, T, D = (8, 1024, 256)
        delta = jax.nn.sigmoid(jnp.einsum('btd,ed->bte', seq, W_delta) + b_delta)
        value = jnp.einsum('btd,ed->bte', seq, W_value) + b_value

        def step(state, dv):
            d, v = dv
            state = (1.0 - d) * state + d * v
            return (state, state)
        init = jnp.zeros((seq.shape[0], seq.shape[-1]), dtype=seq.dtype)
        _, out = jax.lax.scan(step, init, (delta.transpose(1, 0, 2), value.transpose(1, 0, 2)))
        return out.transpose(1, 0, 2)

    def _L0_xattn_ref(query, key, value, Wq, bq, Wk, bk, Wv, bv):
        import jax, jax.numpy as jnp
        import numpy as np
        Q_DIM, K_DIM, V_DIM, OUT_DIM = (256, 192, 192, 256)
        scale = OUT_DIM ** (-0.5)
        q = jnp.einsum('bsd,od->bso', query, Wq) + bq
        k = jnp.einsum('bsd,od->bso', key, Wk) + bk
        v = jnp.einsum('bsd,od->bso', value, Wv) + bv
        scores = jnp.einsum('bqo,bko->bqk', q, k) * scale
        probs = jax.nn.softmax(scores, axis=-1)
        return jnp.einsum('bqk,bko->bqo', probs, v)

    def _L0_ffn_ref(x, Wg, W_in, W_out):
        import math
        import jax, jax.numpy as jnp
        import numpy as np
        B, T, H = (4, 512, 256)
        E, K, F = (8, 2, 512)
        CAP_FACTOR = 1.25

        def _moe_forward(x, Wg, W_in, W_out):
            b, t, h = x.shape
            xf = x.reshape(-1, h)
            S = xf.shape[0]
            C = int(math.ceil(K * S / E * CAP_FACTOR))
            logits = xf @ Wg
            probs = jax.nn.softmax(logits, axis=-1)
            top_vals, top_idx = jax.lax.top_k(probs, K)
            flat_idx = top_idx.T.reshape(-1)
            onehot = jax.nn.one_hot(flat_idx, E, dtype=jnp.int32)
            cum = jnp.cumsum(onehot, axis=0) - 1
            loc = jnp.take_along_axis(cum, flat_idx[:, None], axis=1)[:, 0]
            loc = loc.reshape(K, S).T
            keep = loc < C
            gates = top_vals * keep.astype(top_vals.dtype)
            denom = jnp.maximum(gates.sum(-1, keepdims=True), 1e-09)
            gates = gates / denom
            loc_c = jnp.where(keep, loc, C)
            e_flat = top_idx.reshape(-1)
            l_flat = loc_c.reshape(-1)
            xk = jnp.broadcast_to(xf[:, None, :], (S, K, h)).reshape(-1, h)
            xk = jnp.where(keep.reshape(-1, 1), xk, 0.0)
            buf = jnp.zeros((E, C + 1, h), x.dtype).at[e_flat, l_flat].set(xk)
            inp = buf[:, :C]
            hid = jnp.einsum('ech,ehf->ecf', inp, W_in)
            a, g = jnp.split(hid, 2, axis=-1)
            hid = jax.nn.gelu(a, approximate=False) * g
            out_e = jnp.einsum('ecf,efh->ech', hid, W_out)
            out_pad = jnp.concatenate([out_e, jnp.zeros((E, 1, h), out_e.dtype)], axis=1)
            gathered = out_pad[e_flat, l_flat].reshape(S, K, h)
            y = (gathered * gates[..., None]).sum(axis=1)
            return y.reshape(b, t, h)
        return _moe_forward(x, Wg, W_in, W_out)

    def _L1_attn_ref(x, q_weight, v_weight, out_w, out_b):
        import jax, jax.numpy as jnp
        import numpy as np
        import math
        EMBED_DIM = 256
        NUM_HEADS = 16
        HEAD_DIM = EMBED_DIM // NUM_HEADS
        T, N = (256, 8)
        head_dim = q_weight.shape[-1]
        inv_sqrt_d = 1.0 / math.sqrt(head_dim)
        q = jnp.einsum('tbm,mhd->tbhd', x, q_weight)
        k = q
        q_sq = jnp.einsum('tbhd,tbhd->tbh', q, q)
        k_sq = jnp.einsum('sbhd,sbhd->sbh', k, k)
        qk = jnp.einsum('tbhd,sbhd->tsbh', q, k)
        squared_dist = q_sq[:, None] + k_sq[None, :] - 2.0 * qk
        attn_logits = -squared_dist * inv_sqrt_d
        attn_weights = jax.nn.softmax(attn_logits, axis=1)
        A = jnp.einsum('mhd,nhd->hmn', q_weight, q_weight) * inv_sqrt_d
        XA = jnp.einsum('tbm,hmn->tbhn', x, A)
        PXA = jnp.einsum('tsbh,sbhm->tbhm', attn_weights, XA)
        Tn, Bn = (x.shape[0], x.shape[1])
        PXAV = jnp.einsum('tbhm,mhd->tbhd', PXA, v_weight).reshape(Tn, Bn, -1)
        return PXAV @ out_w.T + out_b

    def _L1_xattn_ref(image_features, text_features, Wq, bq, Wk, bk, Wv, bv):
        import jax, jax.numpy as jnp
        import numpy as np
        IMG_DIM, TXT_DIM, HID = (256, 192, 256)
        B, LQ, LK = (8, 512, 512)
        query = jnp.einsum('bqi,ih->bqh', image_features, Wq) + bq
        key = jnp.einsum('bkt,th->bkh', text_features, Wk) + bk
        value = jnp.einsum('bkt,th->bkh', text_features, Wv) + bv
        scale = 1.0 / jnp.sqrt(jnp.asarray(HID, query.dtype))
        scores = jnp.einsum('bqh,bkh->bqk', query, key) * scale
        weights = jax.nn.softmax(scores, axis=-1)
        attended = jnp.einsum('bqk,bkh->bqh', weights, value)
        return attended

    def _L1_ffn_ref(x, expert_weights, hyperplanes):
        import jax, jax.numpy as jnp
        import numpy as np
        CHUNK = 128
        NUM_BITS = 6
        B, L, D = x.shape
        C = L // CHUNK
        xr = x.reshape(B, C, CHUNK, D)
        chunk_emb = xr.mean(axis=2)
        proj = chunk_emb @ hyperplanes
        bits = (proj > 0).astype(jnp.int32)
        powers = (2 ** jnp.arange(NUM_BITS)).astype(jnp.int32)
        e1 = jnp.sum(bits * powers, axis=-1)
        weakest = jnp.argmin(jnp.abs(proj), axis=-1)
        flip = (2 ** weakest).astype(jnp.int32)
        e2 = jnp.bitwise_xor(e1, flip)
        out = jnp.zeros_like(xr)
        for idx in (e1, e2):
            w = expert_weights[idx]
            out = out + jnp.einsum('bcld,bcde->bcle', xr, w)
        out = out * 0.5
        return out.reshape(B, L, D)
    x = _layernorm(x + _L0_attn_ref(x, L0_attn_W_delta, L0_attn_b_delta, L0_attn_W_value, L0_attn_b_value), axis=-1)
    x = _layernorm(x + _L0_xattn_ref(x, ctx_768, ctx_768, L0_xattn_Wq, L0_xattn_bq, L0_xattn_Wk, L0_xattn_bk, L0_xattn_Wv, L0_xattn_bv), axis=-1)
    x = _layernorm(x + _L0_ffn_ref(x, L0_ffn_Wg, L0_ffn_W_in, L0_ffn_W_out), axis=-1)
    x = _layernorm(x + _L1_attn_ref(x, L1_attn_q_weight, L1_attn_v_weight, L1_attn_out_w, L1_attn_out_b), axis=-1)
    x = _layernorm(x + _L1_xattn_ref(x, ctx_768, L1_xattn_Wq, L1_xattn_bq, L1_xattn_Wk, L1_xattn_bk, L1_xattn_Wv, L1_xattn_bv), axis=-1)
    x = _layernorm(x + _L1_ffn_ref(x, L1_ffn_expert_weights, L1_ffn_hyperplanes), axis=-1)
    return x

_drawn_inputs = setup_inputs


def setup_inputs(seed=0):
    import zlib

    import numpy as np

    out = dict(_drawn_inputs(seed))
    spreads = {'L1_attn_out_b': (0.0, 0.273)}
    factors = {'L0_xattn_bq': 3.242,
     'L0_xattn_bk': 64.0,
     'L1_attn_q_weight': 8.0,
     'L1_attn_v_weight': 8.0,
     'L1_attn_out_w': 8.0,
     'L1_xattn_bq': 8.0,
     'L1_xattn_bk': 64.0}
    for name, (base, spread) in spreads.items():
        noise = np.random.default_rng([zlib.crc32(name.encode()), seed]).standard_normal(out[name].shape)
        drawn = base * np.exp(spread * noise) if base else spread * noise
        out[name] = jnp.asarray(drawn.astype(out[name].dtype))
    for name, factor in factors.items():
        out[name] = (out[name] * factor).astype(out[name].dtype)
    return out
```

```python
from contextlib import ExitStack

import numpy as np

import concourse.bass as bass
import concourse.mybir as mybir

F32 = mybir.dt.float32
BF16 = mybir.dt.bfloat16
I32 = mybir.dt.int32
ALU = mybir.AluOpType
ACT = mybir.ActivationFunctionType
AX = mybir.AxisListType

P = 128
B = 8
T = 256
D = 256
DC = D // P
S = B * T
NT = S // P
TK = 77
CD = 192
CK = CD // 2
E0 = 8
F0 = 512
CAP = 640
ET = CAP // P
NST = E0 * ET
HALF = CAP // 2
NH = 16
HD = 16
NB6 = 6
EPS = 1e-5
BIG = 8192.0

_CF = {}
_n = 0
for _name, _w in (("ident", P), ("bmask", P), ("iota", P), ("w8", NT * E0), ("smask", 2 * NT * E0),
                  ("acon", 2 * NT), ("pcol", 1), ("sel0", P), ("ones", P), ("w6", 2 * NB6), ("p6", 2 * NB6),
                  ("negh", 2)):
    _CF[_name] = (_n, _n + _w)
    _n += _w
CFW = _n


def shape_constants():
    c = np.zeros((P, CFW), np.float32)

    def put(name, v):
        a, b = _CF[name]
        c[:, a:b] = v
    put("ident", np.eye(P))
    put("bmask", np.kron(np.eye(P // HD), np.ones((HD, HD))) * HD ** -0.5)
    put("iota", np.arange(P)[None, :])
    put("w8", np.tile(E0 - np.arange(E0), NT)[None, :])
    m = np.ones((E0, 2 * NT))
    m[:, 0] = 0
    put("smask", m.reshape(1, -1))
    put("acon", (P * np.arange(2 * NT))[None, :])
    put("pcol", np.arange(P)[:, None])
    s0 = np.zeros((P, P))
    s0[0] = 1
    put("sel0", s0)
    put("ones", 1.0)
    put("w6", np.tile(NB6 - np.arange(NB6), 2)[None, :])
    put("p6", np.tile(2.0 ** np.arange(NB6), 2)[None, :])
    put("negh", -0.5)
    return c


def program(nc, A, out, Y, X2):
    ctx = ExitStack()
    with ctx:
        def sb(name, shape, dt=F32):
            return ctx.enter_context(nc.sbuf_tensor("sb_" + name, shape, dt))

        def sem(name):
            return ctx.enter_context(nc.semaphore(name))

        cf = sb("cf", [P, CFW])
        C = {k: cf[:, a:b] for k, (a, b) in _CF.items()}
        ident = C["ident"]
        ltri = sb("ltri", [P, P], BF16)
        onesb = sb("onesb", [P, P], BF16)
        xt = sb("xt", [P, NT, D])
        wdv = sb("wdv", [P, 2 * DC * D])
        wd, wv = (wdv[:, i * DC * D:(i + 1) * DC * D].rearrange("p (c n) -> p c n", c=DC) for i in range(2))
        bdv = sb("bdv", [P, 2, DC])
        bq = [sb(f"bq{l}", [P, DC]) for l in range(2)]
        Ga = [sb(f"G{l}", [P, DC * B * TK]) for l in range(2)]
        G = [a[:].rearrange("p (c n) -> p c n", c=DC) for a in Ga]
        bqk = [sb(f"bqk{l}", [P, B * TK]) for l in range(2)]
        vxa = [sb(f"vx{l}", [P, B * D]) for l in range(2)]
        vx = [a[0:TK, :].rearrange("p (b n) -> p b n", b=B) for a in vxa]
        wg = sb("wg", [P, DC, E0])
        qw = sb("qw", [P, DC, D])
        quw = sb("quw", [P, DC, 2 * D])
        woT = sb("woT", [P, DC, D])
        obr = sb("obr", [P, D])
        hyp = sb("hyp", [P, DC, NB6])
        big = sb("big", [P, 21504])
        def view(a, c, n=None, parts=P):
            return big[0:parts, a:a + c * n].rearrange("p (c n) -> p c n", c=c)
        kf = view(10240, DC, B * TK)
        wk = [view(11520 + l * 512, 2, D, CK + 1) for l in range(2)]
        wvx = [view(12544 + l * 512, 2, D, CK + 1) for l in range(2)]
        wq = [view(13568 + l * 512, DC, D) for l in range(2)]
        bqb = [view(14592 + l * 256, DC, P) for l in range(2)]
        bd = view(15104, DC, P)
        qwT = view(15360, DC, D)
        vw = view(15872, DC, D)
        cx = view(16384, 2, B * TK, CK + 1)
        zero = big[:, 20480:21504]
        xf = big[:, 0:4096].rearrange("p (c t) -> p c t", c=DC)
        WI, WO = 2048, 1024
        win = [big[:, 4096 + i * 3072:4096 + i * 3072 + 2048].rearrange("p (c f) -> p c f", c=DC) for i in range(2)]
        wou = [big[:, 4096 + i * 3072 + 2048:4096 + (i + 1) * 3072].rearrange("p (c f) -> p c f", c=F0 // P) for i in range(2)]
        inpT = [big[:, 10240 + i * 1280:10240 + (i + 1) * 1280].rearrange("p (j n) -> p j n", j=ET) for i in range(2)]
        inpF = [big[:, 12800 + i * 1280:12800 + (i + 1) * 1280].rearrange("p (c n) -> p c n", c=DC) for i in range(2)]
        hid = big[:, 15360:15360 + 2560].rearrange("p (c n) -> p c n", c=F0 // P)
        ge = [big[:, 17920 + i * 320:17920 + (i + 1) * 320] for i in range(2)]
        oe = [big[:, 18560 + i * 256:18560 + (i + 1) * 256] for i in range(4)]
        rA = big[:, 0:4096]
        qa = big[:, 0:2048].rearrange("p (t n) -> p t n", t=B)
        ua = big[:, 2048:4096].rearrange("p (t n) -> p t n", t=B)
        ua2 = big[:, 4096:6144].rearrange("p (t n) -> p t n", t=B)
        qa2 = big[:, 6144:8192].rearrange("p (t n) -> p t n", t=B)
        dif = big[:, 8192:8192 + 7168]
        att = [big[:, 15360 + i * 1024:15360 + (i + 1) * 1024] for i in range(2)]
        prod = [big[:, 17408 + i * 2048:17408 + (i + 1) * 2048].rearrange("p (s n) -> p s n", s=B) for i in range(2)]
        ph = sb("ph", [P, 4 * DC * T])
        d1, a1, dv1, hs = (ph[:, i * DC * T:(i + 1) * DC * T].rearrange("p (c n) -> p c n", c=DC) for i in range(4))
        y1 = [sb(f"y1{i}", [P, DC, T]) for i in range(2)]
        xs = [sb(f"xs{i}", [P, 2, D]) for i in range(2)]
        xsf = [sb(f"xsf{i}", [P, DC, T]) for i in range(2)]
        x2f = [sb(f"x2f{i}", [P, DC, T]) for i in range(2)]
        pr = [sb(f"pr{i}", [P, 2, TK]) for i in range(2)]
        pt = [sb(f"pt{i}", [TK, T]) for i in range(2)]
        y2 = [sb(f"y2{i}", [P, 2, D]) for i in range(2)]
        st = {k: sb(f"st{k}", [P, 2, 2, 6]) for k in range(6)}
        mv = {k: sb(f"mv{k}", [P, 2, 2, 2]) for k in range(6)}
        ve = {k: sb(f"ve{k}", [P, 2, 2]) for k in range(6)}
        rs = {k: sb(f"rs{k}", [P, 2, 2]) for k in range(6)}
        nb = {k: sb(f"nb{k}", [P, 2, 2]) for k in range(6)}
        nm = sb("nm", [P, 2, 2])
        sm = sb("sm", [P, 2, 2])
        rc = sb("rc", [P, 2, 2])
        bk = [ctx.enter_context(nc.psum_tensor(f"bank{i}", [P, 512], F32)) for i in range(8)]

        sems = {}

        def q(name):
            if name not in sems:
                sems[name] = sem(name)
            return sems[name]

        NSETUP = 27
        def tiles_of(m):
            g, i = m // 4, m % 4
            return [2 * (2 * i) + g, 2 * (2 * i + 1) + g]

        yb = [ph[:, i * 4 * D:(i + 1) * 4 * D].rearrange("p (h k n) -> p h k n", h=2, k=2) for i in range(2)]
        y6 = [Ga[0][:, i * 2 * D:(i + 1) * 2 * D].rearrange("p (h n) -> p h n", h=2) for i in range(2)]
        y4 = [sb(f"y4{i}", [P, 2, D]) for i in range(2)]
        x4f = [sb(f"x4f{i}", [P, DC, T]) for i in range(2)]
        aof = [bqk[0][:, i * 2 * P:(i + 1) * 2 * P].rearrange("p (c n) -> p c n", c=DC) for i in range(2)]
        x5s = [sb(f"x5s{i}", [P, 2, D]) for i in range(2)]
        x5f = [sb(f"x5f{i}", [P, DC, T]) for i in range(2)]
        ws = [wdv[:, i * 2 * D:(i + 1) * 2 * D] for i in range(2)]
        we = [vxa[0][:, i * 4 * D:(i + 1) * 4 * D].rearrange("p (k n) -> p k n", k=2) for i in range(2)]
        idx = sb("idx", [P, 2, NST], I32)
        gate = sb("gate", [P, 2, NT])
        widx = [sb(f"widx{i}", [P, 4], I32) for i in range(2)]
        emb = sb("emb", [P, DC, 2])
        eh = sb("eh", [P, DC, 2, NB6])
        rt = sb("rt", [P, 12, 2 * NB6])
        rz = sb("rz", [P, B, NH])
        zz = sb("zz", [P, B, NH])

        bh = sb("bh", [P, DC])
        y6b, y3 = x2f, y1
        xbs = sb("xbs", [P, 2, D])
        OFF = {}
        o = 0
        for r in range(1, B):
            OFF[r] = o
            o += (B - r) * D
        dsq = sb("dsq", [P, 28, NH])

        def dsv(r):
            a = OFF[r] // D
            return dsq[:, a:a + B - r, :]

        def pair(a, r, mirrored):
            start = r * (B * NH if mirrored else NH)
            v = a[:, start:start + (B - r - 1) * (B * NH + NH) + NH]
            return bass.AP(v.tensor, v.offset, [v.ap[0], [B * NH + NH, B - r], [1, NH]])

        rMb_t = sb("rMb", [P, 2 * NT * E0], BF16)
        rMb = rMb_t[:]
        ohl = big[:, 12800:12800 + 2048].bitcast(BF16).rearrange("p (n c) -> p n c", n=2 * NT)
        ohh = big[:, 14848:14848 + 1920].bitcast(BF16).rearrange("p (n c) -> p n c", n=2 * NT)

        sb_small = sb("small", [P, 12, 2 * NT])
        sb_tab = sb("tab_s", [P, 240])

        block = ctx.enter_context(nc.Block())

        @block.sync
        def _(sp):
            xr = A["xT"].rearrange("(c p) t -> p c t", p=P)
            sp.dma_start(xf[:, :, 0:T], xr[:, :, 0:T]).then_inc(q("in_x0"), 16)
            for n, w in (("Wd", wd), ("Wv", wv)):
                sp.dma_start(w[:, :, :], A[n].rearrange("(c p) e -> p c e", p=P)).then_inc(q("in_a"), 16)
            sp.dma_start(bdv[:], A["bdv"]).then_inc(q("in_a"), 16)
            sp.dma_start(xf[:, :, T:2 * T], xr[:, :, T:2 * T]).then_inc(q("in_x1"), 16)
            sp.dma_start(xf[:, :, 2 * T:], xr[:, :, 2 * T:]).then_inc(q("in_x2"), 16)
            for l in range(2):
                sp.dma_start(wvx[l][0:CK, :, :], A[f"Wvx{l}"].rearrange("(c p) e -> p c e", p=CK)).then_inc(q("in_k"), 16)
                sp.dma_start(wvx[l][CK:CK + 1, 1, :], A[f"bvx{l}"]).then_inc(q("in_k"), 16)
                sp.dma_start(wq[l], A[f"Wq{l}"].rearrange("(c p) e -> p c e", p=P)).then_inc(q("in_k"), 16)
                sp.dma_start(bq[l][:], A[f"bq{l}"]).then_inc(q("in_k"), 16)
            sp.dma_start(wg[:], A["Wg"].rearrange("(c p) e -> p c e", p=P)).then_inc(q("in_k"), 16)
            for n, w in (("qw", qw), ("qwT", qwT), ("vw", vw), ("woT", woT)):
                sp.dma_start(w[:, :, :], A[n].rearrange("(c p) e -> p c e", p=P)).then_inc(q("in_w"), 16)
            sp.dma_start(obr[:], A["obr"]).then_inc(q("in_w"), 16)
            sp.dma_start(hyp[:], A["hyp"].rearrange("(p j) k -> p j k", j=DC)).then_inc(q("in_w"), 16)

            sp.wait_ge(q("zero"), 1)
            yz = Y.rearrange("(p r) n -> p (r n)", p=P)
            for i in range(8):
                sp.dma_start(yz[:, i * 1024:(i + 1) * 1024], zero).then_inc(q("yz"), 16)

            def load_expert(e):
                if e >= 2:
                    sp.wait_ge(q("mm2"), ET * (e - 1))
                sp.dma_start(win[e % 2], A["W_in"][e].rearrange("(c p) f -> p c f", p=P)).then_inc(q(f"in_e{e % 2}"), 16)
                sp.dma_start(wou[e % 2], A["W_out"][e].rearrange("(c p) f -> p c f", p=P)).then_inc(q(f"in_e{e % 2}"), 16)
            load_expert(0)
            load_expert(1)
            for b in range(B):
                sp.wait_ge(q("n2"), b + 1)
                sp.dma_start(X2[b * T:(b + 1) * T, :].rearrange("(h p) n -> p h n", p=P), xt[:, 2 * b:2 * b + 2, :]).then_inc(q("x2d"), 16)
            for e in range(2, E0):
                load_expert(e)
            for m in range(8):
                if m == 0:
                    for r in range(4):
                        sp.wait_ge(q(f"sc{r}"), 16 * NST // 4)
                    sp.wait_ge(q("yz"), 128)
                if m >= 2:
                    sp.wait_ge(q("y3"), m - 1)
                for h, n in enumerate(tiles_of(m)):
                    src = Y.rearrange("(k n p) d -> n p k d", k=2, p=P)[n]
                    sp.dma_start(yb[m % 2][:, h, :, :], src).then_inc(q(f"yl{m % 2}"), 16)
            for m in range(8):
                sp.wait_ge(q("n6"), m + 1)
                for h, n in enumerate(tiles_of(m)):
                    sp.dma_start(out[n // 2, (n % 2) * P:(n % 2 + 1) * P, :], y6[m % 2][:, h, :]).then_inc(q(f"od{m % 2}"), 16)
            for r in range(2):
                sp.wait_ge(q(f"od{r}"), 128)

        @block.gpsimd
        def _(pool):
            pool.memset(zero, 0.0).then_inc(q("zero"), 1)

            def power(k, m, n):
                pool.wait_ge(q(f"ve{k}"), m + 1)
                pool.tensor_tensor(rs[k][:, m % 2, :], ve[k][:, m % 2, :], C["negh"], ALU.pow).then_inc(q(f"rs{k}"), 1)
            pool.wait_ge(q("in_c"), 48)
            for s in range(B + 1):
                if s < B:
                    power(0, s, 0)
                if s >= 1:
                    power(1, s - 1, 0)

            def gather(e):
                if e == 0:
                    pool.wait_ge(q("idx"), 1)
                    pool.wait_ge(q("x2d"), 16 * B)
                if e >= 2:
                    pool.wait_ge(q("ttr"), ET * (e - 1))
                for j in range(ET):
                    pool.indirect_dma_start(out=inpT[e % 2][:, j, :], out_offset=None, in_=X2[:, :],
                                            in_offset=bass.IndirectOffsetOnAxis(ap=idx[:, 0, e * ET + j:e * ET + j + 1], axis=0)
                                            ).then_inc(q(f"ga{e % 2}{j}"), 16)

            def scatter(e):
                for j in range(ET):
                    n = e * ET + j
                    if n == 0:
                        pool.wait_ge(q("yz"), 128)
                    pool.wait_ge(q("oe"), n + 1)
                    pool.indirect_dma_start(out=Y[:, :], out_offset=bass.IndirectOffsetOnAxis(ap=idx[:, 1, n:n + 1], axis=0),
                                            in_=oe[n % 4], in_offset=None, bounds_check=2 * S - 1, oob_is_err=False
                                            ).then_inc(q(f"sc{n % 4}"), 16)
            gather(0)
            for e in range(E0):
                if e + 1 < E0:
                    gather(e + 1)
                scatter(e)

            def chunk_weights(m):
                for h in range(2):
                    n = 2 * m + h
                    pool.wait_ge(q("widx"), m + 1)
                    if n >= 2:
                        pool.wait_ge(q("ws"), n - 1)
                    for k in range(2):
                        pool.indirect_dma_start(out=we[n % 2][:, k, :], out_offset=None, in_=A["EW"],
                                                in_offset=bass.IndirectOffsetOnAxis(ap=widx[m % 2][:, 2 * h + k:2 * h + k + 1], axis=0)
                                                ).then_inc(q(f"we{n % 2}"), 16)
            for m in range(4):
                power(2, m, 0)
            for s in range(8 + 2):
                if s < 8:
                    power(3, s, 0)
                if 1 <= s <= 8:
                    power(4, s - 1, 0)
                if 1 <= s <= 8:
                    chunk_weights(s - 1)
                if s >= 2:
                    power(5, s - 2, 0)
                if s < 4:
                    power(2, s + 4, 0)

        @block.scalar
        def _(act):
            act.dma_start(cf[:], A["cf"]).then_inc(q("in_c"), 16)
            act.dma_start(ltri[:], A["ltri"]).then_inc(q("in_c"), 16)
            act.dma_start(onesb[:], A["onesb"]).then_inc(q("in_c"), 16)
            act.dma_start(cx[0:CK, :, :], A["ctxT"].rearrange("(c p) t -> p c t", p=CK)).then_inc(q("in_cx"), 16)
            act.dma_start(cx[CK:CK + 1, 1, :], A["ones1"]).then_inc(q("in_cx"), 16)
            for l in range(2):
                act.dma_start(wk[l][0:CK, :, :], A[f"Wk{l}"].rearrange("(c p) e -> p c e", p=CK)).then_inc(q("in_cx"), 16)
                act.dma_start(wk[l][CK:CK + 1, 1, :], A[f"bk{l}"]).then_inc(q("in_cx"), 16)

            def keys(l):
                for c in range(DC):
                    for h in range(2):
                        n = l * 4 + c * 2 + h
                        act.wait_ge(q("kP"), n + 1)
                        if l == 1 and c == 0 and h == 0:
                            act.wait_ge(q("bqP"), 2)
                        act.activation(kf[:, c, h * 308:(h + 1) * 308], bk[n % 2][:, 0:308], ACT.Copy).then_inc(q("kE"), 1)
                for c in range(DC):
                    for h in range(2):
                        n = l * 4 + c * 2 + h
                        act.wait_ge(q("GP"), n + 1)
                        act.activation(G[l][:, c, h * 308:(h + 1) * 308], bk[2 + n % 2][:, 0:308], ACT.Copy, scale=1.0 / 16).then_inc(q("GE"), 1)
                for h in range(2):
                    n = l * 2 + h
                    act.wait_ge(q("bqP"), n + 1)
                    act.activation(bqk[l][:, h * 308:(h + 1) * 308], bk[4 + n % 2][:, 0:308], ACT.Copy, scale=1.0 / 16).then_inc(q("bqE"), 1)
                for b in range(B):
                    n = l * B + b
                    act.wait_ge(q("vP"), n + 1)
                    act.activation(vx[l][:, b, :], bk[6 + n % 2][0:TK, 0:D], ACT.Copy).then_inc(q("vE"), 1)
            keys(0)
            keys(1)
            act.wait_ge(q("UP"), 1)
            act.activation(quw[:, :, D:2 * D], bk[2][:].rearrange("p (c n) -> p c n", c=DC), ACT.Copy).then_inc(q("UE"), 1)
            act.activation(quw[:, :, 0:D], qw[:], ACT.Copy).then_inc(q("UE"), 1)

            def norm(k, m, src, dst, done, waits=()):
                act.wait_ge(q(f"nb{k}"), m + 1)
                for w, n in waits:
                    if n > 0:
                        act.wait_ge(q(w), n)
                for h in range(2):
                    i = act.activation(dst(h), src(h), ACT.Identity, bias=nb[k][:, m % 2, h:h + 1], scale=rs[k][:, m % 2, h:h + 1])
                i.then_inc(q(done), 1)

            def evac(dst, src, ready, n, done, waits=()):
                act.wait_ge(q(ready), n)
                for w, v in waits:
                    if v > 0:
                        act.wait_ge(q(w), v)
                act.activation(dst, src, ACT.Copy).then_inc(q(done), 1)

            for s in range(B + 2):
                if 1 <= s <= B:
                    b = s - 1
                    evac(xsf[b % 2][:].rearrange("p c t -> p (c t)"), bk[3][:], "x1T", b + 1, "x1f", [("scP", b - 1)])
                if s >= 2:
                    b = s - 2
                    evac(x2f[b % 2][:].rearrange("p c t -> p (c t)"), bk[4][:], "x2T", b + 1, "x2f", [("lg", b - 1)])
                if s < B:
                    act.wait_ge(q("z"), s + 1)
                    if s >= 1:
                        act.wait_ge(q("dv"), s)
                    for c in range(DC):
                        i = act.activation(d1[:, c, :], bk[0][:, c * T:(c + 1) * T], ACT.Tanh, bias=bh[:, c:c + 1], scale=0.5)
                    i.then_inc(q("d"), 1)
                if 1 <= s <= B:
                    b = s - 1
                    act.wait_ge(q("mx"), b + 1)
                    if b >= 2:
                        act.wait_ge(q("pT"), b - 1)
                    for h in range(2):
                        i = act.activation(pr[b % 2][:, h, :], bk[5][:, h * TK:(h + 1) * TK], ACT.Exp, bias=nm[:, b % 2, h:h + 1],
                                           accum_out=sm[:, b % 2, h:h + 1])
                    i.then_inc(q("ex"), 1)
                if s < B:
                    norm(0, s, lambda h: bk[2][:, h * D:(h + 1) * D], lambda h: xs[s % 2][:, h, :], "n1", [("y2", s - 1), ("x1T", s - 1)])
                if 1 <= s <= B:
                    b = s - 1
                    norm(1, b, lambda h: y2[b % 2][:, h, :], lambda h: xt[:, 2 * b + h, :], "n2")
            act.wait_ge(q("r1"), 1)
            act.activation(rA[:, 128:256], rA[:, 0:128], ACT.Exp).then_inc(q("r2"), 1)

            def inp_evac(e):
                for j in range(ET):
                    n = e * ET + j
                    act.wait_ge(q("ttr"), n + 1)
                    if e >= 2:
                        act.wait_ge(q("mm1"), 8 * (e - 1))
                    act.activation(inpF[e % 2][:, :, j * P:(j + 1) * P], bk[6 + n % 2][:, 0:D].rearrange("p (c t) -> p c t", c=DC),
                                   ACT.Copy).then_inc(q("ife"), 1)
            inp_evac(0)
            for e in range(E0):
                for u in range(8):
                    n = 8 * e + u
                    act.wait_ge(q("mm1"), n + 1)
                    if n >= 2:
                        act.wait_ge(q("hid"), n - 1)
                    act.activation(ge[n % 2], bk[n % 2][:, 0:HALF], ACT.Gelu).then_inc(q("ge"), 1)
                if e + 1 < E0:
                    inp_evac(e + 1)

            def lay1_front(m):
                norm(2, m, lambda h: y3[m % 2][:, h, :], lambda h: xt[:, tiles_of(m)[h], :], "n3")
                evac(xsf[m % 2][:].rearrange("p c t -> p (c t)"), bk[3][:], "x3T", m + 1, "x3f", [("qu", 2 * m - 2)])
                for h in range(2):
                    n = 2 * m + h
                    act.wait_ge(q("qu"), n + 1)
                    t = 2 * (m % 4) + h
                    g = m // 4
                    act.activation((qa, qa2)[g][:, t, :], bk[h][:, 0:D], ACT.Copy)
                    act.activation((ua, ua2)[g][:, t, :], bk[h][:, D:2 * D], ACT.Copy).then_inc(q("que"), 1)

            def distances(g):
                for r in range(1, B):
                    o = OFF[r]
                    n = (B - r) * D
                    act.wait_ge(q("dif"), 7 * g + r)
                    act.activation(dif[:, o:o + n], dif[:, o:o + n], ACT.Square).then_inc(q("sq"), 1)
                for r in range(1, B):
                    act.wait_ge(q("ds"), 7 * g + r)
                    act.activation(pair(att[g], r, False), dsv(r), ACT.Exp, scale=-HD ** -0.5).then_inc(q("e1"), 1)
            for m in range(4):
                lay1_front(m)
            for s in range(8 + 2):
                if s in (0, 4):
                    distances(s // 4)
                if 1 <= s <= 8:
                    b = s - 1
                    evac(x4f[b % 2][:].rearrange("p c t -> p (c t)"), bk[4][:], "x4T", b + 1, "x4f", [("scQ", b - 1)])
                if s < 8:
                    for h in range(2):
                        n = 2 * s + h
                        evac(aof[n % 2].rearrange("p c t -> p (c t)"), bk[2][:, h * 256:h * 256 + 256], "ao", n + 1, "aof", [("op", n - 1)])
                if 1 <= s <= 8:
                    act.wait_ge(q("mx2"), b + 1)
                    if b >= 2:
                        act.wait_ge(q("pT2"), b - 1)
                    for h in range(2):
                        i = act.activation(pr[b % 2][:, h, :], bk[5][:, h * TK:(h + 1) * TK], ACT.Exp, bias=nm[:, b % 2, h:h + 1],
                                           accum_out=sm[:, b % 2, h:h + 1])
                    i.then_inc(q("ex2"), 1)
                if s < 8:
                    norm(3, s, lambda h: y4[s % 2][:, h, :], lambda h: xs[s % 2][:, h, :], "n4", [("y5", s - 1), ("x4T", s - 1)])
                if 1 <= s <= 8:
                    b = s - 1
                    norm(4, b, lambda h: y2[b % 2][:, h, :], lambda h: x5s[b % 2][:, h, :], "n5", [("y6", b - 1)])
                    evac(x5f[b % 2][:].rearrange("p c t -> p (c t)"), bk[4][:], "x5T", b + 1, "x5f", [("fm", 2 * b - 2)])
                if s >= 2:
                    b = s - 2
                    norm(5, b, lambda h: y6b[b % 2][:, h, :], lambda h: y6[b % 2][:, h, :], "n6", [(f"od{b % 2}", 32 * (b // 2))])
                if s < 4:
                    lay1_front(s + 4)

        @block.tensor
        def _(pe):
            def tr4(dst, src, ready, n, done, waits=(), strided=False):
                pe.wait_ge(q(ready), n)
                for w, v in waits:
                    if v > 0:
                        pe.wait_ge(q(w), v)
                for a in range(2):
                    for c in range(2):
                        blk = src[:, a, c::2] if strided else src[:, a, c * P:(c + 1) * P]
                        i = pe.transpose(dst[:, c * 256 + a * P:c * 256 + (a + 1) * P], blk, ident)
                i.then_inc(q(done), 1)

            pe.wait_ge(q("in_cx"), 96)
            for l in range(2):
                if l == 0:
                    pe.wait_ge(q("in_k"), 144)
                    pe.wait_ge(q("in_c"), 48)
                for c in range(DC):
                    for h in range(2):
                        n = l * 4 + c * 2 + h
                        if n >= 2:
                            pe.wait_ge(q("kE"), n - 1)
                        for k in range(2):
                            r = CK + k
                            i = pe.matmul(bk[n % 2][:, 0:308], wk[l][0:r, k, c * P:(c + 1) * P], cx[0:r, k, h * 308:(h + 1) * 308],
                                          start=k == 0, stop=k == 1)
                        i.then_inc(q("kP"), 1)
                pe.wait_ge(q("kE"), 4 * l + 4)
                for c in range(DC):
                    for h in range(2):
                        n = l * 4 + c * 2 + h
                        if n >= 2:
                            pe.wait_ge(q("GE"), n - 1)
                        for k in range(DC):
                            i = pe.matmul(bk[2 + n % 2][:, 0:308], wq[l][:, k, c * P:(c + 1) * P], kf[:, k, h * 308:(h + 1) * 308],
                                          start=k == 0, stop=k == DC - 1)
                        i.then_inc(q("GP"), 1)
                pe.wait_ge(q("bqb"), l + 1)
                for h in range(2):
                    n = l * 2 + h
                    if n >= 2:
                        pe.wait_ge(q("bqE"), n - 1)
                    for k in range(DC):
                        i = pe.matmul(bk[4 + n % 2][:, 0:308], bqb[l][:, k, :], kf[:, k, h * 308:(h + 1) * 308], start=k == 0, stop=k == DC - 1)
                    i.then_inc(q("bqP"), 1)
                for b in range(B):
                    n = l * B + b
                    if n >= 2:
                        pe.wait_ge(q("vE"), n - 1)
                    for k in range(2):
                        r = CK + k
                        i = pe.matmul(bk[6 + n % 2][0:TK, 0:D], cx[0:r, k, b * TK:(b + 1) * TK], wvx[l][0:r, k, :], start=k == 0, stop=k == 1)
                    i.then_inc(q("vP"), 1)
            pe.wait_ge(q("in_w"), 96)
            pe.wait_ge(q("kE"), 8)
            for c in range(DC):
                for k in range(DC):
                    i = pe.matmul(bk[0][:, c * P:(c + 1) * P], qw[:, k, c * P:(c + 1) * P], vw[:, k, c * P:(c + 1) * P], start=k == 0, stop=k == DC - 1)
            i.then_inc(q("bdP"), 1)
            pe.wait_ge(q("bd"), 1)
            pe.wait_ge(q("GE"), 8)
            for c in range(DC):
                for h in range(DC):
                    i = pe.matmul(bk[2][:, c * D + h * P:c * D + (h + 1) * P], qwT[:, h, c * P:(c + 1) * P], bd[:, h, :], start=True, stop=True)
            i.then_inc(q("UP"), 1)
            pe.wait_ge(q("UE"), 2)
            pe.wait_ge(q("vE"), 16)
            pe.wait_ge(q("bqE"), 4)

            def scores(l, b, xfm, ready, free, done, seqs):
                pe.wait_ge(q(ready), b + 1)
                if b >= 1:
                    pe.wait_ge(q(free), b)
                for h in range(2):
                    cs = slice(seqs[h] * TK, (seqs[h] + 1) * TK)
                    for k in range(DC):
                        pe.matmul(bk[5][:, h * TK:(h + 1) * TK], xfm[:, k, h * P:(h + 1) * P], G[l][:, k, cs], start=k == 0, stop=False)
                    i = pe.matmul(bk[5][:, h * TK:(h + 1) * TK], C["sel0"], bqk[l][:, cs], start=False, stop=True)
                i.then_inc(q(done), 1)

            def probs_tr(b, ready, free, done):
                pe.wait_ge(q(ready), b + 1)
                if b >= 1:
                    pe.wait_ge(q(free), b)
                for h in range(2):
                    i = pe.transpose(bk[6][0:TK, h * P:(h + 1) * P], pr[b % 2][:, h, :], ident)
                i.then_inc(q(done), 1)

            def values(l, b, ready, free, done, seqs):
                pe.wait_ge(q(ready), b + 1)
                if b >= 1:
                    pe.wait_ge(q(free), b)
                for h in range(2):
                    i = pe.matmul(bk[7][:, h * D:(h + 1) * D], pt[b % 2][:, h * P:(h + 1) * P], vx[l][:, seqs[h], :], start=True, stop=True)
                i.then_inc(q(done), 1)

            for s in range(B + 2):
                if 1 <= s <= B:
                    b = s - 1
                    tr4(bk[3], xs[b % 2], "n1", b + 1, "x1T", [("x1f", b)])
                if s >= 2:
                    b = s - 2
                    tr4(bk[4], xt[:, 2 * b:2 * b + 2, :], "n2", b + 1, "x2T", [("x2f", b)])
                if s < B:
                    if s < 3:
                        pe.wait_ge(q(f"in_x{s}"), 16)
                    if s == 0:
                        pe.wait_ge(q("in_a"), 48)
                    for w, bank, done, free in ((wd, 0, "z", "d"), (wv, 1, "v", "dv")):
                        if s >= 1:
                            pe.wait_ge(q(free), s)
                        for c in range(DC):
                            for k in range(DC):
                                i = pe.matmul(bk[bank][:, c * T:(c + 1) * T], w[:, k, c * P:(c + 1) * P], xf[:, k, s * T:(s + 1) * T],
                                              start=k == 0, stop=k == DC - 1)
                        i.then_inc(q(done), 1)
                if 1 <= s <= B:
                    b = s - 1
                    scores(0, b, xsf[b % 2], "x1f", "ex", "scP", (b, b))
                if s >= 2:
                    b = s - 2
                    pe.wait_ge(q("x2f"), b + 1)
                    pe.wait_ge(q("pte"), b + 1)
                    for h in range(2):
                        n = 2 * b + h
                        for k in range(DC):
                            i = pe.matmul(bk[6][:, 256 + n * E0:256 + (n + 1) * E0], x2f[b % 2][:, k, h * P:(h + 1) * P], wg[:, k, :],
                                          start=k == 0, stop=k == DC - 1)
                    i.then_inc(q("lg"), 1)
                if 1 <= s <= B:
                    probs_tr(s - 1, "ex", "pte", "pT")
                if s < B:
                    pe.wait_ge(q("y1"), s + 1)
                    if s >= 1:
                        pe.wait_ge(q("n1"), s)
                    for h in range(2):
                        for c in range(DC):
                            i = pe.transpose(bk[2][:, h * D + c * P:h * D + (c + 1) * P], y1[s % 2][:, c, h * P:(h + 1) * P], ident)
                    i.then_inc(q("yT"), 1)
                if 1 <= s <= B:
                    values(0, s - 1, "pte", "y2", "pv", (s - 1, s - 1))

            pe.wait_ge(q("rM"), 1)
            pe.matmul(bk[0][:, 0:256], ltri[:], rMb, start=True, stop=True)
            pe.matmul(bk[0][:, 256:512], onesb[:], rMb, start=True, stop=True).then_inc(q("rW"), 1)
            pe.wait_ge(q("oh"), 1)
            for n in range(2 * NT):
                i = pe.matmul(bk[1][:, 0:3 * NST], ohl[:, n, :], ohh[:, n, :], start=n == 0, stop=n == 2 * NT - 1)
            i.then_inc(q("tab"), 1)

            def inp_tr(e):
                for j in range(ET):
                    n = e * ET + j
                    pe.wait_ge(q(f"ga{e % 2}{j}"), 16 * (e // 2 + 1))
                    if n >= 2:
                        pe.wait_ge(q("ife"), n - 1)
                    for c in range(DC):
                        i = pe.transpose(bk[6 + n % 2][:, c * P:(c + 1) * P], inpT[e % 2][:, j, c * P:(c + 1) * P], ident)
                    i.then_inc(q("ttr"), 1)
            inp_tr(0)
            pe.wait_ge(q("idx"), 1)
            for e in range(E0):
                pe.wait_ge(q(f"in_e{e % 2}"), 32 * (e // 2 + 1))
                pe.wait_ge(q("ife"), ET * (e + 1))
                for u in range(8):
                    n = 8 * e + u
                    f, hf = u // 2, u % 2
                    if n >= 2:
                        pe.wait_ge(q("ge"), n - 1)
                        pe.wait_ge(q("hid"), n - 1)
                    for part in range(2):
                        for k in range(DC):
                            i = pe.matmul(bk[n % 2 + 2 * part][:, 0:HALF], win[e % 2][:, k, part * F0 + f * P:part * F0 + (f + 1) * P],
                                          inpF[e % 2][:, k, hf * HALF:(hf + 1) * HALF], start=k == 0, stop=k == DC - 1)
                    i.then_inc(q("mm1"), 1)
                if e + 1 < E0:
                    inp_tr(e + 1)
                pe.wait_ge(q("hid"), 8 * (e + 1))
                for j in range(ET):
                    n = e * ET + j
                    if n >= 2:
                        pe.wait_ge(q("oe"), n - 1)
                    for k in range(F0 // P):
                        i = pe.matmul(bk[4 + n % 2][:, 0:D], hid[:, k, j * P:(j + 1) * P], wou[e % 2][:, k, :], start=k == 0, stop=k == F0 // P - 1)
                    i.then_inc(q("mm2"), 1)

            def lay1_front(m):
                tr4(bk[3], xt3(m), "n3", m + 1, "x3T", [("x3f", m), ("y6", m - 5), ("y4", m - 3)])
                pe.wait_ge(q("x3f"), m + 1)
                for h in range(2):
                    n = 2 * m + h
                    if n >= 2:
                        pe.wait_ge(q("que"), n - 1)
                    for k in range(DC):
                        i = pe.matmul(bk[h][:], xsf[m % 2][:, k, h * P:(h + 1) * P], quw[:, k, :], start=k == 0, stop=k == DC - 1)
                    i.then_inc(q("qu"), 1)

            def xt3(m):
                a, b_ = tiles_of(m)
                return xt[:, a:b_ + 1:2, :]
            pe.wait_ge(q("oe"), NST)
            for m in range(4):
                lay1_front(m)
            for s in range(8 + 2):
                if 1 <= s <= 8:
                    b = s - 1
                    tr4(bk[4], xs[b % 2], "n4", b + 1, "x4T", [("x5f", b - 1 + (b > 0))])
                    if b >= 1:
                        pe.wait_ge(q("pjr"), b)
                    scores(1, b, x4f[b % 2], "x4f", "ex2", "scQ", (2 * (b % 4), 2 * (b % 4) + 1))
                if s < 8:
                    for h in range(2):
                        n = 2 * s + h
                        pe.wait_ge(q("prd"), n + 1)
                        if n >= 2:
                            pe.wait_ge(q("aof"), n - 1)
                        for c in range(DC):
                            for u in range(B):
                                i = pe.matmul(bk[2][:, h * 256 + c * P:h * 256 + (c + 1) * P], prod[n % 2][:, u, c * P:(c + 1) * P], ident,
                                              start=u == 0, stop=u == B - 1)
                        i.then_inc(q("ao"), 1)
                        pe.wait_ge(q("aof"), n + 1)
                        if n >= 2:
                            pe.wait_ge(q("y4"), s)
                        pe.wait_ge(q("que"), 2 * min(s + 4, 8))
                        for k in range(DC):
                            i = pe.matmul(bk[h][:, 0:D], aof[n % 2][:, k, :], woT[:, k, :], start=k == 0, stop=k == DC - 1)
                        i.then_inc(q("op"), 1)
                if 1 <= s <= 8:
                    b = s - 1
                    if b >= 2:
                        pe.wait_ge(q("y6"), b - 1)
                    probs_tr(b, "ex2", "pte2", "pT2")
                    values(1, b, "pte2", "y5", "pv2", (2 * (b % 4), 2 * (b % 4) + 1))
                    tr4(bk[4], x5s[b % 2], "n5", b + 1, "x5T", [("x4f", b + 1)], strided=True)
                    pe.wait_ge(q("eh"), b + 1)
                    for k in range(DC):
                        i = pe.matmul(bk[5][:, 256:256 + 2 * NB6], C["ones"], eh[:, k, :, :].rearrange("p a b -> p (a b)"), start=k == 0, stop=k == DC - 1)
                    i.then_inc(q("pj"), 1)
                if s >= 2:
                    b = s - 2
                    for h in range(2):
                        n = 2 * b + h
                        pe.wait_ge(q("ws"), n + 1)
                        if b >= 1:
                            pe.wait_ge(q("y6"), b)
                        pe.wait_ge(q("pte2"), min(b + 2, 8))
                        pe.wait_ge(q("x3f"), min(b + 6, 8))
                        for k in range(DC):
                            i = pe.matmul(bk[6][:, 256:512] if h == 0 else bk[3][:, 0:D], x5f[b % 2][:, k, h * P:(h + 1) * P], ws[n % 2][:, k * D:(k + 1) * D],
                                          start=k == 0, stop=k == DC - 1)
                        i.then_inc(q("fm"), 1)
                if s < 4:
                    lay1_front(s + 4)

        @block.vector
        def _(v):
            def chain(i):
                link[0] += 1
                i.then_inc(q("own"), 1)
                v.wait_ge(q("own"), link[0])
            link = [0]

            v.wait_ge(q("in_a"), 48)
            chain(v.tensor_scalar(bh[:], bdv[:, 0, :], 0.5, None, ALU.mult))
            v.wait_ge(q("in_c"), 48)
            v.wait_ge(q("in_k"), 144)
            for l in range(2):
                for k in range(DC):
                    i = v.tensor_scalar(bqb[l][:, k, :], C["ones"], bq[l][:, k:k + 1], None, ALU.mult)
                i.then_inc(q("bqb"), 1)
            v.wait_ge(q("bdP"), 1)
            for c in range(DC):
                i = v.tensor_tensor(bd[:, c, :], bk[0][:, c * P:(c + 1) * P], C["bmask"], ALU.mult)
            i.then_inc(q("bd"), 1)

            def stats(k, m, src, ready=None):
                p = m % 2
                if ready:
                    v.wait_ge(q(ready), m + 1)
                for h in range(2):
                    i = v.bn_stats(st[k][:, p, h, :], src(h))
                chain(i)
                for h in range(2):
                    i = v.bn_aggr(mv[k][:, p, h, :], st[k][:, p, h, :])
                chain(i)
                if m >= 2:
                    v.wait_ge(q(f"rs{k}"), m - 1)
                v.tensor_scalar(ve[k][:, p, :], mv[k][:, p, :, 1], EPS, None, ALU.add).then_inc(q(f"ve{k}"), 1)

            def nbias(k, m, waits=()):
                p = m % 2
                v.wait_ge(q(f"rs{k}"), m + 1)
                for w, n in waits:
                    if n > 0:
                        v.wait_ge(q(w), n)
                v.scalar_tensor_tensor(out=nb[k][:, p, :], in0=mv[k][:, p, :, 0], scalar=-1.0, in1=rs[k][:, p, :],
                                       op0=ALU.mult, op1=ALU.mult).then_inc(q(f"nb{k}"), 1)

            def row_max(b, ready, done):
                v.wait_ge(q(ready), b + 1)
                v.tensor_reduce(nm[:, b % 2, :], bk[5][:, 0:2 * TK].rearrange("p (h n) -> p h n", h=2), AX.X, ALU.max, negate=True).then_inc(q(done), 1)

            def probs_evac(b, ready, done, pv):
                v.wait_ge(q(ready), b + 1)
                if b >= 2:
                    v.wait_ge(q(pv), b - 1)
                v.tensor_copy(pt[b % 2][:], bk[6][0:TK, 0:T]).then_inc(q(done), 1)
                chain(v.reciprocal(rc[:, b % 2, :], sm[:, b % 2, :]))

            for s in range(B + 2):
                if s < B:
                    v.wait_ge(q("d"), s + 1)
                    i = v.tensor_scalar(a1, d1, -0.5, 0.5, ALU.mult, ALU.add)
                    chain(v.tensor_scalar(d1, d1, 0.5, 0.5, ALU.mult, ALU.add))
                    v.wait_ge(q("v"), s + 1)
                    for c in range(DC):
                        i = v.scalar_tensor_tensor(out=dv1[:, c, :], in0=bk[1][:, c * T:(c + 1) * T], scalar=bdv[:, 1, c:c + 1],
                                                   in1=d1[:, c, :], op0=ALU.add, op1=ALU.mult)
                    i.then_inc(q("dv"), 1)
                    v.wait_ge(q("dv"), s + 1)
                    for c in range(DC):
                        i = v.tensor_tensor_scan(hs[:, c, :], a1[:, c, :], dv1[:, c, :], 0.0, ALU.mult, ALU.add)
                    chain(i)
                    if s >= 2:
                        v.wait_ge(q("yT"), s - 1)
                    if s < 3:
                        v.wait_ge(q(f"in_x{s}"), 16)
                    v.tensor_tensor(y1[s % 2][:], hs, xf[:, :, s * T:(s + 1) * T], ALU.add).then_inc(q("y1"), 1)
                if 1 <= s <= B:
                    row_max(s - 1, "scP", "mx")
                if s < B:
                    stats(0, s, lambda h: bk[2][:, h * D:(h + 1) * D], "yT")
                if 1 <= s <= B:
                    probs_evac(s - 1, "pT", "pte", "pv")
                if s < B:
                    nbias(0, s, [("n1", s - 1)])
                if 1 <= s <= B:
                    b = s - 1
                    v.wait_ge(q("pv"), b + 1)
                    if b >= 2:
                        v.wait_ge(q("n2"), b - 1)
                    for h in range(2):
                        i = v.scalar_tensor_tensor(out=y2[b % 2][:, h, :], in0=bk[7][:, h * D:(h + 1) * D], scalar=rc[:, b % 2, h:h + 1],
                                                   in1=xs[b % 2][:, h, :], op0=ALU.mult, op1=ALU.add)
                    i.then_inc(q("y2"), 1)
                    v.wait_ge(q("y2"), b + 1)
                    stats(1, b, lambda h: y2[b % 2][:, h, :])
                    nbias(1, b, [("n2", b - 1)])

            def R(a):
                return rA[:, a * 128:(a + 1) * 128].rearrange("p (n e) -> p n e", e=E0)
            sc_ = sb_small
            k2 = NT * 2

            def over(x, w=E0):
                return x.unsqueeze(2).to_broadcast([P, x.shape[1], w])
            v.wait_ge(q("lg"), B)
            lg = bk[6][:, 256:384].rearrange("p (n e) -> p n e", e=E0)
            chain(v.tensor_reduce(sc_[:, 0, 0:NT], lg, AX.X, ALU.max))
            v.tensor_tensor(R(0), lg, over(sc_[:, 0, 0:NT]), ALU.subtract).then_inc(q("r1"), 1)
            v.wait_ge(q("r2"), 1)
            chain(v.tensor_reduce(sc_[:, 1, 0:NT], R(1), AX.X, ALU.add))
            chain(v.reciprocal(sc_[:, 2, 0:NT], sc_[:, 1, 0:NT]))
            chain(v.tensor_tensor(R(2), R(1), over(sc_[:, 2, 0:NT]), ALU.mult))
            w8 = C["w8"].rearrange("p (n e) -> p n e", e=E0)
            M = rA[:, 1024:1280].rearrange("p (n e) -> p n e", e=E0)
            top = sc_[:, 3, 0:k2]
            c8 = sc_[:, 4, 0:k2]
            for k in range(2):
                a, b_ = k * NT, (k + 1) * NT
                chain(v.tensor_reduce(top[:, a:b_], R(2), AX.X, ALU.max))
                chain(v.tensor_tensor(R(3), R(2), over(top[:, a:b_]), ALU.is_equal))
                chain(v.tensor_tensor(R(4), R(3), w8, ALU.mult))
                chain(v.tensor_reduce(c8[:, a:b_], R(4), AX.X, ALU.max))
                chain(v.tensor_tensor(M[:, a:b_, :], w8, over(c8[:, a:b_]), ALU.is_equal))
                if k == 0:
                    chain(v.scalar_tensor_tensor(out=R(2), in0=M[:, 0:NT, :], scalar=-2.0, in1=R(2), op0=ALU.mult, op1=ALU.add))
            v.tensor_copy(rMb, rA[:, 1024:1280]).then_inc(q("rM"), 1)
            v.wait_ge(q("rW"), 1)
            totE = rA[:, 1280:1536]
            incl = rA[:, 1536:1792]
            chain(v.tensor_copy(totE.rearrange("p (e n) -> p n e", e=E0), bk[0][:, 256:512].rearrange("p (n e) -> p n e", e=E0)))
            chain(v.tensor_tensor_scan(incl, C["smask"], totE, 0.0, ALU.mult, ALU.add))
            chain(v.tensor_tensor(incl, incl, totE, ALU.subtract))
            loc8 = rA[:, 1792:2048].rearrange("p (n e) -> p n e", e=E0)
            chain(v.tensor_tensor(loc8, bk[0][:, 0:256].rearrange("p (n e) -> p n e", e=E0), incl.rearrange("p (e n) -> p n e", e=E0), ALU.add))
            chain(v.tensor_tensor(loc8, loc8, M, ALU.mult))
            loc, hi, lo, keep = (sc_[:, i, 0:k2] for i in (5, 6, 7, 8))
            chain(v.tensor_reduce(loc, loc8, AX.X, ALU.add))
            chain(v.tensor_scalar(hi, loc, float(P), None, ALU.is_ge))
            for j in range(2, ET):
                chain(v.scalar_tensor_tensor(out=hi, in0=loc, scalar=float(P * j), in1=hi, op0=ALU.is_ge, op1=ALU.add))
            chain(v.scalar_tensor_tensor(out=lo, in0=hi, scalar=-float(P), in1=loc, op0=ALU.mult, op1=ALU.add))
            chain(v.scalar_tensor_tensor(out=hi, in0=c8, scalar=-float(ET), in1=hi, op0=ALU.mult, op1=ALU.add))
            chain(v.tensor_scalar(keep, loc, float(CAP), None, ALU.is_lt))
            chain(v.tensor_scalar(hi, hi, float(ET * E0) + 1000.0, None, ALU.add))
            chain(v.scalar_tensor_tensor(out=hi, in0=keep, scalar=-1000.0, in1=hi, op0=ALU.mult, op1=ALU.add))
            ohf = rA[:, 2048:2048 + 1280].rearrange("p (n c) -> p n c", n=k2)
            chain(v.tensor_tensor(ohf, C["iota"][:, 0:NST].unsqueeze(1).to_broadcast([P, k2, NST]), over(hi, NST), ALU.is_equal))
            v.tensor_tensor(ohl, C["iota"].unsqueeze(1).to_broadcast([P, k2, P]), over(lo, P), ALU.is_equal)
            v.tensor_copy(ohh[:, :, 2 * NST:3 * NST], ohf)
            v.tensor_scalar(ohh[:, :, NST:2 * NST], ohf, C["pcol"], None, ALU.mult)
            v.tensor_tensor(ohh[:, :, 0:NST], ohf, over(C["acon"], NST), ALU.mult).then_inc(q("oh"), 1)
            v.wait_ge(q("tab"), 1)
            tb = sb_tab
            chain(v.tensor_copy(tb[:, 0:3 * NST], bk[1][:, 0:3 * NST]))
            chain(v.tensor_tensor(tb[:, 120:160], tb[:, 0:40], tb[:, 40:80], ALU.add))
            chain(v.tensor_scalar(tb[:, 160:200], tb[:, 120:160], float(S), -float(S), ALU.is_ge, ALU.mult))
            v.tensor_tensor(idx[:, 0, :], tb[:, 120:160], tb[:, 160:200], ALU.add)
            chain(v.scalar_tensor_tensor(out=tb[:, 200:240], in0=tb[:, 80:120], scalar=-BIG, in1=tb[:, 120:160], op0=ALU.mult, op1=ALU.add))
            v.tensor_scalar(idx[:, 1, :], tb[:, 200:240], BIG, None, ALU.add).then_inc(q("idx"), 1)
            g0 = sc_[:, 9, 0:k2]
            den = sc_[:, 10, 0:NT]
            chain(v.tensor_tensor(g0, top, keep, ALU.mult))
            chain(v.tensor_tensor(den, g0[:, 0:NT], g0[:, NT:k2], ALU.add))
            chain(v.tensor_scalar(den, den, 1e-9, None, ALU.max))
            chain(v.reciprocal(sc_[:, 11, 0:NT], den))
            for k in range(2):
                i = v.tensor_tensor(gate[:, k, :], g0[:, k * NT:(k + 1) * NT], sc_[:, 11, 0:NT], ALU.mult)
            chain(i)

            for e in range(E0):
                for u in range(8):
                    n = 8 * e + u
                    f, hf = u // 2, u % 2
                    v.wait_ge(q("ge"), n + 1)
                    if u == 0 and e >= 1:
                        v.wait_ge(q("mm2"), ET * e)
                    v.tensor_tensor(hid[:, f, hf * HALF:(hf + 1) * HALF], ge[n % 2], bk[2 + n % 2][:, 0:HALF], ALU.mult).then_inc(q("hid"), 1)
                for j in range(ET):
                    n = e * ET + j
                    v.wait_ge(q("mm2"), n + 1)
                    if n >= 4:
                        v.wait_ge(q(f"sc{n % 4}"), 16 * (n // 4))
                    v.tensor_copy(oe[n % 4], bk[4 + n % 2][:, 0:D]).then_inc(q("oe"), 1)

            def lay1_front(m):
                v.wait_ge(q(f"yl{m % 2}"), 32 * (m // 2 + 1))
                if m >= 2:
                    v.wait_ge(q("n3"), m - 1)
                for h, n in enumerate(tiles_of(m)):
                    i = v.scalar_tensor_tensor(out=y3[m % 2][:, h, :], in0=yb[m % 2][:, h, 0, :], scalar=gate[:, 0, n:n + 1], in1=xt[:, n, :],
                                               op0=ALU.mult, op1=ALU.add)
                chain(i)
                for h, n in enumerate(tiles_of(m)):
                    i = v.scalar_tensor_tensor(out=y3[m % 2][:, h, :], in0=yb[m % 2][:, h, 1, :], scalar=gate[:, 1, n:n + 1], in1=y3[m % 2][:, h, :],
                                               op0=ALU.mult, op1=ALU.add)
                i.then_inc(q("y3"), 1)
                v.wait_ge(q("y3"), m + 1)
                stats(2, m, lambda h: y3[m % 2][:, h, :])
                nbias(2, m, [("n3", m - 1)])

            def distances(g):
                Q = (qa, qa2)[g]
                v.wait_ge(q("que"), 8 * g + 8)
                for r in range(1, B):
                    o = OFF[r]
                    n = B - r
                    v.tensor_tensor(dif[:, o:o + n * D].rearrange("p (t n) -> p t n", t=n), Q[:, r:B, :], Q[:, 0:n, :], ALU.subtract).then_inc(q("dif"), 1)
                for r in range(1, B):
                    o = OFF[r]
                    n = B - r
                    v.wait_ge(q("sq"), 7 * g + r)
                    if g == 1 and r == 1:
                        v.wait_ge(q("e1"), 7)
                    v.tensor_reduce(dsv(r), dif[:, o:o + n * D].rearrange("p (t h d) -> p t h d", h=NH, d=HD), AX.X, ALU.add).then_inc(q("ds"), 1)
                a = att[g]
                at3 = a.rearrange("p (t s h) -> p t s h", t=B, s=B)
                for t in range(B):
                    v.memset(at3[:, t, t, :], 1.0)
                for r in range(1, B):
                    v.wait_ge(q("e1"), 7 * g + r)
                    i = v.tensor_copy(pair(a, r, True), pair(a, r, False))
                chain(i)
                chain(v.tensor_reduce(zz[:], a.rearrange("p (t s h) -> p t h s", t=B, s=B), AX.X, ALU.add))
                chain(v.reciprocal(rz[:], zz[:]))
                for t in range(B):
                    i = v.tensor_tensor(at3[:, t, :, :], at3[:, t, :, :], rz[:, t, :].unsqueeze(1).to_broadcast([P, B, NH]), ALU.mult)
                chain(i)

            for m in range(4):
                lay1_front(m)
            for s in range(8 + 2):
                if s in (0, 4):
                    distances(s // 4)
                if s < 8:
                    g = s // 4
                    U = (ua, ua2)[g]
                    for h in range(2):
                        n = 2 * s + h
                        t = 2 * (s % 4) + h
                        if n >= 2:
                            v.wait_ge(q("ao"), n - 1)
                        w = att[g].rearrange("p (t s h) -> p t s h", t=B, s=B)[:, t, :, :]
                        v.tensor_tensor(prod[n % 2].rearrange("p s (h d) -> p (s h) d", d=HD),
                                        U.rearrange("p s (h d) -> p (s h) d", d=HD),
                                        w.rearrange("p s h -> p (s h)").unsqueeze(2).to_broadcast([P, B * NH, HD]), ALU.mult).then_inc(q("prd"), 1)
                    for h, n in enumerate(tiles_of(s)):
                        i = v.tensor_tensor(xbs[:, h, :], xt[:, n, :], obr[:], ALU.add)
                    chain(i)
                if 1 <= s <= 8:
                    row_max(s - 1, "scQ", "mx2")
                if s < 8:
                    v.wait_ge(q("op"), 2 * s + 2)
                    if s >= 2:
                        v.wait_ge(q("n4"), s - 1)
                    for h in range(2):
                        i = v.tensor_tensor(y4[s % 2][:, h, :], bk[h][:, 0:D], xbs[:, h, :], ALU.add)
                    i.then_inc(q("y4"), 1)
                    v.wait_ge(q("y4"), s + 1)
                    stats(3, s, lambda h: y4[s % 2][:, h, :])
                if 1 <= s <= 8:
                    probs_evac(s - 1, "pT2", "pte2", "pv2")
                if s < 8:
                    nbias(3, s, [("n4", s - 1)])
                if 1 <= s <= 8:
                    b = s - 1
                    v.wait_ge(q("pv2"), b + 1)
                    if b >= 2:
                        v.wait_ge(q("n5"), b - 1)
                    for h in range(2):
                        i = v.scalar_tensor_tensor(out=y2[b % 2][:, h, :], in0=bk[7][:, h * D:(h + 1) * D], scalar=rc[:, b % 2, h:h + 1],
                                                   in1=xs[b % 2][:, h, :], op0=ALU.mult, op1=ALU.add)
                    i.then_inc(q("y5"), 1)
                    v.wait_ge(q("y5"), b + 1)
                    stats(4, b, lambda h: y2[b % 2][:, h, :])
                    nbias(4, b, [("n5", b - 1)])
                    v.wait_ge(q("x5f"), b + 1)
                    chain(v.tensor_reduce(emb[:], x5f[b % 2][:].rearrange("p c (h t) -> p c h t", h=2), AX.X, ALU.add))
                    if b >= 1:
                        v.wait_ge(q("pj"), b)
                    for h in range(2):
                        i = v.tensor_tensor(eh[:, :, h, :], hyp[:], emb[:, :, h:h + 1].to_broadcast([P, DC, NB6]), ALU.mult)
                    i.then_inc(q("eh"), 1)
                    v.wait_ge(q("pj"), b + 1)

                    def V6(i):
                        return rt[:, i, :].rearrange("p (h n) -> p h n", h=2)
                    v.tensor_copy(rt[:, 0, :], bk[5][:, 256:256 + 2 * NB6]).then_inc(q("pjr"), 1)
                    v.wait_ge(q("pjr"), b + 1)
                    chain(v.tensor_scalar(rt[:, 1, :], rt[:, 0, :], 0.0, None, ALU.is_gt))
                    chain(v.tensor_tensor(rt[:, 1, :], rt[:, 1, :], C["p6"], ALU.mult))
                    chain(v.scalar_tensor_tensor(out=rt[:, 2, :], in0=rt[:, 0, :], scalar=-1.0, in1=rt[:, 0, :], op0=ALU.mult, op1=ALU.max))
                    e1, mn, fc, fl, bt, e2 = (rt[:, i, 0:2] for i in (3, 4, 5, 6, 7, 8))
                    v.tensor_reduce(e1, V6(1), AX.X, ALU.add)
                    chain(v.tensor_reduce(mn, V6(2), AX.X, ALU.min))
                    chain(v.tensor_tensor(V6(9), V6(2), over(mn, NB6), ALU.is_equal))
                    chain(v.tensor_tensor(rt[:, 9, :], rt[:, 9, :], C["w6"], ALU.mult))
                    chain(v.tensor_reduce(fc, V6(9), AX.X, ALU.max))
                    chain(v.tensor_tensor(V6(9), C["w6"].rearrange("p (h n) -> p h n", h=2), over(fc, NB6), ALU.is_equal))
                    v.tensor_tensor(rt[:, 10, :], rt[:, 9, :], C["p6"], ALU.mult)
                    chain(v.tensor_tensor(rt[:, 11, :], rt[:, 9, :], rt[:, 1, :], ALU.mult))
                    v.tensor_reduce(fl, V6(10), AX.X, ALU.add)
                    chain(v.tensor_reduce(bt, V6(11), AX.X, ALU.add))
                    chain(v.tensor_tensor(e2, e1, fl, ALU.add))
                    chain(v.scalar_tensor_tensor(out=e2, in0=bt, scalar=-2.0, in1=e2, op0=ALU.mult, op1=ALU.add))
                    if b >= 2:
                        v.wait_ge(q(f"we0"), 32 * (b - 1))
                        v.wait_ge(q(f"we1"), 32 * (b - 1))
                    wi = widx[b % 2][:].rearrange("p (h k) -> p h k", k=2)
                    v.tensor_scalar(wi[:, :, 0], e1, float(P), C["pcol"], ALU.mult, ALU.add)
                    v.tensor_scalar(wi[:, :, 1], e2, float(P), C["pcol"], ALU.mult, ALU.add).then_inc(q("widx"), 1)
                if s >= 2:
                    b = s - 2
                    for h in range(2):
                        n = 2 * b + h
                        v.wait_ge(q(f"we{n % 2}"), 32 * (b + 1))
                        if n >= 2:
                            v.wait_ge(q("fm"), n - 1)
                        v.tensor_tensor(ws[n % 2], we[n % 2][:, 0, :], we[n % 2][:, 1, :], ALU.add).then_inc(q("ws"), 1)
                    v.wait_ge(q("fm"), 2 * b + 2)
                    if b >= 2:
                        v.wait_ge(q("n6"), b - 1)
                    for h in range(2):
                        i = v.scalar_tensor_tensor(out=y6b[b % 2][:, h, :], in0=bk[6][:, 256:512] if h == 0 else bk[3][:, 0:D], scalar=0.5,
                                                   in1=x5s[b % 2][:, h, :], op0=ALU.mult, op1=ALU.add)
                    i.then_inc(q("y6"), 1)
                    v.wait_ge(q("y6"), b + 1)
                    stats(5, b, lambda h: y6b[b % 2][:, h, :])
                    nbias(5, b, [("n6", b - 1)])
                if s < 4:
                    lay1_front(s + 4)



def kernel(x, ctx_768, L0_attn_W_delta, L0_attn_b_delta, L0_attn_W_value, L0_attn_b_value, L0_xattn_Wq, L0_xattn_bq, L0_xattn_Wk,
           L0_xattn_bk, L0_xattn_Wv, L0_xattn_bv, L0_ffn_Wg, L0_ffn_W_in, L0_ffn_W_out, L1_attn_q_weight, L1_attn_v_weight, L1_attn_out_w,
           L1_attn_out_b, L1_xattn_Wq, L1_xattn_bq, L1_xattn_Wk, L1_xattn_bk, L1_xattn_Wv, L1_xattn_bv, L1_ffn_expert_weights,
           L1_ffn_hyperplanes):
    import concourse.bacc as bacc
    from concourse.bass_utils import run_bass_kernel_spmd
    import ml_dtypes

    c = np.ascontiguousarray
    n = np.asarray
    arrays = {
        "xT": c(n(x).reshape(S, D).T), "ctxT": c(n(ctx_768).reshape(B * TK, CD).T),
        "Wd": c(n(L0_attn_W_delta).T), "Wv": c(n(L0_attn_W_value).T),
        "bdv": c(np.stack([n(L0_attn_b_delta), n(L0_attn_b_value)]).reshape(2, DC, P).transpose(2, 0, 1)),
        "Wq0": c(n(L0_xattn_Wq)), "bq0": c(n(L0_xattn_bq).reshape(DC, P).T), "Wk0": c(n(L0_xattn_Wk).T), "bk0": c(n(L0_xattn_bk)[None]),
        "Wvx0": c(n(L0_xattn_Wv).T), "bvx0": c(n(L0_xattn_bv)[None]),
        "Wq1": c(n(L1_xattn_Wq).T), "bq1": c(n(L1_xattn_bq).reshape(DC, P).T), "Wk1": c(n(L1_xattn_Wk)), "bk1": c(n(L1_xattn_bk)[None]),
        "Wvx1": c(n(L1_xattn_Wv)), "bvx1": c(n(L1_xattn_bv)[None]),
        "Wg": c(n(L0_ffn_Wg)), "W_in": c(n(L0_ffn_W_in)), "W_out": c(n(L0_ffn_W_out)),
        "qw": c(n(L1_attn_q_weight).reshape(D, D)), "qwT": c(n(L1_attn_q_weight).reshape(D, D).T),
        "vw": c(n(L1_attn_v_weight).reshape(D, D)), "woT": c(n(L1_attn_out_w).T),
        "obr": c(np.broadcast_to(n(L1_attn_out_b), (P, D))), "hyp": c(n(L1_ffn_hyperplanes)),
        "EW": c(n(L1_ffn_expert_weights).reshape(64 * P, 2 * D)),
        "cf": shape_constants(), "ones1": np.ones((1, B * TK), np.float32),
        "ltri": np.triu(np.ones((P, P), np.float32), 1).astype(ml_dtypes.bfloat16),
        "onesb": np.ones((P, P), ml_dtypes.bfloat16),
    }
    nc = bacc.Bacc("TRN2", target_bir_lowering=False, num_devices=1)
    A = {k: nc.dram_tensor(k, a.shape, mybir.dt.from_np(a.dtype), kind="ExternalInput").ap() for k, a in arrays.items()}
    out = nc.dram_tensor("out", (B, T, D), F32, kind="ExternalOutput").ap()
    Y = nc.dram_tensor("expert_rows", (2 * S, D), F32, kind="Internal").ap()
    X2 = nc.dram_tensor("x2_rows", (S, D), F32, kind="Internal").ap()
    program(nc, A, out, Y, X2)
    r = run_bass_kernel_spmd(nc, [arrays], core_ids=[0])
    return r.results[0]["out"]
```

```python
from contextlib import ExitStack

import numpy as np

import concourse.bass as bass
import concourse.mybir as mybir

F32 = mybir.dt.float32
BF16 = mybir.dt.bfloat16
F32R = mybir.dt.float32r
I32 = mybir.dt.int32
ALU = mybir.AluOpType
ACT = mybir.ActivationFunctionType
AX = mybir.AxisListType

P = 128
B = 8
T = 256
D = 256
DC = D // P
S = B * T
NT = S // P
TK = 77
CD = 192
CK = CD // 2
E0 = 8
F0 = 512
CAP = 640
ET = CAP // P
NST = E0 * ET
HALF = CAP // 2
NH = 16
HD = 16
NB6 = 6
EPS = 1e-5
BIG = 8192.0

_CF = {}
_n = 0
for _name, _w in (("ident", P), ("bmask", P), ("iota", P), ("w8", NT * E0), ("smask", 2 * NT * E0),
                  ("acon", 2 * NT), ("pcol", 1), ("sel0", P), ("ones", P), ("w6", 2 * NB6), ("p6", 2 * NB6),
                  ("negh", 2)):
    _CF[_name] = (_n, _n + _w)
    _n += _w
CFW = _n


def shape_constants():
    c = np.zeros((P, CFW), np.float32)

    def put(name, v):
        a, b = _CF[name]
        c[:, a:b] = v
    put("ident", np.eye(P))
    put("bmask", np.kron(np.eye(P // HD), np.ones((HD, HD))) * HD ** -0.5)
    put("iota", np.arange(P)[None, :])
    put("w8", np.tile(E0 - np.arange(E0), NT)[None, :])
    m = np.ones((E0, 2 * NT))
    m[:, 0] = 0
    put("smask", m.reshape(1, -1))
    put("acon", (P * np.arange(2 * NT))[None, :])
    put("pcol", np.arange(P)[:, None])
    s0 = np.zeros((P, P))
    s0[0] = 1
    put("sel0", s0)
    put("ones", 1.0)
    put("w6", np.tile(NB6 - np.arange(NB6), 2)[None, :])
    put("p6", np.tile(2.0 ** np.arange(NB6), 2)[None, :])
    put("negh", -0.5)
    return c


def program(nc, A, out, Y, X2):
    ctx = ExitStack()
    with ctx:
        def sb(name, shape, dt=F32):
            return ctx.enter_context(nc.sbuf_tensor("sb_" + name, shape, dt))

        def sem(name):
            return ctx.enter_context(nc.semaphore(name))

        cf = sb("cf", [P, CFW])
        C = {k: cf[:, a:b] for k, (a, b) in _CF.items()}
        ident = C["ident"]
        ltri = sb("ltri", [P, P], BF16)
        onesb = sb("onesb", [P, P], BF16)
        xt = sb("xt", [P, NT, D])
        wdv = sb("wdv", [P, 2 * DC * D])
        wd, wv = (wdv[:, i * DC * D:(i + 1) * DC * D].rearrange("p (c n) -> p c n", c=DC) for i in range(2))
        bdv = sb("bdv", [P, 2, DC])
        bq = [sb(f"bq{l}", [P, DC]) for l in range(2)]
        Ga = [sb(f"G{l}", [P, DC * B * TK]) for l in range(2)]
        G = [a[:].rearrange("p (c n) -> p c n", c=DC) for a in Ga]
        bqk = [sb(f"bqk{l}", [P, B * TK]) for l in range(2)]
        vxa = [sb(f"vx{l}", [P, B * D]) for l in range(2)]
        vx = [a[0:TK, :].rearrange("p (b n) -> p b n", b=B) for a in vxa]
        wg = sb("wg", [P, DC, E0])
        qw = sb("qw", [P, DC, D])
        quw = sb("quw", [P, DC, 2 * D])
        woT = sb("woT", [P, DC, D])
        obr = sb("obr", [P, D])
        hyp = sb("hyp", [P, DC, NB6])
        with nc.sbuf_tensor("sb_big", [P, 21504], F32) as big:
            pass
        part = {}
        for name, words in (("hidH", 2560), ("gap0", 4608), ("winH", 2048), ("wouH", 1024), ("winL", 2048), ("wouL", 1024), ("gap1", 2560),
                            ("inpH", 1280), ("inpL", 1280), ("hidL", 2560), ("gap2", 512)):
            part[name] = sb(name, [P, words], F32 if name.startswith("gap") else F32R)
        def view(a, c, n=None, parts=P):
            return big[0:parts, a:a + c * n].rearrange("p (c n) -> p c n", c=c)
        kf = view(10240, DC, B * TK)
        wk = [view(11520 + l * 512, 2, D, CK + 1) for l in range(2)]
        wvx = [view(12544 + l * 512, 2, D, CK + 1) for l in range(2)]
        wq = [view(13568 + l * 512, DC, D) for l in range(2)]
        bqb = [view(14592 + l * 256, DC, P) for l in range(2)]
        bd = view(15104, DC, P)
        qwT = view(15360, DC, D)
        vw = view(15872, DC, D)
        cx = view(16384, 2, B * TK, CK + 1)
        zero = big[:, 20480:21504]
        xf = big[:, 0:4096].rearrange("p (c t) -> p c t", c=DC)
        FC = F0 // P

        win = view(4096, DC, 2 * F0)
        wou = view(6144, FC, D)
        winH, winL, inpH, inpL = (part[k][:].rearrange("p (c n) -> p c n", c=DC) for k in ("winH", "winL", "inpH", "inpL"))
        wouH, wouL, hidH, hidL = (part[k][:].rearrange("p (c n) -> p c n", c=FC) for k in ("wouH", "wouL", "hidH", "hidL"))
        winH4, inpH4, wouH4, hidH4 = (x.bitcast(F32) for x in (winH, inpH, wouH, hidH))
        inpT = [view(13312 + i * 1280, ET, D) for i in range(2)]
        oe = [big[:, 2560 + i * 256:2560 + (i + 1) * 256] for i in range(4)]
        rA = big[:, 0:4096]
        qa = big[:, 0:2048].rearrange("p (t n) -> p t n", t=B)
        ua = big[:, 2048:4096].rearrange("p (t n) -> p t n", t=B)
        ua2 = big[:, 4096:6144].rearrange("p (t n) -> p t n", t=B)
        qa2 = big[:, 6144:8192].rearrange("p (t n) -> p t n", t=B)
        dif = [big[:, 8192 + i * 13 * D:8192 + (i + 1) * 13 * D] for i in range(2)]
        att = [big[:, 15360 + i * 1024:15360 + (i + 1) * 1024] for i in range(2)]
        prod = [big[:, 17408 + i * 2048:17408 + (i + 1) * 2048].rearrange("p (s n) -> p s n", s=B) for i in range(2)]
        ph = sb("ph", [P, 4 * DC * T])
        th, a1, dv1, hs = (ph[:, i * DC * T:(i + 1) * DC * T].rearrange("p (c n) -> p c n", c=DC) for i in range(4))
        ge = [ph[:, i * HALF:(i + 1) * HALF] for i in range(2)]
        hid = [ph[:, (2 + i) * HALF:(3 + i) * HALF] for i in range(2)]
        y1 = [sb(f"y1{i}", [P, DC, T]) for i in range(2)]
        xs = [sb(f"xs{i}", [P, 2, D]) for i in range(2)]
        xsf = [sb(f"xsf{i}", [P, DC, T]) for i in range(2)]
        x2f = [sb(f"x2f{i}", [P, DC, T]) for i in range(2)]
        vb = [sb(f"vb{i}", [P, DC, T]) for i in range(1)][0]
        pr = [sb(f"pr{i}", [P, 2, TK]) for i in range(2)]
        pt = [sb(f"pt{i}", [TK, T]) for i in range(2)]
        y2 = [sb(f"y2{i}", [P, 2, D]) for i in range(2)]
        st = {k: sb(f"st{k}", [P, 2, 2, 6]) for k in range(6)}
        mv = {k: sb(f"mv{k}", [P, 2, 2, 2]) for k in range(6)}
        ve = {k: sb(f"ve{k}", [P, 2, 2]) for k in range(6)}
        rs = {k: sb(f"rs{k}", [P, 2, 2]) for k in range(6)}
        ng = {k: sb(f"ng{k}", [P, 2, 2]) for k in range(6)}
        nb = {k: sb(f"nb{k}", [P, 2, 2]) for k in range(6)}
        nm = sb("nm", [P, 2, 2])
        sm = sb("sm", [P, 2, 2])
        rc = sb("rc", [P, 2, 2])
        bk = [ctx.enter_context(nc.psum_tensor(f"bank{i}", [P, 512], F32)) for i in range(8)]

        sems = {}

        def q(name):
            if name not in sems:
                sems[name] = sem(name)
            return sems[name]

        NSETUP = 27
        def tiles_of(m):
            g, i = m // 4, m % 4
            return [2 * (2 * i) + g, 2 * (2 * i + 1) + g]

        yb = [ph[:, i * 4 * D:(i + 1) * 4 * D].rearrange("p (h k n) -> p h k n", h=2, k=2) for i in range(2)]
        y6 = [Ga[0][:, i * 2 * D:(i + 1) * 2 * D].rearrange("p (h n) -> p h n", h=2) for i in range(2)]
        y4 = [sb(f"y4{i}", [P, 2, D]) for i in range(2)]
        x4f = [sb(f"x4f{i}", [P, DC, T]) for i in range(2)]
        aof = [bqk[0][:, i * 2 * P:(i + 1) * 2 * P].rearrange("p (c n) -> p c n", c=DC) for i in range(2)]
        x5s = [sb(f"x5s{i}", [P, 2, D]) for i in range(2)]
        x5f = [sb(f"x5f{i}", [P, DC, T]) for i in range(2)]
        ws = [wdv[:, i * 2 * D:(i + 1) * 2 * D] for i in range(2)]
        we = [vxa[0][:, i * 4 * D:(i + 1) * 4 * D].rearrange("p (k n) -> p k n", k=2) for i in range(2)]
        idx = sb("idx", [P, 2, NST], I32)
        gate = sb("gate", [P, 2, NT])
        widx = [sb(f"widx{i}", [P, 4], I32) for i in range(2)]
        emb = sb("emb", [P, DC, 2])
        eh = sb("eh", [P, DC, 2, NB6])
        rt = sb("rt", [P, 12, 2 * NB6])
        rz = sb("rz", [P, B, NH])
        zz = sb("zz", [P, B, NH])

        bh = sb("bh", [P, 2, DC])
        y6b, y3 = x2f, y1
        xbs = sb("xbs", [P, 2, D])
        dsq = sb("dsq", [P, 28, NH])

        rMb_t = sb("rMb", [P, 2 * NT * E0], BF16)
        rMb = rMb_t[:]
        ohl = ph[:].bitcast(BF16).rearrange("p (n c) -> p n c", n=2 * NT)
        ohh = big[:, 18560:20480].bitcast(BF16).rearrange("p (n c) -> p n c", n=2 * NT)

        sb_small = sb("small", [P, 12, 2 * NT])
        sb_tab = big[:, 3328:3568]

        block = ctx.enter_context(nc.Block())

        @block.sync
        def _(sp):
            xr = A["xT"].rearrange("(c p) t -> p c t", p=P)
            sp.dma_start(xf[:, :, 0:T], xr[:, :, 0:T]).then_inc(q("in_x0"), 16)
            sp.dma_start(wv, A["Wv"].rearrange("(c p) e -> p c e", p=P)).then_inc(q("in_a"), 16)
            sp.dma_start(bdv[:], A["bdv"]).then_inc(q("in_a"), 16)
            sp.dma_start(xf[:, :, T:2 * T], xr[:, :, T:2 * T]).then_inc(q("in_x1"), 16)
            sp.dma_start(xf[:, :, 2 * T:], xr[:, :, 2 * T:]).then_inc(q("in_x2"), 16)
            for l in range(2):
                sp.dma_start(wvx[l][0:CK, :, :], A[f"Wvx{l}"].rearrange("(c p) e -> p c e", p=CK)).then_inc(q("in_k"), 16)
                sp.dma_start(wvx[l][CK:CK + 1, 1, :], A[f"bvx{l}"]).then_inc(q("in_k"), 16)
                sp.dma_start(wq[l], A[f"Wq{l}"].rearrange("(c p) e -> p c e", p=P)).then_inc(q("in_k"), 16)
                sp.dma_start(bq[l][:], A[f"bq{l}"]).then_inc(q("in_k"), 16)
            sp.dma_start(wg[:], A["Wg"].rearrange("(c p) e -> p c e", p=P)).then_inc(q("in_k"), 16)
            for n, w in (("qw", qw), ("qwT", qwT), ("vw", vw), ("woT", woT)):
                sp.dma_start(w[:, :, :], A[n].rearrange("(c p) e -> p c e", p=P)).then_inc(q("in_w"), 16)
            sp.dma_start(obr[:], A["obr"]).then_inc(q("in_w"), 16)
            sp.dma_start(hyp[:], A["hyp"].rearrange("(p j) k -> p j k", j=DC)).then_inc(q("in_w"), 16)

            sp.wait_ge(q("zero"), 1)
            yz = Y.rearrange("(p r) n -> p (r n)", p=P)
            for i in range(8):
                sp.dma_start(yz[:, i * 1024:(i + 1) * 1024], zero).then_inc(q("yz"), 16)

            def load_expert(e):
                if e >= 1:
                    sp.wait_ge(q("wiL"), e)
                sp.dma_start(win, A["W_in"][e].rearrange("(c p) f -> p c f", p=P)).then_inc(q("in_wi"), 16)
                if e >= 1:
                    sp.wait_ge(q("woL"), e)
                sp.dma_start(wou, A["W_out"][e].rearrange("(c p) f -> p c f", p=P)).then_inc(q("in_wo"), 16)
            load_expert(0)
            for b in range(B):
                sp.wait_ge(q("n2"), b + 1)
                sp.dma_start(X2[b * T:(b + 1) * T, :].rearrange("(h p) n -> p h n", p=P), xt[:, 2 * b:2 * b + 2, :]).then_inc(q("x2d"), 16)
            for e in range(1, E0):
                load_expert(e)
            for m in range(8):
                if m == 0:
                    for r in range(4):
                        sp.wait_ge(q(f"sc{r}"), 16 * NST // 4)
                    sp.wait_ge(q("yz"), 128)
                if m >= 2:
                    sp.wait_ge(q("y3"), m - 1)
                for h, n in enumerate(tiles_of(m)):
                    src = Y.rearrange("(k n p) d -> n p k d", k=2, p=P)[n]
                    sp.dma_start(yb[m % 2][:, h, :, :], src).then_inc(q(f"yl{m % 2}"), 16)
            for m in range(8):
                sp.wait_ge(q("n6"), m + 1)
                for h, n in enumerate(tiles_of(m)):
                    sp.dma_start(out[n // 2, (n % 2) * P:(n % 2 + 1) * P, :], y6[m % 2][:, h, :]).then_inc(q(f"od{m % 2}"), 16)
            for r in range(2):
                sp.wait_ge(q(f"od{r}"), 128)

        @block.gpsimd
        def _(pool):
            pool.memset(zero, 0.0).then_inc(q("zero"), 1)

            def power(k, m):
                p = m % 2
                pool.wait_ge(q(f"mv{k}"), m + 1)
                if m >= 2:
                    pool.wait_ge(q(f"n{k + 1}"), m - 1)
                pool.tensor_scalar(ve[k][:, p, :], mv[k][:, p, :, 1], EPS, None, ALU.add).then_inc(q("ve"), 1)
                pool.tensor_scalar(ng[k][:, p, :], mv[k][:, p, :, 0], -1.0, None, ALU.mult)
                pool.wait_ge(q("ve"), powers[0] + 1)
                pool.tensor_tensor(rs[k][:, p, :], ve[k][:, p, :], C["negh"], ALU.pow).then_inc(q("rs"), 1)
                powers[0] += 1
                pool.wait_ge(q("rs"), powers[0])
                pool.tensor_tensor(nb[k][:, p, :], ng[k][:, p, :], rs[k][:, p, :], ALU.mult).then_inc(q(f"nb{k}"), 1)
            powers = [0]
            pool.wait_ge(q("in_c"), 48)
            for s in range(B + 2):
                if 1 <= s <= B:
                    power(0, s - 1)
                if s < B:
                    pool.wait_ge(q("th"), s + 1)
                    if s >= 1:
                        pool.wait_ge(q("scan"), s)
                    pool.tensor_scalar(a1, th, -0.5, 0.5, ALU.mult, ALU.add).then_inc(q("a1"), 1)
                if s >= 2:
                    power(1, s - 2)
            pool.wait_ge(q("bdE"), 1)
            for c in range(DC):
                i = pool.tensor_tensor(bd[:, c, :], bd[:, c, :], C["bmask"], ALU.mult)
            i.then_inc(q("bd"), 1)

            def gather(e):
                if e == 0:
                    pool.wait_ge(q("idx"), 1)
                    pool.wait_ge(q("UP"), 1)
                    pool.wait_ge(q("x2d"), 16 * B)
                if e >= 2:
                    pool.wait_ge(q("ttr"), ET * (e - 1))
                for j in range(ET):
                    pool.indirect_dma_start(out=inpT[e % 2][:, j, :], out_offset=None, in_=X2[:, :],
                                            in_offset=bass.IndirectOffsetOnAxis(ap=idx[:, 0, e * ET + j:e * ET + j + 1], axis=0)
                                            ).then_inc(q(f"ga{e % 2}{j}"), 16)

            def scatter(e):
                for j in range(ET):
                    n = e * ET + j
                    if n == 0:
                        pool.wait_ge(q("yz"), 128)
                    pool.wait_ge(q("oe"), n + 1)
                    pool.indirect_dma_start(out=Y[:, :], out_offset=bass.IndirectOffsetOnAxis(ap=idx[:, 1, n:n + 1], axis=0),
                                            in_=oe[n % 4], in_offset=None, bounds_check=2 * S - 1, oob_is_err=False
                                            ).then_inc(q(f"sc{n % 4}"), 16)
            gather(0)
            for e in range(E0):
                if e + 1 < E0:
                    gather(e + 1)
                scatter(e)

            def chunk_weights(m):
                for h in range(2):
                    n = 2 * m + h
                    pool.wait_ge(q("widx"), m + 1)
                    if n >= 2:
                        pool.wait_ge(q("ws"), n - 1)
                    for k in range(2):
                        pool.indirect_dma_start(out=we[n % 2][:, k, :], out_offset=None, in_=A["EW"],
                                                in_offset=bass.IndirectOffsetOnAxis(ap=widx[m % 2][:, 2 * h + k:2 * h + k + 1], axis=0)
                                                ).then_inc(q(f"we{n % 2}"), 16)
            def subtract(m):
                g, i = m // 4, m % 4
                t = 2 * i
                if t == 0:
                    return
                pool.wait_ge(q("que"), 2 * m + 1)
                if m >= 2:
                    pool.wait_ge(q("ds"), m - 1)
                Q = (qa, qa2)[g]
                pool.tensor_tensor(dif[m % 2][:, 0:t * D].rearrange("p (s n) -> p s n", s=t), Q[:, t:t + 1, :].to_broadcast([P, t, D]), Q[:, 0:t, :],
                                   ALU.subtract).then_inc(q("difP"), 1)

            def add_bias(s):
                if s >= 1:
                    pool.wait_ge(q("y4"), s)
                pool.wait_ge(q("n3"), s + 1)
                for h, n in enumerate(tiles_of(s)):
                    i = pool.tensor_tensor(xbs[:, h, :], xt[:, n, :], obr[:], ALU.add)
                i.then_inc(q("xb"), 1)

            def sum_weights(b):
                for h in range(2):
                    n = 2 * b + h
                    pool.wait_ge(q(f"we{n % 2}"), 32 * (b + 1))
                    if n >= 2:
                        pool.wait_ge(q("fm"), n - 1)
                    pool.tensor_tensor(ws[n % 2], we[n % 2][:, 0, :], we[n % 2][:, 1, :], ALU.add).then_inc(q("ws"), 1)

            for f in range(8):
                power(2, f)
                if 1 <= f:
                    subtract(f - 1)
            for s in range(8 + 3):
                if s < 8:
                    add_bias(s)
                if 3 <= s:
                    sum_weights(s - 3)
                if 8 <= s <= 9:
                    chunk_weights(s - 2)
                if 1 <= s <= 8:
                    power(4, s - 1)
                if 3 <= s:
                    power(5, s - 3)
                if s < 8:
                    power(3, s)
                if 2 <= s < 8:
                    chunk_weights(s - 2)
                if s == 0:
                    subtract(7)

        @block.scalar
        def _(act):
            act.dma_start(wd, A["Wd"].rearrange("(c p) e -> p c e", p=P)).then_inc(q("in_d"), 16)
            act.dma_start(cf[:], A["cf"]).then_inc(q("in_c"), 16)
            act.dma_start(ltri[:], A["ltri"]).then_inc(q("in_c"), 16)
            act.dma_start(onesb[:], A["onesb"]).then_inc(q("in_c"), 16)
            act.dma_start(cx[0:CK, :, :], A["ctxT"].rearrange("(c p) t -> p c t", p=CK)).then_inc(q("in_cx"), 16)
            act.dma_start(cx[CK:CK + 1, 1, :], A["ones1"]).then_inc(q("in_cx"), 16)
            for l in range(2):
                act.dma_start(wk[l][0:CK, :, :], A[f"Wk{l}"].rearrange("(c p) e -> p c e", p=CK)).then_inc(q("in_cx"), 16)
                act.dma_start(wk[l][CK:CK + 1, 1, :], A[f"bk{l}"]).then_inc(q("in_cx"), 16)

            def keys(l, k0, g0):
                for c in range(DC):
                    for h in range(2):
                        n = l * 4 + c * 2 + h
                        act.wait_ge(q("kP"), n + 1)
                        if l == 1 and c == 0 and h == 0:
                            act.wait_ge(q("bqP"), 2)
                        act.activation(kf[:, c, h * 308:(h + 1) * 308], bk[k0 + n % 2][:, 0:308], ACT.Copy).then_inc(q("kE"), 1)
                for c in range(DC):
                    for h in range(2):
                        n = l * 4 + c * 2 + h
                        act.wait_ge(q("GP"), n + 1)
                        act.activation(G[l][:, c, h * 308:(h + 1) * 308], bk[g0 + n % 2][:, 0:308], ACT.Copy, scale=1.0 / 16).then_inc(q("GE"), 1)
                for h in range(2):
                    n = l * 2 + h
                    act.wait_ge(q("bqP"), n + 1)
                    act.activation(bqk[l][:, h * 308:(h + 1) * 308], bk[k0 + n % 2][:, 0:308], ACT.Copy, scale=1.0 / 16).then_inc(q("bqE"), 1)
                for b in range(B):
                    n = l * B + b
                    act.wait_ge(q("vP"), n + 1)
                    act.activation(vx[l][:, b, :], bk[g0 + n % 2][0:TK, 0:D], ACT.Copy).then_inc(q("vE"), 1)

            def norm(k, m, src, dst, done, waits=()):
                act.wait_ge(q(f"nb{k}"), m + 1)
                for w, n in waits:
                    if n > 0:
                        act.wait_ge(q(w), n)
                for h in range(2):
                    i = act.activation(dst(h), src(h), ACT.Identity, bias=nb[k][:, m % 2, h:h + 1], scale=rs[k][:, m % 2, h:h + 1])
                i.then_inc(q(done), 1)

            def evac(dst, src, ready, n, done, waits=()):
                act.wait_ge(q(ready), n)
                for w, v in waits:
                    if v > 0:
                        act.wait_ge(q(w), v)
                act.activation(dst, src, ACT.Copy).then_inc(q(done), 1)

            def softmax_exp(b, ready, done, free):
                act.wait_ge(q(ready), b + 1)
                if b >= 2:
                    act.wait_ge(q(free), b - 1)
                for h in range(2):
                    i = act.activation(pr[b % 2][:, h, :], bk[5][:, h * TK:(h + 1) * TK], ACT.Exp, bias=nm[:, b % 2, h:h + 1],
                                       accum_out=sm[:, b % 2, h:h + 1])
                i.then_inc(q(done), 1)

            for s in range(B + 3):
                if s >= 3:
                    b = s - 3
                    norm(1, b, lambda h: y2[b % 2][:, h, :], lambda h: xt[:, 2 * b + h, :], "n2")
                if 1 <= s <= B:
                    b = s - 1
                    norm(0, b, lambda h: bk[2][:, h * D:(h + 1) * D], lambda h: xs[b % 2][:, h, :], "n1", [("y2", b - 1), ("x1T", b - 1)])
                if s < B:
                    act.wait_ge(q("z"), s + 1)
                    if s == 0:
                        act.wait_ge(q("bh"), 1)
                    if s >= 1:
                        act.wait_ge(q("dv"), s)
                        act.wait_ge(q("a1"), s)
                    for c in range(DC):
                        i = act.activation(th[:, c, :], bk[0][:, c * T:(c + 1) * T], ACT.Tanh, bias=bh[:, 0, c:c + 1], scale=0.5)
                    i.then_inc(q("th"), 1)
                    act.wait_ge(q("v"), s + 1)
                    for c in range(DC):
                        i = act.activation(vb[:, c, :], bk[1][:, c * T:(c + 1) * T], ACT.Identity, bias=bh[:, 1, c:c + 1], scale=0.5)
                    i.then_inc(q("vb"), 1)
                if s == 1:
                    keys(0, 4, 6)
                if 1 <= s <= B:
                    b = s - 1
                    evac(xsf[b % 2][:].rearrange("p c t -> p (c t)"), bk[3][:], "x1T", b + 1, "x1f", [("scP", b - 1)])
                if 2 <= s <= B + 1:
                    b = s - 2
                    evac(pt[b % 2][:], bk[6][0:TK, 0:T], "pT", b + 1, "pte", [("pv", b - 1)])
                if s >= 3:
                    b = s - 3
                    evac(x2f[b % 2][:].rearrange("p c t -> p (c t)"), bk[4][:], "x2T", b + 1, "x2f", [("lg", b - 1)])
                if 1 <= s <= B:
                    softmax_exp(s - 1, "mx", "ex", "pT")
            act.wait_ge(q("bdP"), 1)
            act.activation(bd[:, :, :], bk[2][:, 0:2 * P].rearrange("p (c n) -> p c n", c=DC), ACT.Copy).then_inc(q("bdE"), 1)
            act.wait_ge(q("r1"), 1)
            act.activation(rA[:, 128:256], rA[:, 0:128], ACT.Exp).then_inc(q("r2"), 1)
            keys(1, 3, 5)
            act.wait_ge(q("UP"), 1)
            act.activation(quw[:, :, D:2 * D], bk[2][:].rearrange("p (c n) -> p c n", c=DC), ACT.Copy).then_inc(q("UE"), 1)
            act.activation(quw[:, :, 0:D], qw[:], ACT.Copy).then_inc(q("UE"), 1)

            def inp_high(e, j):
                n = e * ET + j
                act.wait_ge(q("ttr"), n + 1)
                if e >= 1 and j == 0:
                    act.wait_ge(q("mm1"), 8 * e)
                act.activation(inpH[:, :, j * P:(j + 1) * P], bk[6 + n % 2][:, 0:D].rearrange("p (c t) -> p c t", c=DC),
                               ACT.Copy).then_inc(q("inH"), 1)

            def win_high(e, c):
                act.wait_ge(q("in_wi"), 16 * (e + 1))
                act.activation(winH[:, c, :], win[:, c, :], ACT.Copy).then_inc(q("wiH"), 1)

            def hid_high(n):
                u = n % 8
                f, hf = u % FC, u // FC
                act.wait_ge(q("hid"), n + 1)
                act.activation(hidH[:, f, hf * HALF:(hf + 1) * HALF], hid[n % 2], ACT.Copy).then_inc(q("hiH"), 1)

            for c in range(DC):
                win_high(0, c)
            for j in range(3):
                inp_high(0, j)
            for e in range(E0):
                for u in range(8):
                    n = 8 * e + u
                    if n == FC:
                        inp_high(0, 3)
                        inp_high(0, 4)
                    act.wait_ge(q("mm1"), n + 1)
                    if n >= 2:
                        act.wait_ge(q("hid"), n - 1)
                    act.activation(ge[n % 2], bk[n % 2][:, 0:HALF], ACT.Gelu).then_inc(q("ge"), 1)
                    if u == 0:
                        if e >= 1:
                            act.wait_ge(q("mm2"), ET * e)
                        act.wait_ge(q("in_wo"), 16 * (e + 1))
                        act.activation(wouH, wou, ACT.Copy).then_inc(q("woH"), 1)
                    else:
                        hid_high(n - 1)
                hid_high(8 * e + 7)
                if e + 1 < E0:
                    for j in range(ET):
                        inp_high(e + 1, j)
                        if j in (2, 3):
                            win_high(e + 1, j - 2)

            def front(m):
                evac(xsf[m % 2][:].rearrange("p c t -> p (c t)"), bk[4][:], "x3T", m + 1, "x3f", [("qu", 2 * m - 2)])

            def front_out(m):
                g = m // 4
                for h in range(2):
                    n = 2 * m + h
                    act.wait_ge(q("qu"), n + 1)
                    t = 2 * (m % 4) + h
                    act.activation((qa, qa2)[g][:, t, :], bk[h][:, 0:D], ACT.Copy)
                    act.activation((ua, ua2)[g][:, t, :], bk[h][:, D:2 * D], ACT.Copy).then_inc(q("que"), 1)

            def squares(m):
                g, i = m // 4, m % 4
                for h in range(2):
                    t = 2 * i + h
                    if t == 0:
                        continue
                    if h == 0:
                        act.wait_ge(q("difP"), 3 * g + i)
                    else:
                        act.wait_ge(q("dif"), m + 1)
                    o = (0, 6 * D)[h]
                    act.activation(dif[m % 2][:, o:o + t * D], dif[m % 2][:, o:o + t * D], ACT.Square).then_inc(q("sq"), 1)

            def kernels(m):
                g, i = m // 4, m % 4
                at3 = att[g].rearrange("p (t s h) -> p t s h", t=B, s=B)
                act.wait_ge(q("ds"), m + 1)
                for h in range(2):
                    t = 2 * i + h
                    if t:
                        a = t * (t - 1) // 2
                        act.activation(at3[:, t, 0:t, :], dsq[:, a:a + t, :], ACT.Exp, scale=-HD ** -0.5).then_inc(q("e1"), 1)

            def norm3(m):
                norm(2, m, lambda h: y3[m % 2][:, h, :], lambda h: xt[:, tiles_of(m)[h], :], "n3")
            norm3(0)
            for f in range(8):
                front(f)
                if f < 7:
                    norm3(f + 1)
                front_out(f)
                if 1 <= f:
                    squares(f - 1)
                if 2 <= f:
                    kernels(f - 2)

            def attended_fm(s, h):
                evac(aof[h].rearrange("p c t -> p (c t)"), bk[2 + h][:, 0:256], "ao", 2 * s + h + 1, "aof", [("op", 2 * s + h - 1)])
            attended_fm(0, 0)
            for s in range(8 + 3):
                b = s - 1
                if 0 <= b < 8:
                    evac(x4f[b % 2][:].rearrange("p c t -> p (c t)"), bk[4][:], "x4T", b + 1, "x4f", [("scQ", b - 1)])
                if 0 <= b < 8:
                    softmax_exp(b, "mx2", "ex2", "pT2")
                if 0 <= b < 8:
                    evac(pt[b % 2][:], bk[6][0:TK, 0:T], "pT2", b + 1, "pte2", [("pv2", b - 1)])
                if s < 8:
                    attended_fm(s, 1)
                if 0 <= b < 8:
                    norm(4, b, lambda h: y2[b % 2][:, h, :], lambda h: x5s[b % 2][:, h, :], "n5", [("y6", b - 1), ("x5T", b - 1)])
                if s >= 3:
                    d = s - 3
                    norm(5, d, lambda h: y6b[d % 2][:, h, :], lambda h: y6[d % 2][:, h, :], "n6", [(f"od{d % 2}", 32 * (d // 2))])
                if 0 <= b < 8:
                    act.wait_ge(q("x5T"), b + 1)
                    if b >= 1:
                        act.wait_ge(q("eh"), b)
                    if b >= 2:
                        act.wait_ge(q("fm"), 2 * b - 2)
                    for c in range(DC):
                        for h in range(2):
                            i = act.activation(x5f[b % 2][:, c, h * P:(h + 1) * P], bk[4][:, c * T + h * P:c * T + (h + 1) * P], ACT.Copy,
                                               accum_out=emb[:, c, h:h + 1])
                    i.then_inc(q("x5f"), 1)
                if s < 8:
                    norm(3, s, lambda h: y4[s % 2][:, h, :], lambda h: xs[s % 2][:, h, :], "n4", [("y5", s - 1), ("x4T", s - 1)])
                if s < 2:
                    kernels(s + 6)
                if s == 0:
                    squares(7)
                if s < 7:
                    attended_fm(s + 1, 0)

        @block.tensor
        def _(pe):
            def tr4(dst, src, ready, n, done, waits=(), strided=False):
                pe.wait_ge(q(ready), n)
                for w, v in waits:
                    if v > 0:
                        pe.wait_ge(q(w), v)
                for a in range(2):
                    for c in range(2):
                        blk = src[:, a, c::2] if strided else src[:, a, c * P:(c + 1) * P]
                        i = pe.transpose(dst[:, c * 256 + a * P:c * 256 + (a + 1) * P], blk, ident)
                i.then_inc(q(done), 1)

            def keys(l, k0, g0, part):
                if part == 0:
                    if l == 0:
                        pe.wait_ge(q("in_cx"), 96)
                        pe.wait_ge(q("in_k"), 144)
                    for c in range(DC):
                        for h in range(2):
                            n = l * 4 + c * 2 + h
                            if n >= 2:
                                pe.wait_ge(q("kE"), n - 1)
                            for k in range(2):
                                r = CK + k
                                i = pe.matmul(bk[k0 + n % 2][:, 0:308], wk[l][0:r, k, c * P:(c + 1) * P], cx[0:r, k, h * 308:(h + 1) * 308],
                                              start=k == 0, stop=k == 1)
                            i.then_inc(q("kP"), 1)
                    return
                pe.wait_ge(q("kE"), 4 * l + 4)
                for c in range(DC):
                    for h in range(2):
                        n = l * 4 + c * 2 + h
                        if n >= 2:
                            pe.wait_ge(q("GE"), n - 1)
                        for k in range(DC):
                            i = pe.matmul(bk[g0 + n % 2][:, 0:308], wq[l][:, k, c * P:(c + 1) * P], kf[:, k, h * 308:(h + 1) * 308],
                                          start=k == 0, stop=k == DC - 1)
                        i.then_inc(q("GP"), 1)
                pe.wait_ge(q("bqb"), l + 1)
                for h in range(2):
                    n = l * 2 + h
                    if n >= 2:
                        pe.wait_ge(q("bqE"), n - 1)
                    for k in range(DC):
                        i = pe.matmul(bk[k0 + n % 2][:, 0:308], bqb[l][:, k, :], kf[:, k, h * 308:(h + 1) * 308], start=k == 0, stop=k == DC - 1)
                    i.then_inc(q("bqP"), 1)
                pe.wait_ge(q("GE"), 4 * l + 4)
                for b in range(B):
                    n = l * B + b
                    if n >= 2:
                        pe.wait_ge(q("vE"), n - 1)
                    for k in range(2):
                        r = CK + k
                        i = pe.matmul(bk[g0 + n % 2][0:TK, 0:D], cx[0:r, k, b * TK:(b + 1) * TK], wvx[l][0:r, k, :], start=k == 0, stop=k == 1)
                    i.then_inc(q("vP"), 1)

            def scores(l, b, xfm, ready, free, done, seqs):
                pe.wait_ge(q(ready), b + 1)
                if b >= 1:
                    pe.wait_ge(q(free), b)
                for h in range(2):
                    cs = slice(seqs[h] * TK, (seqs[h] + 1) * TK)
                    for k in range(DC):
                        pe.matmul(bk[5][:, h * TK:(h + 1) * TK], xfm[:, k, h * P:(h + 1) * P], G[l][:, k, cs], start=k == 0, stop=False)
                    i = pe.matmul(bk[5][:, h * TK:(h + 1) * TK], C["sel0"], bqk[l][:, cs], start=False, stop=True)
                i.then_inc(q(done), 1)

            def probs_tr(b, ready, free, done):
                pe.wait_ge(q(ready), b + 1)
                if b >= 1:
                    pe.wait_ge(q(free), b)
                for h in range(2):
                    i = pe.transpose(bk[6][0:TK, h * P:(h + 1) * P], pr[b % 2][:, h, :], ident)
                i.then_inc(q(done), 1)

            def values(l, b, ready, free, done, seqs):
                pe.wait_ge(q(ready), b + 1)
                if b >= 1:
                    pe.wait_ge(q(free), b)
                for h in range(2):
                    i = pe.matmul(bk[7][:, h * D:(h + 1) * D], pt[b % 2][:, h * P:(h + 1) * P], vx[l][:, seqs[h], :], start=True, stop=True)
                i.then_inc(q(done), 1)

            for s in range(B + 3):
                if 1 <= s <= B:
                    b = s - 1
                    pe.wait_ge(q("y1"), b + 1)
                    if b == 0:
                        pe.wait_ge(q("in_c"), 48)
                    if b >= 1:
                        pe.wait_ge(q("n1"), b)
                    for h in range(2):
                        for c in range(DC):
                            i = pe.transpose(bk[2][:, h * D + c * P:h * D + (c + 1) * P], y1[b % 2][:, c, h * P:(h + 1) * P], ident)
                    i.then_inc(q("yT"), 1)
                if s < B:
                    if s < 3:
                        pe.wait_ge(q(f"in_x{s}"), 16)
                    if s == 0:
                        pe.wait_ge(q("in_d"), 16)
                    for w, bank, done, free in ((wd, 0, "z", "th"), (wv, 1, "v", "vb")):
                        if s >= 1:
                            pe.wait_ge(q(free), s)
                        if s == 0 and bank == 1:
                            pe.wait_ge(q("in_a"), 32)
                        for c in range(DC):
                            for k in range(DC):
                                i = pe.matmul(bk[bank][:, c * T:(c + 1) * T], w[:, k, c * P:(c + 1) * P], xf[:, k, s * T:(s + 1) * T],
                                              start=k == 0, stop=k == DC - 1)
                        i.then_inc(q(done), 1)
                if s == 1:
                    keys(0, 4, 6, 0)
                    keys(0, 4, 6, 1)
                    pe.wait_ge(q("bqE"), 2)
                    pe.wait_ge(q("vE"), B)
                if 1 <= s <= B:
                    b = s - 1
                    tr4(bk[3], xs[b % 2], "n1", b + 1, "x1T", [("x1f", b)])
                if 2 <= s <= B + 1:
                    probs_tr(s - 2, "ex", "pte", "pT")
                if s >= 3:
                    b = s - 3
                    tr4(bk[4], xt[:, 2 * b:2 * b + 2, :], "n2", b + 1, "x2T", [("x2f", b)])
                if 2 <= s <= B + 1:
                    values(0, s - 2, "pte", "y2", "pv", (s - 2, s - 2))
                if 1 <= s <= B:
                    b = s - 1
                    scores(0, b, xsf[b % 2], "x1f", "ex", "scP", (b, b))
                if s >= 3:
                    b = s - 3
                    pe.wait_ge(q("x2f"), b + 1)
                    pe.wait_ge(q("pte"), min(b + 2, B))
                    for h in range(2):
                        n = 2 * b + h
                        for k in range(DC):
                            i = pe.matmul(bk[6][:, 256 + n * E0:256 + (n + 1) * E0], x2f[b % 2][:, k, h * P:(h + 1) * P], wg[:, k, :],
                                          start=k == 0, stop=k == DC - 1)
                    i.then_inc(q("lg"), 1)

            pe.wait_ge(q("in_w"), 96)
            pe.wait_ge(q("n1"), B)
            for c in range(DC):
                for k in range(DC):
                    i = pe.matmul(bk[2][:, c * P:(c + 1) * P], qw[:, k, c * P:(c + 1) * P], vw[:, k, c * P:(c + 1) * P], start=k == 0, stop=k == DC - 1)
            i.then_inc(q("bdP"), 1)
            pe.wait_ge(q("x2f"), B)
            keys(1, 3, 5, 0)
            pe.wait_ge(q("rM"), 1)
            pe.matmul(bk[0][:, 0:256], ltri[:], rMb, start=True, stop=True)
            pe.matmul(bk[0][:, 256:512], onesb[:], rMb, start=True, stop=True).then_inc(q("rW"), 1)
            keys(1, 3, 5, 1)
            pe.wait_ge(q("bd"), 1)
            for c in range(DC):
                for h in range(DC):
                    i = pe.matmul(bk[2][:, c * D + h * P:c * D + (h + 1) * P], qwT[:, h, c * P:(c + 1) * P], bd[:, h, :], start=True, stop=True)
            i.then_inc(q("UP"), 1)
            for n in range(2 * NT):
                if n % (NT // 2) == 0:
                    pe.wait_ge(q("oh"), n // (NT // 2) + 1)
                i = pe.matmul(bk[1][:, 0:3 * NST], ohl[:, n, :], ohh[:, n, :], start=n == 0, stop=n == 2 * NT - 1)
            i.then_inc(q("tab"), 1)
            pe.wait_ge(q("UE"), 2)
            pe.wait_ge(q("vE"), 2 * B)

            def inp_tr(e, j):
                n = e * ET + j
                pe.wait_ge(q(f"ga{e % 2}{j}"), 16 * (e // 2 + 1))
                if n >= 2:
                    pe.wait_ge(q("inL"), n - 1)
                for c in range(DC):
                    i = pe.transpose(bk[6 + n % 2][:, c * P:(c + 1) * P], inpT[e % 2][:, j, c * P:(c + 1) * P], ident)
                i.then_inc(q("ttr"), 1)

            def product(dst, lhs, rhs):
                (lh, ll), (rh, rl) = lhs, rhs
                last = len(lh) - 1
                for k in range(last + 1):
                    pe.matmul(dst, lh[k], rh[k], start=k == 0, stop=False)
                    pe.matmul(dst, lh[k], rl[k], start=False, stop=False)
                    i = pe.matmul(dst, ll[k], rh[k], start=False, stop=k == last)
                return i

            for j in range(3):
                inp_tr(0, j)
            for e in range(E0):
                pe.wait_ge(q("wiL"), e + 1)
                for u in range(8):
                    n = 8 * e + u
                    f, hf = u % FC, u // FC
                    if u == 0:
                        pe.wait_ge(q("inL"), ET * e + 3)
                    if u == FC:
                        if e == 0:
                            inp_tr(0, 3)
                            inp_tr(0, 4)
                        pe.wait_ge(q("inL"), ET * (e + 1))
                    if n >= 2:
                        pe.wait_ge(q("ge"), n - 1)
                        pe.wait_ge(q("hid"), n - 1)
                    for part in range(2):
                        a = part * F0 + f * P
                        i = product(bk[n % 2 + 2 * part][:, 0:HALF],
                                    [[w[:, k, a:a + P] for k in range(DC)] for w in (winH, winL)],
                                    [[x[:, k, hf * HALF:(hf + 1) * HALF] for k in range(DC)] for x in (inpH, inpL)])
                    i.then_inc(q("mm1"), 1)
                if e + 1 < E0:
                    inp_tr(e + 1, 0)
                    inp_tr(e + 1, 1)
                pe.wait_ge(q("woL"), e + 1)
                for j in range(ET):
                    n = e * ET + j
                    if j == 0:
                        pe.wait_ge(q("hiL"), 8 * e + FC)
                    if j == 2:
                        pe.wait_ge(q("hiL"), 8 * (e + 1))
                    if n >= 2:
                        pe.wait_ge(q("oe"), n - 1)
                    i = product(bk[4 + n % 2][:, 0:D],
                                [[x[:, k, j * P:(j + 1) * P] for k in range(FC)] for x in (hidH, hidL)],
                                [[w[:, k, :] for k in range(FC)] for w in (wouH, wouL)])
                    i.then_inc(q("mm2"), 1)
                    if e + 1 < E0 and j < 3:
                        inp_tr(e + 1, j + 2)

            def front(m):
                a, b_ = tiles_of(m)
                tr4(bk[4], xt[:, a:b_ + 1:2, :], "n3", m + 1, "x3T", [("x3f", m)])
                pe.wait_ge(q("x3f"), m + 1)
                for h in range(2):
                    n = 2 * m + h
                    if n >= 2:
                        pe.wait_ge(q("que"), n - 1)
                    for k in range(DC):
                        i = pe.matmul(bk[h][:], xsf[m % 2][:, k, h * P:(h + 1) * P], quw[:, k, :], start=k == 0, stop=k == DC - 1)
                    i.then_inc(q("qu"), 1)

            def attend(s, h):
                n = 2 * s + h
                pe.wait_ge(q("prd"), n + 1)
                if n >= 2:
                    pe.wait_ge(q("aof"), n - 1)
                parts = (B, B // 2)[h]
                for c in range(DC):
                    for u in range(parts):
                        i = pe.matmul(bk[2 + h][:, c * P:(c + 1) * P], prod[h][:, u, c * P:(c + 1) * P], ident, start=u == 0, stop=u == parts - 1)
                i.then_inc(q("ao"), 1)

            pe.wait_ge(q("oe"), NST)
            for m in range(8):
                front(m)
            pe.wait_ge(q("que"), 16)
            attend(0, 0)
            for s in range(8 + 3):
                b = s - 1
                seqs = (2 * (b % 4), 2 * (b % 4) + 1)
                if 0 <= b < 8:
                    tr4(bk[4], xs[b % 2], "n4", b + 1, "x4T", [("x5f", b), ("x3f", 8)])
                    scores(1, b, x4f[b % 2], "x4f", "ex2", "scQ", seqs)
                if 2 <= s <= 9:
                    d = s - 2
                    pe.wait_ge(q("eh"), d + 1)
                    pe.wait_ge(q("pte2"), min(d + 1, 8))
                    for k in range(DC):
                        i = pe.matmul(bk[6][:, 256:256 + 2 * NB6], C["ones"], eh[:, k, :, :].rearrange("p a b -> p (a b)"), start=k == 0, stop=k == DC - 1)
                    i.then_inc(q("pj"), 1)
                if s < 8:
                    attend(s, 1)
                if 0 <= b < 8:
                    if b >= 1:
                        pe.wait_ge(q("pjr"), b)
                    probs_tr(b, "ex2", "pte2", "pT2")
                    values(1, b, "pte2", "y5", "pv2", seqs)
                if s >= 3:
                    d = s - 3
                    for h in range(2):
                        n = 2 * d + h
                        pe.wait_ge(q("ws"), n + 1)
                        if d >= 1:
                            pe.wait_ge(q("y6"), d)
                        for k in range(DC):
                            i = pe.matmul(bk[1][:, h * D:(h + 1) * D], x5f[d % 2][:, k, h * P:(h + 1) * P], ws[n % 2][:, k * D:(k + 1) * D],
                                          start=k == 0, stop=k == DC - 1)
                        i.then_inc(q("fm"), 1)
                if s < 8:
                    for h in range(2):
                        n = 2 * s + h
                        pe.wait_ge(q("aof"), n + 1)
                        if n >= 2:
                            pe.wait_ge(q("y4"), s)
                        for k in range(DC):
                            i = pe.matmul(bk[0][:, h * D:(h + 1) * D], aof[h][:, k, :], woT[:, k, :], start=k == 0, stop=k == DC - 1)
                        i.then_inc(q("op"), 1)
                if 0 <= b < 8:
                    tr4(bk[4], x5s[b % 2], "n5", b + 1, "x5T", [("x4f", b + 1)], strided=True)
                if s < 7:
                    attend(s + 1, 0)

        @block.vector
        def _(v):
            def chain(i):
                link[0] += 1
                i.then_inc(q("own"), 1)
                v.wait_ge(q("own"), link[0])
            link = [0]

            v.wait_ge(q("in_a"), 32)
            v.tensor_scalar(bh[:], bdv[:], 0.5, None, ALU.mult).then_inc(q("bh"), 1)
            def bias_rows():
                v.wait_ge(q("in_c"), 48)
                v.wait_ge(q("in_k"), 144)
                for l in range(2):
                    for k in range(DC):
                        i = v.tensor_scalar(bqb[l][:, k, :], C["ones"], bq[l][:, k:k + 1], None, ALU.mult)
                    i.then_inc(q("bqb"), 1)

            def stats(k, m, src, ready=None):
                p = m % 2
                if ready:
                    v.wait_ge(q(ready), m + 1)
                for h in range(2):
                    i = v.bn_stats(st[k][:, p, h, :], src(h))
                chain(i)
                if m >= 2:
                    v.wait_ge(q(f"nb{k}"), m - 1)
                for h in range(2):
                    i = v.bn_aggr(mv[k][:, p, h, :], st[k][:, p, h, :])
                i.then_inc(q(f"mv{k}"), 1)

            def row_max(b, ready, done):
                v.wait_ge(q(ready), b + 1)
                v.tensor_reduce(nm[:, b % 2, :], bk[5][:, 0:2 * TK].rearrange("p (h n) -> p h n", h=2), AX.X, ALU.max, negate=True).then_inc(q(done), 1)

            def attended(b, pv, y, free, k):
                v.wait_ge(q(pv), b + 1)
                if b >= 2:
                    v.wait_ge(q(free), b - 1)
                chain(v.reciprocal(rc[:, b % 2, :], sm[:, b % 2, :]))
                for h in range(2):
                    i = v.scalar_tensor_tensor(out=y2[b % 2][:, h, :], in0=bk[7][:, h * D:(h + 1) * D], scalar=rc[:, b % 2, h:h + 1],
                                               in1=xs[b % 2][:, h, :], op0=ALU.mult, op1=ALU.add)
                i.then_inc(q(y), 1)
                v.wait_ge(q(y), b + 1)
                stats(k, b, lambda h: y2[b % 2][:, h, :])

            for s in range(B + 3):
                if 1 <= s <= B:
                    stats(0, s - 1, lambda h: bk[2][:, h * D:(h + 1) * D], "yT")
                if s < B:
                    v.wait_ge(q("th"), s + 1)
                    v.wait_ge(q("vb"), s + 1)
                    v.scalar_tensor_tensor(out=dv1, in0=th, scalar=1.0, in1=vb[:], op0=ALU.add, op1=ALU.mult).then_inc(q("dv"), 1)
                    v.wait_ge(q("dv"), s + 1)
                    v.wait_ge(q("a1"), s + 1)
                    for c in range(DC):
                        i = v.tensor_tensor_scan(hs[:, c, :], a1[:, c, :], dv1[:, c, :], 0.0, ALU.mult, ALU.add)
                    i.then_inc(q("scan"), 1)
                    v.wait_ge(q("scan"), s + 1)
                    if s >= 2:
                        v.wait_ge(q("yT"), s - 1)
                    if s < 3:
                        v.wait_ge(q(f"in_x{s}"), 16)
                    v.tensor_tensor(y1[s % 2][:], hs, xf[:, :, s * T:(s + 1) * T], ALU.add).then_inc(q("y1"), 1)
                if s == 0:
                    bias_rows()
                if 2 <= s <= B + 1:
                    attended(s - 2, "pv", "y2", "n2", 1)
                if 1 <= s <= B:
                    row_max(s - 1, "scP", "mx")

            def R(a):
                return rA[:, a * 128:(a + 1) * 128].rearrange("p (n e) -> p n e", e=E0)
            sc_ = sb_small
            k2 = NT * 2

            def over(x, w=E0):
                return x.unsqueeze(2).to_broadcast([P, x.shape[1], w])
            v.wait_ge(q("lg"), B)
            lg = bk[6][:, 256:384].rearrange("p (n e) -> p n e", e=E0)
            chain(v.tensor_reduce(sc_[:, 0, 0:NT], lg, AX.X, ALU.max))
            v.tensor_tensor(R(0), lg, over(sc_[:, 0, 0:NT]), ALU.subtract).then_inc(q("r1"), 1)
            v.wait_ge(q("r2"), 1)
            chain(v.tensor_reduce(sc_[:, 1, 0:NT], R(1), AX.X, ALU.add))
            chain(v.reciprocal(sc_[:, 2, 0:NT], sc_[:, 1, 0:NT]))
            chain(v.tensor_tensor(R(2), R(1), over(sc_[:, 2, 0:NT]), ALU.mult))
            w8 = C["w8"].rearrange("p (n e) -> p n e", e=E0)
            M = rA[:, 1024:1280].rearrange("p (n e) -> p n e", e=E0)
            top = sc_[:, 3, 0:k2]
            c8 = sc_[:, 4, 0:k2]
            for k in range(2):
                a, b_ = k * NT, (k + 1) * NT
                chain(v.tensor_reduce(top[:, a:b_], R(2), AX.X, ALU.max))
                chain(v.tensor_tensor(R(3), R(2), over(top[:, a:b_]), ALU.is_equal))
                chain(v.tensor_tensor(R(4), R(3), w8, ALU.mult))
                chain(v.tensor_reduce(c8[:, a:b_], R(4), AX.X, ALU.max))
                chain(v.tensor_tensor(M[:, a:b_, :], w8, over(c8[:, a:b_]), ALU.is_equal))
                if k == 0:
                    chain(v.scalar_tensor_tensor(out=R(2), in0=M[:, 0:NT, :], scalar=-2.0, in1=R(2), op0=ALU.mult, op1=ALU.add))
            v.tensor_copy(rMb, rA[:, 1024:1280]).then_inc(q("rM"), 1)
            v.wait_ge(q("rW"), 1)
            totE = rA[:, 1280:1536]
            incl = rA[:, 1536:1792]
            chain(v.tensor_copy(totE.rearrange("p (e n) -> p n e", e=E0), bk[0][:, 256:512].rearrange("p (n e) -> p n e", e=E0)))
            chain(v.tensor_tensor_scan(incl, C["smask"], totE, 0.0, ALU.mult, ALU.add))
            chain(v.tensor_tensor(incl, incl, totE, ALU.subtract))
            loc8 = rA[:, 1792:2048].rearrange("p (n e) -> p n e", e=E0)
            chain(v.tensor_tensor(loc8, bk[0][:, 0:256].rearrange("p (n e) -> p n e", e=E0), incl.rearrange("p (e n) -> p n e", e=E0), ALU.add))
            chain(v.tensor_tensor(loc8, loc8, M, ALU.mult))
            loc, hi, lo, keep = (sc_[:, i, 0:k2] for i in (5, 6, 7, 8))
            chain(v.tensor_reduce(loc, loc8, AX.X, ALU.add))
            chain(v.tensor_scalar(hi, loc, float(P), None, ALU.is_ge))
            for j in range(2, ET):
                chain(v.scalar_tensor_tensor(out=hi, in0=loc, scalar=float(P * j), in1=hi, op0=ALU.is_ge, op1=ALU.add))
            chain(v.scalar_tensor_tensor(out=lo, in0=hi, scalar=-float(P), in1=loc, op0=ALU.mult, op1=ALU.add))
            chain(v.scalar_tensor_tensor(out=hi, in0=c8, scalar=-float(ET), in1=hi, op0=ALU.mult, op1=ALU.add))
            chain(v.tensor_scalar(keep, loc, float(CAP), None, ALU.is_lt))
            chain(v.tensor_scalar(hi, hi, float(ET * E0) + 1000.0, None, ALU.add))
            chain(v.scalar_tensor_tensor(out=hi, in0=keep, scalar=-1000.0, in1=hi, op0=ALU.mult, op1=ALU.add))
            ohf = rA[:, 2048:2048 + 1280].rearrange("p (n c) -> p n c", n=k2)
            chain(v.tensor_tensor(ohf, C["iota"][:, 0:NST].unsqueeze(1).to_broadcast([P, k2, NST]), over(hi, NST), ALU.is_equal))
            v.tensor_copy(ohh[:, :, 2 * NST:3 * NST], ohf)
            v.tensor_scalar(ohh[:, :, NST:2 * NST], ohf, C["pcol"], None, ALU.mult)
            v.tensor_tensor(ohh[:, :, 0:NST], ohf, over(C["acon"], NST), ALU.mult)
            for h in range(4):
                r = slice(h * k2 // 4, (h + 1) * k2 // 4)
                v.tensor_tensor(ohl[:, r, :], C["iota"].unsqueeze(1).to_broadcast([P, k2 // 4, P]), over(lo[:, r], P), ALU.is_equal).then_inc(q("oh"), 1)
            v.wait_ge(q("tab"), 1)
            tb = sb_tab
            chain(v.tensor_copy(tb[:, 0:3 * NST], bk[1][:, 0:3 * NST]))
            chain(v.tensor_tensor(tb[:, 120:160], tb[:, 0:40], tb[:, 40:80], ALU.add))
            chain(v.tensor_scalar(tb[:, 160:200], tb[:, 120:160], float(S), -float(S), ALU.is_ge, ALU.mult))
            v.tensor_tensor(idx[:, 0, :], tb[:, 120:160], tb[:, 160:200], ALU.add)
            chain(v.scalar_tensor_tensor(out=tb[:, 200:240], in0=tb[:, 80:120], scalar=-BIG, in1=tb[:, 120:160], op0=ALU.mult, op1=ALU.add))
            v.tensor_scalar(idx[:, 1, :], tb[:, 200:240], BIG, None, ALU.add).then_inc(q("idx"), 1)
            g0 = sc_[:, 9, 0:k2]
            den = sc_[:, 10, 0:NT]
            chain(v.tensor_tensor(g0, top, keep, ALU.mult))
            chain(v.tensor_tensor(den, g0[:, 0:NT], g0[:, NT:k2], ALU.add))
            chain(v.tensor_scalar(den, den, 1e-9, None, ALU.max))
            chain(v.reciprocal(sc_[:, 11, 0:NT], den))
            for k in range(2):
                i = v.tensor_tensor(gate[:, k, :], g0[:, k * NT:(k + 1) * NT], sc_[:, 11, 0:NT], ALU.mult)
            chain(i)

            def inp_low(e, j):
                n = e * ET + j
                v.wait_ge(q("inH"), n + 1)
                v.tensor_tensor(inpL[:, :, j * P:(j + 1) * P], bk[6 + n % 2][:, 0:D].rearrange("p (c t) -> p c t", c=DC),
                                inpH4[:, :, j * P:(j + 1) * P], ALU.subtract).then_inc(q("inL"), 1)

            def hid_low(n):
                u = n % 8
                f, hf = u % FC, u // FC
                v.wait_ge(q("hiH"), n + 1)
                v.tensor_tensor(hidL[:, f, hf * HALF:(hf + 1) * HALF], hid[n % 2], hidH4[:, f, hf * HALF:(hf + 1) * HALF],
                                ALU.subtract).then_inc(q("hiL"), 1)

            def win_low(e, c):
                v.wait_ge(q("wiH"), DC * e + c + 1)
                if e == 0:
                    v.wait_ge(q("UP"), 1)
                i = v.tensor_tensor(winL[:, c, :], win[:, c, :], winH4[:, c, :], ALU.subtract)
                if c == DC - 1:
                    i.then_inc(q("wiL"), 1)

            def back(n):
                v.wait_ge(q("mm2"), n + 1)
                if n >= 4:
                    v.wait_ge(q(f"sc{n % 4}"), 16 * (n // 4))
                v.tensor_copy(oe[n % 4], bk[4 + n % 2][:, 0:D]).then_inc(q("oe"), 1)

            for c in range(DC):
                win_low(0, c)
            for j in range(3):
                inp_low(0, j)
            for e in range(E0):
                for u in range(8):
                    n = 8 * e + u
                    if n == FC:
                        inp_low(0, 3)
                        inp_low(0, 4)
                    v.wait_ge(q("ge"), n + 1)
                    if n >= 2:
                        v.wait_ge(q("hiL"), n - 1)
                    v.tensor_tensor(hid[n % 2], ge[n % 2], bk[2 + n % 2][:, 0:HALF], ALU.mult).then_inc(q("hid"), 1)
                    if u >= 1:
                        hid_low(n - 1)
                    if u == 2:
                        v.wait_ge(q("woH"), e + 1)
                        v.tensor_tensor(wouL, wou, wouH4, ALU.subtract).then_inc(q("woL"), 1)
                hid_low(8 * e + 7)
                if e + 1 < E0:
                    inp_low(e + 1, 0)
                    inp_low(e + 1, 1)
                for j in range(ET):
                    back(e * ET + j)
                    if e + 1 < E0 and j < 3:
                        inp_low(e + 1, j + 2)
                    if e + 1 < E0 and j in (2, 3):
                        win_low(e + 1, j - 2)

            def returned(m):
                v.wait_ge(q(f"yl{m % 2}"), 32 * (m // 2 + 1))
                if m >= 2:
                    v.wait_ge(q("n3"), m - 1)
                for h, n in enumerate(tiles_of(m)):
                    i = v.scalar_tensor_tensor(out=y3[m % 2][:, h, :], in0=yb[m % 2][:, h, 0, :], scalar=gate[:, 0, n:n + 1], in1=xt[:, n, :],
                                               op0=ALU.mult, op1=ALU.add)
                chain(i)
                for h, n in enumerate(tiles_of(m)):
                    i = v.scalar_tensor_tensor(out=y3[m % 2][:, h, :], in0=yb[m % 2][:, h, 1, :], scalar=gate[:, 1, n:n + 1], in1=y3[m % 2][:, h, :],
                                               op0=ALU.mult, op1=ALU.add)
                i.then_inc(q("y3"), 1)
                v.wait_ge(q("y3"), m + 1)
                stats(2, m, lambda h: y3[m % 2][:, h, :])

            def distances(m):
                g, i_ = m // 4, m % 4
                Q = (qa, qa2)[g]
                t = 2 * i_ + 1
                v.wait_ge(q("que"), 2 * m + 2)
                if m >= 2:
                    v.wait_ge(q("ds"), m - 1)
                v.tensor_tensor(dif[m % 2][:, 6 * D:(6 + t) * D].rearrange("p (s n) -> p s n", s=t), Q[:, t:t + 1, :].to_broadcast([P, t, D]), Q[:, 0:t, :],
                                ALU.subtract).then_inc(q("dif"), 1)

            def reduce_distances(m):
                g, i_ = m // 4, m % 4
                v.wait_ge(q("sq"), 7 * g + 2 * i_ + 1)
                if g == 1 and i_ == 0:
                    v.wait_ge(q("e1"), 7)
                for t in (2 * i_, 2 * i_ + 1):
                    if t:
                        a = t * (t - 1) // 2
                        o = 0 if t % 2 == 0 else 6 * D
                        i = v.tensor_reduce(dsq[:, a:a + t, :], dif[m % 2][:, o:o + t * D].rearrange("p (s h d) -> p s h d", h=NH, d=HD), AX.X, ALU.add)
                i.then_inc(q("ds"), 1)

            def weights(g):
                a = att[g]
                at3 = a.rearrange("p (t s h) -> p t s h", t=B, s=B)
                v.wait_ge(q("e1"), 7 * g + 7)
                for t in range(B):
                    i = v.memset(at3[:, t, t, :], 1.0)
                    if t:
                        i = v.tensor_copy(at3[:, 0:t, t, :], at3[:, t, 0:t, :])
                chain(i)
                chain(v.tensor_reduce(zz[:], a.rearrange("p (t s h) -> p t h s", t=B, s=B), AX.X, ALU.add))
                chain(v.reciprocal(rz[:], zz[:]))
                chain(v.tensor_tensor(at3, at3, rz[:].unsqueeze(2).to_broadcast([P, B, B, NH]), ALU.mult))

            def weigh(s, h):
                g = s // 4
                n = 2 * s + h
                t = 2 * (s % 4) + h
                if n >= 2:
                    v.wait_ge(q("ao"), n - 1)
                w = att[g].rearrange("p (t s h) -> p t s h", t=B, s=B)[:, t, :, :]
                v.tensor_tensor(prod[n % 2].rearrange("p s (h d) -> p (s h) d", d=HD),
                                (ua, ua2)[g].rearrange("p s (h d) -> p (s h) d", d=HD),
                                w.rearrange("p s h -> p (s h)").unsqueeze(2).to_broadcast([P, B * NH, HD]), ALU.mult).then_inc(q(("prd", "prw")[h]), 1)
                if h == 1:
                    v.wait_ge(q("prw"), s + 1)
                    v.tensor_tensor(prod[h][:, 0:B // 2, :], prod[h][:, 0:B // 2, :], prod[h][:, B // 2:B, :], ALU.add).then_inc(q("prd"), 1)

            def on_hyperplanes(b):
                v.wait_ge(q("x5f"), b + 1)
                if b >= 1:
                    v.wait_ge(q("pj"), b)
                for h in range(2):
                    i = v.tensor_tensor(eh[:, :, h, :], hyp[:], emb[:, :, h:h + 1].to_broadcast([P, DC, NB6]), ALU.mult)
                i.then_inc(q("eh"), 1)

            def V6(i):
                return rt[:, i, :].rearrange("p (h n) -> p h n", h=2)

            def projections(b):
                v.wait_ge(q("pj"), b + 1)
                v.tensor_copy(rt[:, 0, :], bk[6][:, 256:256 + 2 * NB6]).then_inc(q("pjr"), 1)

            e1, mn, fc, fl, bt, e2 = (rt[:, i, 0:2] for i in (3, 4, 5, 6, 7, 8))

            def hash_bits(b):
                v.wait_ge(q("pjr"), b + 1)
                v.scalar_tensor_tensor(out=rt[:, 1, :], in0=rt[:, 0, :], scalar=0.0, in1=C["p6"], op0=ALU.is_gt, op1=ALU.mult)
                chain(v.scalar_tensor_tensor(out=rt[:, 2, :], in0=rt[:, 0, :], scalar=-1.0, in1=rt[:, 0, :], op0=ALU.mult, op1=ALU.max))
                v.tensor_reduce(e1, V6(1), AX.X, ALU.add)
                chain(v.tensor_reduce(mn, V6(2), AX.X, ALU.min))

            def hash_flip(b):
                chain(v.tensor_tensor(V6(9), V6(2), over(mn, NB6), ALU.is_equal))
                chain(v.tensor_tensor(rt[:, 9, :], rt[:, 9, :], C["w6"], ALU.mult))
                chain(v.tensor_reduce(fc, V6(9), AX.X, ALU.max))
                chain(v.tensor_tensor(V6(9), C["w6"].rearrange("p (h n) -> p h n", h=2), over(fc, NB6), ALU.is_equal))
                v.tensor_tensor(rt[:, 10, :], rt[:, 9, :], C["p6"], ALU.mult)
                chain(v.tensor_tensor(rt[:, 11, :], rt[:, 9, :], rt[:, 1, :], ALU.mult))
                v.tensor_reduce(fl, V6(10), AX.X, ALU.add)
                chain(v.tensor_reduce(bt, V6(11), AX.X, ALU.add))
                chain(v.tensor_tensor(e2, e1, fl, ALU.add))
                chain(v.scalar_tensor_tensor(out=e2, in0=bt, scalar=-2.0, in1=e2, op0=ALU.mult, op1=ALU.add))
                if b >= 2:
                    v.wait_ge(q("we0"), 32 * (b - 1))
                    v.wait_ge(q("we1"), 32 * (b - 1))
                wi = widx[b % 2][:].rearrange("p (h k) -> p h k", k=2)
                v.tensor_scalar(wi[:, :, 0], e1, float(P), C["pcol"], ALU.mult, ALU.add)
                v.tensor_scalar(wi[:, :, 1], e2, float(P), C["pcol"], ALU.mult, ALU.add).then_inc(q("widx"), 1)

            returned(0)
            returned(1)
            for f in range(8):
                if f < 6:
                    returned(f + 2)
                if f == 7:
                    weights(0)
                if 1 <= f:
                    distances(f - 1)
                if 2 <= f:
                    reduce_distances(f - 2)
            weigh(0, 0)
            for s in range(8 + 3):
                b = s - 1
                if 2 <= s <= 9:
                    on_hyperplanes(s - 2)
                if s < 8:
                    weigh(s, 1)
                if 2 <= s <= 9:
                    projections(s - 2)
                if 0 <= b < 8:
                    row_max(b, "scQ", "mx2")
                if 8 <= s <= 9:
                    hash_bits(s - 2)
                    hash_flip(s - 2)
                if s < 7:
                    weigh(s + 1, 0)
                if s == 0:
                    distances(7)
                if 0 <= b < 8:
                    attended(b, "pv2", "y5", "n5", 4)
                if s < 2:
                    reduce_distances(s + 6)
                if s >= 3:
                    d = s - 3
                    v.wait_ge(q("fm"), 2 * d + 2)
                    if d >= 2:
                        v.wait_ge(q("n6"), d - 1)
                    v.scalar_tensor_tensor(out=y6b[d % 2][:].rearrange("p h n -> p (h n)"), in0=bk[1][:], scalar=0.5,
                                           in1=x5s[d % 2][:].rearrange("p h n -> p (h n)"), op0=ALU.mult, op1=ALU.add).then_inc(q("y6"), 1)
                    v.wait_ge(q("y6"), d + 1)
                    stats(5, d, lambda h: y6b[d % 2][:, h, :])
                if s < 8:
                    v.wait_ge(q("op"), 2 * s + 2)
                    v.wait_ge(q("xb"), s + 1)
                    if s >= 2:
                        v.wait_ge(q("n4"), s - 1)
                    v.tensor_tensor(y4[s % 2][:], bk[0][:].rearrange("p (h n) -> p h n", h=2), xbs[:], ALU.add).then_inc(q("y4"), 1)
                    v.wait_ge(q("y4"), s + 1)
                    stats(3, s, lambda h: y4[s % 2][:, h, :])
                if 2 <= s < 8:
                    hash_bits(s - 2)
                if 2 <= s < 8:
                    hash_flip(s - 2)
                if s == 2:
                    weights(1)


def kernel(x, ctx_768, L0_attn_W_delta, L0_attn_b_delta, L0_attn_W_value, L0_attn_b_value, L0_xattn_Wq, L0_xattn_bq, L0_xattn_Wk,
           L0_xattn_bk, L0_xattn_Wv, L0_xattn_bv, L0_ffn_Wg, L0_ffn_W_in, L0_ffn_W_out, L1_attn_q_weight, L1_attn_v_weight, L1_attn_out_w,
           L1_attn_out_b, L1_xattn_Wq, L1_xattn_bq, L1_xattn_Wk, L1_xattn_bk, L1_xattn_Wv, L1_xattn_bv, L1_ffn_expert_weights,
           L1_ffn_hyperplanes):
    import concourse.bacc as bacc
    from concourse.bass_utils import run_bass_kernel_spmd
    import ml_dtypes

    c = np.ascontiguousarray
    n = np.asarray
    arrays = {
        "xT": c(n(x).reshape(S, D).T), "ctxT": c(n(ctx_768).reshape(B * TK, CD).T),
        "Wd": c(n(L0_attn_W_delta).T), "Wv": c(n(L0_attn_W_value).T),
        "bdv": c(np.stack([n(L0_attn_b_delta), n(L0_attn_b_value)]).reshape(2, DC, P).transpose(2, 0, 1)),
        "Wq0": c(n(L0_xattn_Wq)), "bq0": c(n(L0_xattn_bq).reshape(DC, P).T), "Wk0": c(n(L0_xattn_Wk).T), "bk0": c(n(L0_xattn_bk)[None]),
        "Wvx0": c(n(L0_xattn_Wv).T), "bvx0": c(n(L0_xattn_bv)[None]),
        "Wq1": c(n(L1_xattn_Wq).T), "bq1": c(n(L1_xattn_bq).reshape(DC, P).T), "Wk1": c(n(L1_xattn_Wk)), "bk1": c(n(L1_xattn_bk)[None]),
        "Wvx1": c(n(L1_xattn_Wv)), "bvx1": c(n(L1_xattn_bv)[None]),
        "Wg": c(n(L0_ffn_Wg)), "W_in": c(n(L0_ffn_W_in)), "W_out": c(n(L0_ffn_W_out)),
        "qw": c(n(L1_attn_q_weight).reshape(D, D)), "qwT": c(n(L1_attn_q_weight).reshape(D, D).T),
        "vw": c(n(L1_attn_v_weight).reshape(D, D)), "woT": c(n(L1_attn_out_w).T),
        "obr": c(np.broadcast_to(n(L1_attn_out_b), (P, D))), "hyp": c(n(L1_ffn_hyperplanes)),
        "EW": c(n(L1_ffn_expert_weights).reshape(64 * P, 2 * D)),
        "cf": shape_constants(), "ones1": np.ones((1, B * TK), np.float32),
        "ltri": np.triu(np.ones((P, P), np.float32), 1).astype(ml_dtypes.bfloat16),
        "onesb": np.ones((P, P), ml_dtypes.bfloat16),
    }
    nc = bacc.Bacc("TRN2", target_bir_lowering=False, num_devices=1)
    A = {k: nc.dram_tensor(k, a.shape, mybir.dt.from_np(a.dtype), kind="ExternalInput").ap() for k, a in arrays.items()}
    out = nc.dram_tensor("out", (B, T, D), F32, kind="ExternalOutput").ap()
    Y = nc.dram_tensor("expert_rows", (2 * S, D), F32, kind="Internal").ap()
    X2 = nc.dram_tensor("x2_rows", (S, D), F32, kind="Internal").ap()
    program(nc, A, out, Y, X2)
    r = run_bass_kernel_spmd(nc, [arrays], core_ids=[0])
    return r.results[0]["out"]
```

```python
from contextlib import ExitStack

import numpy as np

import concourse.bass as bass
import concourse.mybir as mybir

F32 = mybir.dt.float32
BF16 = mybir.dt.bfloat16
F32R = mybir.dt.float32r
I32 = mybir.dt.int32
ALU = mybir.AluOpType
ACT = mybir.ActivationFunctionType
AX = mybir.AxisListType

P = 128
B = 8
T = 256
D = 256
DC = D // P
S = B * T
NT = S // P
TK = 77
CD = 192
CK = CD // 2
E0 = 8
F0 = 512
CAP = 640
ET = CAP // P
NST = E0 * ET
HALF = CAP // 2
NH = 16
HD = 16
NB6 = 6
EPS = 1e-5
BIG = 8192.0

_CF = {}
_n = 0
for _name, _w in (("ident", P), ("bmask", P), ("iota", P), ("w8", NT * E0), ("smask", 2 * NT * E0),
                  ("acon", 2 * NT), ("pcol", 1), ("sel0", P), ("ones", P), ("w6", 2 * NB6), ("p6", 2 * NB6),
                  ("negh", 2)):
    _CF[_name] = (_n, _n + _w)
    _n += _w
CFW = _n


def shape_constants():
    c = np.zeros((P, CFW), np.float32)

    def put(name, v):
        a, b = _CF[name]
        c[:, a:b] = v
    put("ident", np.eye(P))
    put("bmask", np.kron(np.eye(P // HD), np.ones((HD, HD))) * HD ** -0.5)
    put("iota", np.arange(P)[None, :])
    put("w8", np.tile(E0 - np.arange(E0), NT)[None, :])
    m = np.ones((E0, 2 * NT))
    m[:, 0] = 0
    put("smask", m.reshape(1, -1))
    put("acon", (P * np.arange(2 * NT))[None, :])
    put("pcol", np.arange(P)[:, None])
    s0 = np.zeros((P, P))
    s0[0] = 1
    put("sel0", s0)
    put("ones", 1.0)
    put("w6", np.tile(NB6 - np.arange(NB6), 2)[None, :])
    put("p6", np.tile(2.0 ** np.arange(NB6), 2)[None, :])
    put("negh", -0.5)
    return c


def program(nc, A, out, Y, X2):
    ctx = ExitStack()
    with ctx:
        def sb(name, shape, dt=F32):
            return ctx.enter_context(nc.sbuf_tensor("sb_" + name, shape, dt))

        cf = sb("cf", [P, CFW])
        C = {k: cf[:, a:b] for k, (a, b) in _CF.items()}
        ident = C["ident"]
        ltri = sb("ltri", [P, P], BF16)
        onesb = sb("onesb", [P, P], BF16)
        xt = sb("xt", [P, NT, D])
        wdv = sb("wdv", [P, 2 * DC * D])
        wd, wv = (wdv[:, i * DC * D:(i + 1) * DC * D].rearrange("p (c n) -> p c n", c=DC) for i in range(2))
        bdv = sb("bdv", [P, 2, DC])
        bq = [sb(f"bq{l}", [P, DC]) for l in range(2)]
        Ga = [sb(f"G{l}", [P, DC * B * TK]) for l in range(2)]
        G = [a[:].rearrange("p (c n) -> p c n", c=DC) for a in Ga]
        bqk = [sb(f"bqk{l}", [P, B * TK]) for l in range(2)]
        vxa = [sb(f"vx{l}", [P, B * D]) for l in range(2)]
        vx = [a[0:TK, :].rearrange("p (b n) -> p b n", b=B) for a in vxa]
        wg = sb("wg", [P, DC, E0])
        qw = sb("qw", [P, DC, D])
        quw = sb("quw", [P, DC, 2 * D])
        woT = sb("woT", [P, DC, D])
        obr = sb("obr", [P, D])
        hyp = sb("hyp", [P, DC, NB6])
        with nc.sbuf_tensor("sb_big", [P, 21504], F32) as big:
            pass
        part = {}
        for name, words in (("hidH", 2560), ("gap0", 4608), ("winH", 2048), ("wouH", 1024), ("winL", 2048), ("wouL", 1024), ("gap1", 2560),
                            ("inpH", 1280), ("inpL", 1280), ("hidL", 2560), ("gap2", 512)):
            part[name] = sb(name, [P, words], F32 if name.startswith("gap") else F32R)
        def view(a, c, n, parts=P):
            return big[0:parts, a:a + c * n].rearrange("p (c n) -> p c n", c=c)
        kf = view(10240, DC, B * TK)
        wk = [view(11520 + l * 512, 2, D, CK + 1) for l in range(2)]
        wvx = [view(12544 + l * 512, 2, D, CK + 1) for l in range(2)]
        wq = [view(13568 + l * 512, DC, D) for l in range(2)]
        bqb = [view(14592 + l * 256, DC, P) for l in range(2)]
        bd = view(15104, DC, P)
        qwT = view(15360, DC, D)
        vw = view(15872, DC, D)
        cx = view(16384, 2, B * TK, CK + 1)
        zero = big[:, 20480:21504]
        xf = big[:, 0:4096].rearrange("p (c t) -> p c t", c=DC)
        FC = F0 // P
        win = view(4096, DC, 2 * F0)
        wou = view(6144, FC, D)
        winH, winL, inpH, inpL = (part[k][:].rearrange("p (c n) -> p c n", c=DC) for k in ("winH", "winL", "inpH", "inpL"))
        wouH, wouL, hidH, hidL = (part[k][:].rearrange("p (c n) -> p c n", c=FC) for k in ("wouH", "wouL", "hidH", "hidL"))
        winH4, inpH4, wouH4, hidH4 = (x.bitcast(F32) for x in (winH, inpH, wouH, hidH))
        inpT = [view(13312 + i * 1280, ET, D) for i in range(2)]
        oe = [big[:, 2560 + i * 256:2560 + (i + 1) * 256] for i in range(4)]
        rA = big[:, 0:4096]
        qa = big[:, 0:2048].rearrange("p (t n) -> p t n", t=B)
        ua = big[:, 2048:4096].rearrange("p (t n) -> p t n", t=B)
        ua2 = big[:, 4096:6144].rearrange("p (t n) -> p t n", t=B)
        qa2 = big[:, 6144:8192].rearrange("p (t n) -> p t n", t=B)
        dif = [big[:, 8192 + i * 13 * D:8192 + (i + 1) * 13 * D] for i in range(2)]
        att = [big[:, 15360 + i * 1024:15360 + (i + 1) * 1024] for i in range(2)]
        prod = [big[:, 17408 + i * 2048:17408 + (i + 1) * 2048].rearrange("p (s n) -> p s n", s=B) for i in range(2)]
        ph = sb("ph", [P, 4 * DC * T])
        th, a1, dv1, hs = (ph[:, i * DC * T:(i + 1) * DC * T].rearrange("p (c n) -> p c n", c=DC) for i in range(4))
        ge = [ph[:, i * HALF:(i + 1) * HALF] for i in range(2)]
        hid = [ph[:, (2 + i) * HALF:(3 + i) * HALF] for i in range(2)]
        y1 = [sb(f"y1{i}", [P, DC, T]) for i in range(2)]
        xs = [sb(f"xs{i}", [P, 2, D]) for i in range(2)]
        xsf = [sb(f"xsf{i}", [P, DC, T]) for i in range(2)]
        x2f = [sb(f"x2f{i}", [P, DC, T]) for i in range(2)]
        vb = sb("vb", [P, DC, T])
        pr = [sb(f"pr{i}", [P, 2, TK]) for i in range(2)]
        pt = [sb(f"pt{i}", [TK, T]) for i in range(2)]
        y2 = [sb(f"y2{i}", [P, 2, D]) for i in range(2)]
        st = {k: sb(f"st{k}", [P, 2, 2, 6]) for k in range(6)}
        mv = {k: sb(f"mv{k}", [P, 2, 2, 2]) for k in range(6)}
        ve = {k: sb(f"ve{k}", [P, 2, 2]) for k in range(6)}
        rs = {k: sb(f"rs{k}", [P, 2, 2]) for k in range(6)}
        ng = {k: sb(f"ng{k}", [P, 2, 2]) for k in range(6)}
        nb = {k: sb(f"nb{k}", [P, 2, 2]) for k in range(6)}
        nm = sb("nm", [P, 2, 2])
        sm = sb("sm", [P, 2, 2])
        rc = sb("rc", [P, 2, 2])
        bk = [ctx.enter_context(nc.psum_tensor(f"bank{i}", [P, 512], F32)) for i in range(8)]

        sems = {}

        def q(name):
            if name not in sems:
                sems[name] = ctx.enter_context(nc.semaphore(name))
            return sems[name]

        def tiles_of(m):
            g, i = m // 4, m % 4
            return [2 * (2 * i) + g, 2 * (2 * i + 1) + g]

        yb = [ph[:, i * 4 * D:(i + 1) * 4 * D].rearrange("p (h k n) -> p h k n", h=2, k=2) for i in range(2)]
        y6 = [Ga[0][:, i * 2 * D:(i + 1) * 2 * D].rearrange("p (h n) -> p h n", h=2) for i in range(2)]
        x4f = [sb(f"x4f{i}", [P, DC, T]) for i in range(2)]
        aof = [bqk[0][:, i * 2 * P:(i + 1) * 2 * P].rearrange("p (c n) -> p c n", c=DC) for i in range(2)]
        x5s = [sb(f"x5s{i}", [P, 2, D]) for i in range(2)]
        x5f = [sb(f"x5f{i}", [P, DC, T]) for i in range(2)]
        ws = [wdv[:, i * 2 * D:(i + 1) * 2 * D] for i in range(2)]
        we = [vxa[0][:, i * 4 * D:(i + 1) * 4 * D].rearrange("p (k n) -> p k n", k=2) for i in range(2)]
        idx = sb("idx", [P, 2, NST], I32)
        gate = sb("gate", [P, 2, NT])
        widx = [sb(f"widx{i}", [P, 4], I32) for i in range(2)]
        emb = sb("emb", [P, DC, 2])
        eh = sb("eh", [P, DC, 2, NB6])
        rt = sb("rt", [P, 12, 2 * NB6])
        zz = sb("zz", [P, B, NH])
        rz = sb("rz", [P, B, NH])
        bh = sb("bh", [P, 2, DC])
        y6b, y3 = x2f, y1
        xbs = sb("xbs", [P, 2, D])
        dsq = sb("dsq", [P, 28, NH])

        rMb = sb("rMb", [P, 2 * NT * E0], BF16)[:]
        ohl = ph[:].bitcast(BF16).rearrange("p (n c) -> p n c", n=2 * NT)
        ohh = big[:, 18560:20480].bitcast(BF16).rearrange("p (n c) -> p n c", n=2 * NT)

        route = sb("route", [P, 12, 2 * NT])
        table = big[:, 3328:3568]

        block = ctx.enter_context(nc.Block())

        @block.sync
        def _(sp):
            xr = A["xT"].rearrange("(c p) t -> p c t", p=P)
            sp.dma_start(xf[:, :, 0:T], xr[:, :, 0:T]).then_inc(q("loaded_x0"), 16)
            sp.dma_start(wv, A["Wv"].rearrange("(c p) e -> p c e", p=P)).then_inc(q("loaded_value_weight"), 16)
            sp.dma_start(bdv[:], A["bdv"]).then_inc(q("loaded_value_weight"), 16)
            sp.dma_start(xf[:, :, T:2 * T], xr[:, :, T:2 * T]).then_inc(q("loaded_x1"), 16)
            sp.dma_start(xf[:, :, 2 * T:], xr[:, :, 2 * T:]).then_inc(q("loaded_x2"), 16)
            for l in range(2):
                sp.dma_start(wvx[l][0:CK, :, :], A[f"Wvx{l}"].rearrange("(c p) e -> p c e", p=CK)).then_inc(q("loaded_xattn_weights"), 16)
                sp.dma_start(wvx[l][CK:CK + 1, 1, :], A[f"bvx{l}"]).then_inc(q("loaded_xattn_weights"), 16)
                sp.dma_start(wq[l], A[f"Wq{l}"].rearrange("(c p) e -> p c e", p=P)).then_inc(q("loaded_xattn_weights"), 16)
                sp.dma_start(bq[l][:], A[f"bq{l}"]).then_inc(q("loaded_xattn_weights"), 16)
            sp.dma_start(wg[:], A["Wg"].rearrange("(c p) e -> p c e", p=P)).then_inc(q("loaded_xattn_weights"), 16)
            for n, w in (("qw", qw), ("qwT", qwT), ("vw", vw), ("woT", woT)):
                sp.dma_start(w[:, :, :], A[n].rearrange("(c p) e -> p c e", p=P)).then_inc(q("loaded_layer1_weights"), 16)
            sp.dma_start(obr[:], A["obr"]).then_inc(q("loaded_layer1_weights"), 16)
            sp.dma_start(hyp[:], A["hyp"].rearrange("(p j) k -> p j k", j=DC)).then_inc(q("loaded_layer1_weights"), 16)

            sp.wait_ge(q("zeros_ready"), 1)
            yz = Y.rearrange("(p r) n -> p (r n)", p=P)
            for i in range(8):
                sp.dma_start(yz[:, i * 1024:(i + 1) * 1024], zero).then_inc(q("expert_rows_zeroed"), 16)

            def load_expert(e):
                if e >= 1:
                    sp.wait_ge(q("w_in_low"), e)
                sp.dma_start(win, A["W_in"][e].rearrange("(c p) f -> p c f", p=P)).then_inc(q("loaded_w_in"), 16)
                if e >= 1:
                    sp.wait_ge(q("w_out_low"), e)
                sp.dma_start(wou, A["W_out"][e].rearrange("(c p) f -> p c f", p=P)).then_inc(q("loaded_w_out"), 16)
            load_expert(0)
            for b in range(B):
                sp.wait_ge(q("norm2_done"), b + 1)
                sp.dma_start(X2[b * T:(b + 1) * T, :].rearrange("(h p) n -> p h n", p=P), xt[:, 2 * b:2 * b + 2, :]
                                ).then_inc(q("x2_stored"), 16)
            for e in range(1, E0):
                load_expert(e)
            for m in range(8):
                if m == 0:
                    for r in range(4):
                        sp.wait_ge(q(f"scattered{r}"), 16 * NST // 4)
                    sp.wait_ge(q("expert_rows_zeroed"), 128)
                if m >= 2:
                    sp.wait_ge(q("y3_ready"), m - 1)
                for h, n in enumerate(tiles_of(m)):
                    src = Y.rearrange("(k n p) d -> n p k d", k=2, p=P)[n]
                    sp.dma_start(yb[m % 2][:, h, :, :], src).then_inc(q(f"loaded_returned{m % 2}"), 16)
            for m in range(8):
                sp.wait_ge(q("norm6_done"), m + 1)
                for h, n in enumerate(tiles_of(m)):
                    sp.dma_start(out[n // 2, (n % 2) * P:(n % 2 + 1) * P, :], y6[m % 2][:, h, :]).then_inc(q(f"stored_out{m % 2}"), 16)
            for r in range(2):
                sp.wait_ge(q(f"stored_out{r}"), 128)

        @block.gpsimd
        def _(pool):
            pool.memset(zero, 0.0).then_inc(q("zeros_ready"), 1)

            def power(k, m):
                p = m % 2
                pool.wait_ge(q(f"moments{k}_ready"), m + 1)
                if m >= 2:
                    pool.wait_ge(q(f"norm{k + 1}_done"), m - 1)
                pool.tensor_scalar(ve[k][:, p, :], mv[k][:, p, :, 1], EPS, None, ALU.add).then_inc(q("variance_eps_ready"), 1)
                pool.tensor_scalar(ng[k][:, p, :], mv[k][:, p, :, 0], -1.0, None, ALU.mult)
                pool.wait_ge(q("variance_eps_ready"), powers[0] + 1)
                pool.tensor_tensor(rs[k][:, p, :], ve[k][:, p, :], C["negh"], ALU.pow).then_inc(q("power_ready"), 1)
                powers[0] += 1
                pool.wait_ge(q("power_ready"), powers[0])
                pool.tensor_tensor(nb[k][:, p, :], ng[k][:, p, :], rs[k][:, p, :], ALU.mult).then_inc(q(f"shift{k}_ready"), 1)
            powers = [0]
            pool.wait_ge(q("loaded_constants"), 48)
            for s in range(B + 2):
                if 1 <= s <= B:
                    power(0, s - 1)
                if s < B:
                    pool.wait_ge(q("tanh_ready"), s + 1)
                    if s >= 1:
                        pool.wait_ge(q("state_ready"), s)
                    pool.tensor_scalar(a1, th, -0.5, 0.5, ALU.mult, ALU.add).then_inc(q("decay_ready"), 1)
                if s >= 2:
                    power(1, s - 2)
            pool.wait_ge(q("blocks_copied"), 1)
            for c in range(DC):
                i = pool.tensor_tensor(bd[:, c, :], bd[:, c, :], C["bmask"], ALU.mult)
            i.then_inc(q("blocks_masked"), 1)

            def gather(e):
                if e == 0:
                    pool.wait_ge(q("slot_index_ready"), 1)
                    pool.wait_ge(q("u_weight_summed"), 1)
                    pool.wait_ge(q("x2_stored"), 16 * B)
                if e >= 2:
                    pool.wait_ge(q("slots_turned"), ET * (e - 1))
                for j in range(ET):
                    pool.indirect_dma_start(out=inpT[e % 2][:, j, :], out_offset=None, in_=X2[:, :],
                                            in_offset=bass.IndirectOffsetOnAxis(ap=idx[:, 0, e * ET + j:e * ET + j + 1], axis=0)
                                            ).then_inc(q(f"gathered_slots{e % 2}{j}"), 16)

            def scatter(e):
                for j in range(ET):
                    n = e * ET + j
                    if n == 0:
                        pool.wait_ge(q("expert_rows_zeroed"), 128)
                    pool.wait_ge(q("returned_copied"), n + 1)
                    pool.indirect_dma_start(out=Y[:, :], out_offset=bass.IndirectOffsetOnAxis(ap=idx[:, 1, n:n + 1], axis=0),
                                            in_=oe[n % 4], in_offset=None, bounds_check=2 * S - 1, oob_is_err=False
                                            ).then_inc(q(f"scattered{n % 4}"), 16)
            gather(0)
            for e in range(E0):
                if e + 1 < E0:
                    gather(e + 1)
                scatter(e)

            def chunk_weights(m):
                for h in range(2):
                    n = 2 * m + h
                    pool.wait_ge(q("chunk_index_ready"), m + 1)
                    if n >= 2:
                        pool.wait_ge(q("chunk_weights_ready"), n - 1)
                    for k in range(2):
                        pool.indirect_dma_start(out=we[n % 2][:, k, :], out_offset=None, in_=A["EW"],
                                                in_offset=bass.IndirectOffsetOnAxis(ap=widx[m % 2][:, 2 * h + k:2 * h + k + 1], axis=0)
                                                ).then_inc(q(f"gathered_chunk_weights{n % 2}"), 16)

            def subtract(m):
                g, i = m // 4, m % 4
                t = 2 * i
                if t == 0:
                    return
                pool.wait_ge(q("qu_copied"), 2 * m + 1)
                if m >= 2:
                    pool.wait_ge(q("distances_ready"), m - 1)
                Q = (qa, qa2)[g]
                pool.tensor_tensor(dif[m % 2][:, 0:t * D].rearrange("p (s n) -> p s n", s=t), Q[:, t:t + 1, :].to_broadcast([P, t, D]), Q[:, 0:t, :],
                                   ALU.subtract).then_inc(q("even_differences_ready"), 1)

            def add_bias(s):
                if s >= 1:
                    pool.wait_ge(q("projection_summed"), 2 * s)
                pool.wait_ge(q("norm3_done"), s + 1)
                for h, n in enumerate(tiles_of(s)):
                    i = pool.tensor_tensor(xbs[:, h, :], xt[:, n, :], obr[:], ALU.add)
                i.then_inc(q("biased_residual_ready"), 1)

            def sum_weights(b):
                for h in range(2):
                    n = 2 * b + h
                    pool.wait_ge(q(f"gathered_chunk_weights{n % 2}"), 32 * (b + 1))
                    if n >= 2:
                        pool.wait_ge(q("ffn_summed"), n - 1)
                    pool.tensor_tensor(ws[n % 2], we[n % 2][:, 0, :], we[n % 2][:, 1, :], ALU.add).then_inc(q("chunk_weights_ready"), 1)

            for f in range(8):
                power(2, f)
                if 1 <= f:
                    subtract(f - 1)
            for s in range(8 + 3):
                if s < 8:
                    add_bias(s)
                if 3 <= s:
                    sum_weights(s - 3)
                if 8 <= s <= 9:
                    chunk_weights(s - 2)
                if 1 <= s <= 8:
                    power(4, s - 1)
                if 3 <= s:
                    power(5, s - 3)
                if s < 8:
                    power(3, s)
                if 2 <= s < 8:
                    chunk_weights(s - 2)
                if s == 0:
                    subtract(7)

        @block.scalar
        def _(act):
            act.dma_start(wd, A["Wd"].rearrange("(c p) e -> p c e", p=P)).then_inc(q("loaded_delta_weight"), 16)
            act.dma_start(cf[:], A["cf"]).then_inc(q("loaded_constants"), 16)
            act.dma_start(ltri[:], A["ltri"]).then_inc(q("loaded_constants"), 16)
            act.dma_start(onesb[:], A["onesb"]).then_inc(q("loaded_constants"), 16)
            act.dma_start(cx[0:CK, :, :], A["ctxT"].rearrange("(c p) t -> p c t", p=CK)).then_inc(q("loaded_context"), 16)
            act.dma_start(cx[CK:CK + 1, 1, :], A["ones1"]).then_inc(q("loaded_context"), 16)
            for l in range(2):
                act.dma_start(wk[l][0:CK, :, :], A[f"Wk{l}"].rearrange("(c p) e -> p c e", p=CK)).then_inc(q("loaded_context"), 16)
                act.dma_start(wk[l][CK:CK + 1, 1, :], A[f"bk{l}"]).then_inc(q("loaded_context"), 16)

            def keys(l, k0, g0):
                for c in range(DC):
                    for h in range(2):
                        n = l * 4 + c * 2 + h
                        act.wait_ge(q("keys_summed"), n + 1)
                        if l == 1 and c == 0 and h == 0:
                            act.wait_ge(q("bias_row_summed"), 2)
                        act.activation(kf[:, c, h * 308:(h + 1) * 308], bk[k0 + n % 2][:, 0:308], ACT.Copy).then_inc(q("keys_copied"), 1)
                for c in range(DC):
                    for h in range(2):
                        n = l * 4 + c * 2 + h
                        act.wait_ge(q("folded_summed"), n + 1)
                        act.activation(G[l][:, c, h * 308:(h + 1) * 308], bk[g0 + n % 2][:, 0:308], ACT.Copy, scale=1.0 / 16
                                        ).then_inc(q("folded_copied"), 1)
                for h in range(2):
                    n = l * 2 + h
                    act.wait_ge(q("bias_row_summed"), n + 1)
                    act.activation(bqk[l][:, h * 308:(h + 1) * 308], bk[k0 + n % 2][:, 0:308], ACT.Copy, scale=1.0 / 16
                                    ).then_inc(q("bias_row_copied"), 1)
                for b in range(B):
                    n = l * B + b
                    act.wait_ge(q("context_values_summed"), n + 1)
                    act.activation(vx[l][:, b, :], bk[g0 + n % 2][0:TK, 0:D], ACT.Copy).then_inc(q("context_values_copied"), 1)

            def norm(k, m, src, dst, done, waits=()):
                act.wait_ge(q(f"shift{k}_ready"), m + 1)
                for w, n in waits:
                    if n > 0:
                        act.wait_ge(q(w), n)
                for h in range(2):
                    i = act.activation(dst(h), src(h), ACT.Identity, bias=nb[k][:, m % 2, h:h + 1], scale=rs[k][:, m % 2, h:h + 1])
                i.then_inc(q(done), 1)

            def evac(dst, src, ready, n, done, waits=()):
                act.wait_ge(q(ready), n)
                for w, v in waits:
                    if v > 0:
                        act.wait_ge(q(w), v)
                act.activation(dst, src, ACT.Copy).then_inc(q(done), 1)

            def softmax_exp(b, ready, done, free):
                act.wait_ge(q(ready), b + 1)
                if b >= 2:
                    act.wait_ge(q(free), b - 1)
                for h in range(2):
                    i = act.activation(pr[b % 2][:, h, :], bk[5][:, h * TK:(h + 1) * TK], ACT.Exp, bias=nm[:, b % 2, h:h + 1],
                                       accum_out=sm[:, b % 2, h:h + 1])
                i.then_inc(q(done), 1)

            for s in range(B + 3):
                if s >= 3:
                    b = s - 3
                    norm(1, b, lambda h: y2[b % 2][:, h, :], lambda h: xt[:, 2 * b + h, :], "norm2_done")
                if 1 <= s <= B:
                    b = s - 1
                    norm(0, b, lambda h: bk[2][:, h * D:(h + 1) * D], lambda h: xs[b % 2][:, h, :], "norm1_done", [("y2_ready", b - 1), ("x1_turned", b - 1)])
                if s < B:
                    act.wait_ge(q("delta_summed"), s + 1)
                    if s == 0:
                        act.wait_ge(q("half_biases_ready"), 1)
                    if s >= 1:
                        act.wait_ge(q("delta_value_ready"), s)
                        act.wait_ge(q("decay_ready"), s)
                    for c in range(DC):
                        i = act.activation(th[:, c, :], bk[0][:, c * T:(c + 1) * T], ACT.Tanh, bias=bh[:, 0, c:c + 1], scale=0.5)
                    i.then_inc(q("tanh_ready"), 1)
                    act.wait_ge(q("value_summed"), s + 1)
                    for c in range(DC):
                        i = act.activation(vb[:, c, :], bk[1][:, c * T:(c + 1) * T], ACT.Identity, bias=bh[:, 1, c:c + 1], scale=0.5)
                    i.then_inc(q("half_value_ready"), 1)
                if s == 1:
                    keys(0, 4, 6)
                if 1 <= s <= B:
                    b = s - 1
                    evac(xsf[b % 2][:].rearrange("p c t -> p (c t)"), bk[3][:], "x1_turned", b + 1, "x1_copied", [("scores0_summed", b - 1)])
                if 2 <= s <= B + 1:
                    b = s - 2
                    evac(pt[b % 2][:], bk[6][0:TK, 0:T], "probs0_turned", b + 1, "probs0_copied", [("attended0_summed", b - 1)])
                if s >= 3:
                    b = s - 3
                    evac(x2f[b % 2][:].rearrange("p c t -> p (c t)"), bk[4][:], "x2_turned", b + 1, "x2_copied", [("logits_summed", b - 1)])
                if 1 <= s <= B:
                    softmax_exp(s - 1, "max0_ready", "probs0_ready", "probs0_turned")
            act.wait_ge(q("blocks_summed"), 1)
            act.activation(bd[:, :, :], bk[2][:, 0:2 * P].rearrange("p (c n) -> p c n", c=DC), ACT.Copy).then_inc(q("blocks_copied"), 1)
            act.wait_ge(q("logits_shifted"), 1)
            act.activation(rA[:, 128:256], rA[:, 0:128], ACT.Exp).then_inc(q("logits_exp_ready"), 1)
            keys(1, 3, 5)
            act.wait_ge(q("u_weight_summed"), 1)
            act.activation(quw[:, :, D:2 * D], bk[2][:].rearrange("p (c n) -> p c n", c=DC), ACT.Copy).then_inc(q("u_weight_copied"), 1)
            act.activation(quw[:, :, 0:D], qw[:], ACT.Copy).then_inc(q("u_weight_copied"), 1)

            def inp_high(e, j):
                n = e * ET + j
                act.wait_ge(q("slots_turned"), n + 1)
                if e >= 1 and j == 0:
                    act.wait_ge(q("hidden_summed"), 8 * e)
                act.activation(inpH[:, :, j * P:(j + 1) * P], bk[6 + n % 2][:, 0:D].rearrange("p (c t) -> p c t", c=DC),
                               ACT.Copy).then_inc(q("inputs_high"), 1)

            def win_high(e, c):
                act.wait_ge(q("loaded_w_in"), 16 * (e + 1))
                act.activation(winH[:, c, :], win[:, c, :], ACT.Copy).then_inc(q("w_in_high"), 1)

            def hid_high(n):
                u = n % 8
                f, hf = u % FC, u // FC
                act.wait_ge(q("hidden_ready"), n + 1)
                act.activation(hidH[:, f, hf * HALF:(hf + 1) * HALF], hid[n % 2], ACT.Copy).then_inc(q("hidden_high"), 1)

            for c in range(DC):
                win_high(0, c)
            for j in range(3):
                inp_high(0, j)
            for e in range(E0):
                for u in range(8):
                    n = 8 * e + u
                    if n == FC:
                        inp_high(0, 3)
                        inp_high(0, 4)
                    act.wait_ge(q("hidden_summed"), n + 1)
                    if n >= 2:
                        act.wait_ge(q("hidden_ready"), n - 1)
                    act.activation(ge[n % 2], bk[n % 2][:, 0:HALF], ACT.Gelu).then_inc(q("gelu_ready"), 1)
                    if u == 0:
                        if e >= 1:
                            act.wait_ge(q("returned_summed"), ET * e)
                        act.wait_ge(q("loaded_w_out"), 16 * (e + 1))
                        act.activation(wouH, wou, ACT.Copy).then_inc(q("w_out_high"), 1)
                    else:
                        hid_high(n - 1)
                hid_high(8 * e + 7)
                if e + 1 < E0:
                    for j in range(ET):
                        inp_high(e + 1, j)
                        if j in (2, 3):
                            win_high(e + 1, j - 2)

            def front(m):
                evac(xsf[m % 2][:].rearrange("p c t -> p (c t)"), bk[4][:], "x3_turned", m + 1, "x3_copied", [("qu_summed", 2 * m - 2)])

            def front_out(m):
                g = m // 4
                for h in range(2):
                    n = 2 * m + h
                    act.wait_ge(q("qu_summed"), n + 1)
                    t = 2 * (m % 4) + h
                    act.activation((qa, qa2)[g][:, t, :], bk[h][:, 0:D], ACT.Copy)
                    act.activation((ua, ua2)[g][:, t, :], bk[h][:, D:2 * D], ACT.Copy).then_inc(q("qu_copied"), 1)

            def squares(m):
                g, i = m // 4, m % 4
                for h in range(2):
                    t = 2 * i + h
                    if t == 0:
                        continue
                    if h == 0:
                        act.wait_ge(q("even_differences_ready"), 3 * g + i)
                    else:
                        act.wait_ge(q("odd_differences_ready"), m + 1)
                    o = (0, 6 * D)[h]
                    act.activation(dif[m % 2][:, o:o + t * D], dif[m % 2][:, o:o + t * D], ACT.Square).then_inc(q("squares_ready"), 1)

            def kernels(m):
                g, i = m // 4, m % 4
                at3 = att[g].rearrange("p (t s h) -> p t s h", t=B, s=B)
                act.wait_ge(q("distances_ready"), m + 1)
                for h in range(2):
                    t = 2 * i + h
                    if t:
                        a = t * (t - 1) // 2
                        act.activation(at3[:, t, 0:t, :], dsq[:, a:a + t, :], ACT.Exp, scale=-HD ** -0.5).then_inc(q("kernels_ready"), 1)

            def norm3(m):
                norm(2, m, lambda h: y3[m % 2][:, h, :], lambda h: xt[:, tiles_of(m)[h], :], "norm3_done")
            norm3(0)
            for f in range(8):
                front(f)
                if f < 7:
                    norm3(f + 1)
                front_out(f)
                if 1 <= f:
                    squares(f - 1)
                if 2 <= f:
                    kernels(f - 2)

            def attended_fm(s, h):
                evac(aof[h].rearrange("p c t -> p (c t)"), bk[2 + h][:, 0:256], "attention_summed", 2 * s + h + 1, "attention_copied", [("projection_summed", 2 * s + h - 1)])
            attended_fm(0, 0)
            for s in range(8 + 3):
                b = s - 1
                if 0 <= b < 8:
                    evac(x4f[b % 2][:].rearrange("p c t -> p (c t)"), bk[4][:], "x4_turned", b + 1, "x4_copied", [("scores1_summed", b - 1)])
                if 0 <= b < 8:
                    softmax_exp(b, "max1_ready", "probs1_ready", "probs1_turned")
                if 0 <= b < 8:
                    evac(pt[b % 2][:], bk[6][0:TK, 0:T], "probs1_turned", b + 1, "probs1_copied", [("attended1_summed", b - 1)])
                if s < 8:
                    attended_fm(s, 1)
                if 0 <= b < 8:
                    norm(4, b, lambda h: y2[b % 2][:, h, :], lambda h: x5s[b % 2][:, h, :], "norm5_done", [("y6_ready", b - 1), ("x5_turned", b - 1)])
                if 0 <= b < 8:
                    act.wait_ge(q("x5_turned"), b + 1)
                    if b >= 1:
                        act.wait_ge(q("hyperplane_products_ready"), b)
                    if b >= 2:
                        act.wait_ge(q("ffn_summed"), 2 * b - 2)
                    for c in range(DC):
                        for h in range(2):
                            i = act.activation(x5f[b % 2][:, c, h * P:(h + 1) * P], bk[4][:, c * T + h * P:c * T + (h + 1) * P], ACT.Copy,
                                               accum_out=emb[:, c, h:h + 1])
                    i.then_inc(q("x5_copied"), 1)
                if s < 8:
                    norm(3, s, lambda h: bk[0][:, h * D:(h + 1) * D], lambda h: xs[s % 2][:, h, :], "norm4_done", [("y5_ready", s - 1), ("x4_turned", s - 1)])
                if s >= 3:
                    d = s - 3
                    norm(5, d, lambda h: y6b[d % 2][:, h, :], lambda h: y6[d % 2][:, h, :], "norm6_done", [(f"stored_out{d % 2}", 32 * (d // 2))])
                if s < 2:
                    kernels(s + 6)
                if s == 0:
                    squares(7)
                if s < 7:
                    attended_fm(s + 1, 0)

        @block.tensor
        def _(pe):
            def tr4(dst, src, ready, n, done, waits=(), strided=False):
                pe.wait_ge(q(ready), n)
                for w, v in waits:
                    if v > 0:
                        pe.wait_ge(q(w), v)
                for a in range(2):
                    for c in range(2):
                        blk = src[:, a, c::2] if strided else src[:, a, c * P:(c + 1) * P]
                        i = pe.transpose(dst[:, c * 256 + a * P:c * 256 + (a + 1) * P], blk, ident)
                i.then_inc(q(done), 1)

            def keys(l, k0, g0, part):
                if part == 0:
                    if l == 0:
                        pe.wait_ge(q("loaded_context"), 96)
                        pe.wait_ge(q("loaded_xattn_weights"), 144)
                    for c in range(DC):
                        for h in range(2):
                            n = l * 4 + c * 2 + h
                            if n >= 2:
                                pe.wait_ge(q("keys_copied"), n - 1)
                            for k in range(2):
                                r = CK + k
                                i = pe.matmul(bk[k0 + n % 2][:, 0:308], wk[l][0:r, k, c * P:(c + 1) * P], cx[0:r, k, h * 308:(h + 1) * 308],
                                              start=k == 0, stop=k == 1)
                            i.then_inc(q("keys_summed"), 1)
                    return
                pe.wait_ge(q("keys_copied"), 4 * l + 4)
                for c in range(DC):
                    for h in range(2):
                        n = l * 4 + c * 2 + h
                        if n >= 2:
                            pe.wait_ge(q("folded_copied"), n - 1)
                        for k in range(DC):
                            i = pe.matmul(bk[g0 + n % 2][:, 0:308], wq[l][:, k, c * P:(c + 1) * P], kf[:, k, h * 308:(h + 1) * 308],
                                          start=k == 0, stop=k == DC - 1)
                        i.then_inc(q("folded_summed"), 1)
                pe.wait_ge(q("bias_spread"), l + 1)
                for h in range(2):
                    n = l * 2 + h
                    if n >= 2:
                        pe.wait_ge(q("bias_row_copied"), n - 1)
                    for k in range(DC):
                        i = pe.matmul(bk[k0 + n % 2][:, 0:308], bqb[l][:, k, :], kf[:, k, h * 308:(h + 1) * 308], start=k == 0, stop=k == DC - 1)
                    i.then_inc(q("bias_row_summed"), 1)
                pe.wait_ge(q("folded_copied"), 4 * l + 4)
                for b in range(B):
                    n = l * B + b
                    if n >= 2:
                        pe.wait_ge(q("context_values_copied"), n - 1)
                    for k in range(2):
                        r = CK + k
                        i = pe.matmul(bk[g0 + n % 2][0:TK, 0:D], cx[0:r, k, b * TK:(b + 1) * TK], wvx[l][0:r, k, :], start=k == 0, stop=k == 1)
                    i.then_inc(q("context_values_summed"), 1)

            def scores(l, b, xfm, ready, free, done, seqs):
                pe.wait_ge(q(ready), b + 1)
                if b >= 1:
                    pe.wait_ge(q(free), b)
                for h in range(2):
                    cs = slice(seqs[h] * TK, (seqs[h] + 1) * TK)
                    for k in range(DC):
                        pe.matmul(bk[5][:, h * TK:(h + 1) * TK], xfm[:, k, h * P:(h + 1) * P], G[l][:, k, cs], start=k == 0, stop=False)
                    i = pe.matmul(bk[5][:, h * TK:(h + 1) * TK], C["sel0"], bqk[l][:, cs], start=False, stop=True)
                i.then_inc(q(done), 1)

            def probs_tr(b, ready, free, done):
                pe.wait_ge(q(ready), b + 1)
                if b >= 1:
                    pe.wait_ge(q(free), b)
                for h in range(2):
                    i = pe.transpose(bk[6][0:TK, h * P:(h + 1) * P], pr[b % 2][:, h, :], ident)
                i.then_inc(q(done), 1)

            def values(l, b, ready, free, done, seqs):
                pe.wait_ge(q(ready), b + 1)
                if b >= 1:
                    pe.wait_ge(q(free), b)
                for h in range(2):
                    i = pe.matmul(bk[7][:, h * D:(h + 1) * D], pt[b % 2][:, h * P:(h + 1) * P], vx[l][:, seqs[h], :], start=True, stop=True)
                i.then_inc(q(done), 1)

            for s in range(B + 3):
                if 1 <= s <= B:
                    b = s - 1
                    pe.wait_ge(q("y1_ready"), b + 1)
                    if b == 0:
                        pe.wait_ge(q("loaded_constants"), 48)
                    if b >= 1:
                        pe.wait_ge(q("norm1_done"), b)
                    for h in range(2):
                        for c in range(DC):
                            i = pe.transpose(bk[2][:, h * D + c * P:h * D + (c + 1) * P], y1[b % 2][:, c, h * P:(h + 1) * P], ident)
                    i.then_inc(q("y1_turned"), 1)
                if s < B:
                    if s < 3:
                        pe.wait_ge(q(f"loaded_x{s}"), 16)
                    if s == 0:
                        pe.wait_ge(q("loaded_delta_weight"), 16)
                    for w, bank, done, free in ((wd, 0, "delta_summed", "tanh_ready"), (wv, 1, "value_summed", "half_value_ready")):
                        if s >= 1:
                            pe.wait_ge(q(free), s)
                        if s == 0 and bank == 1:
                            pe.wait_ge(q("loaded_value_weight"), 32)
                        for c in range(DC):
                            for k in range(DC):
                                i = pe.matmul(bk[bank][:, c * T:(c + 1) * T], w[:, k, c * P:(c + 1) * P], xf[:, k, s * T:(s + 1) * T],
                                              start=k == 0, stop=k == DC - 1)
                        i.then_inc(q(done), 1)
                if s == 1:
                    keys(0, 4, 6, 0)
                    keys(0, 4, 6, 1)
                    pe.wait_ge(q("bias_row_copied"), 2)
                    pe.wait_ge(q("context_values_copied"), B)
                if 1 <= s <= B:
                    b = s - 1
                    tr4(bk[3], xs[b % 2], "norm1_done", b + 1, "x1_turned", [("x1_copied", b)])
                if 2 <= s <= B + 1:
                    probs_tr(s - 2, "probs0_ready", "probs0_copied", "probs0_turned")
                if s >= 3:
                    b = s - 3
                    tr4(bk[4], xt[:, 2 * b:2 * b + 2, :], "norm2_done", b + 1, "x2_turned", [("x2_copied", b)])
                if 2 <= s <= B + 1:
                    values(0, s - 2, "probs0_copied", "y2_ready", "attended0_summed", (s - 2, s - 2))
                if 1 <= s <= B:
                    b = s - 1
                    scores(0, b, xsf[b % 2], "x1_copied", "probs0_ready", "scores0_summed", (b, b))
                if s >= 3:
                    b = s - 3
                    pe.wait_ge(q("x2_copied"), b + 1)
                    pe.wait_ge(q("probs0_copied"), min(b + 2, B))
                    for h in range(2):
                        n = 2 * b + h
                        for k in range(DC):
                            i = pe.matmul(bk[6][:, 256 + n * E0:256 + (n + 1) * E0], x2f[b % 2][:, k, h * P:(h + 1) * P], wg[:, k, :],
                                          start=k == 0, stop=k == DC - 1)
                    i.then_inc(q("logits_summed"), 1)

            pe.wait_ge(q("loaded_layer1_weights"), 96)
            pe.wait_ge(q("norm1_done"), B)
            for c in range(DC):
                for k in range(DC):
                    i = pe.matmul(bk[2][:, c * P:(c + 1) * P], qw[:, k, c * P:(c + 1) * P], vw[:, k, c * P:(c + 1) * P], start=k == 0, stop=k == DC - 1)
            i.then_inc(q("blocks_summed"), 1)
            pe.wait_ge(q("x2_copied"), B)
            keys(1, 3, 5, 0)
            pe.wait_ge(q("choices_ready"), 1)
            pe.matmul(bk[0][:, 0:256], ltri[:], rMb, start=True, stop=True)
            pe.matmul(bk[0][:, 256:512], onesb[:], rMb, start=True, stop=True).then_inc(q("ranks_summed"), 1)
            keys(1, 3, 5, 1)
            pe.wait_ge(q("blocks_masked"), 1)
            for c in range(DC):
                for h in range(DC):
                    i = pe.matmul(bk[2][:, c * D + h * P:c * D + (h + 1) * P], qwT[:, h, c * P:(c + 1) * P], bd[:, h, :], start=True, stop=True)
            i.then_inc(q("u_weight_summed"), 1)
            for n in range(2 * NT):
                if n % (NT // 2) == 0:
                    pe.wait_ge(q("onehots_ready"), n // (NT // 2) + 1)
                i = pe.matmul(bk[1][:, 0:3 * NST], ohl[:, n, :], ohh[:, n, :], start=n == 0, stop=n == 2 * NT - 1)
            i.then_inc(q("slot_table_summed"), 1)
            pe.wait_ge(q("u_weight_copied"), 2)
            pe.wait_ge(q("context_values_copied"), 2 * B)

            def inp_tr(e, j):
                n = e * ET + j
                pe.wait_ge(q(f"gathered_slots{e % 2}{j}"), 16 * (e // 2 + 1))
                if n >= 2:
                    pe.wait_ge(q("inputs_low"), n - 1)
                for c in range(DC):
                    i = pe.transpose(bk[6 + n % 2][:, c * P:(c + 1) * P], inpT[e % 2][:, j, c * P:(c + 1) * P], ident)
                i.then_inc(q("slots_turned"), 1)

            def product(dst, lhs, rhs):
                (lh, ll), (rh, rl) = lhs, rhs
                last = len(lh) - 1
                for k in range(last + 1):
                    pe.matmul(dst, lh[k], rh[k], start=k == 0, stop=False)
                    pe.matmul(dst, lh[k], rl[k], start=False, stop=False)
                    i = pe.matmul(dst, ll[k], rh[k], start=False, stop=k == last)
                return i

            for j in range(3):
                inp_tr(0, j)
            for e in range(E0):
                pe.wait_ge(q("w_in_low"), e + 1)
                for u in range(8):
                    n = 8 * e + u
                    f, hf = u % FC, u // FC
                    if u == 0:
                        pe.wait_ge(q("inputs_low"), ET * e + 3)
                    if u == FC:
                        if e == 0:
                            inp_tr(0, 3)
                            inp_tr(0, 4)
                        pe.wait_ge(q("inputs_low"), ET * (e + 1))
                    if n >= 2:
                        pe.wait_ge(q("gelu_ready"), n - 1)
                        pe.wait_ge(q("hidden_ready"), n - 1)
                    for part in range(2):
                        a = part * F0 + f * P
                        i = product(bk[n % 2 + 2 * part][:, 0:HALF],
                                    [[w[:, k, a:a + P] for k in range(DC)] for w in (winH, winL)],
                                    [[x[:, k, hf * HALF:(hf + 1) * HALF] for k in range(DC)] for x in (inpH, inpL)])
                    i.then_inc(q("hidden_summed"), 1)
                if e + 1 < E0:
                    inp_tr(e + 1, 0)
                    inp_tr(e + 1, 1)
                pe.wait_ge(q("w_out_low"), e + 1)
                for j in range(ET):
                    n = e * ET + j
                    if j == 0:
                        pe.wait_ge(q("hidden_low"), 8 * e + FC)
                    if j == 2:
                        pe.wait_ge(q("hidden_low"), 8 * (e + 1))
                    if n >= 2:
                        pe.wait_ge(q("returned_copied"), n - 1)
                    i = product(bk[4 + n % 2][:, 0:D],
                                [[x[:, k, j * P:(j + 1) * P] for k in range(FC)] for x in (hidH, hidL)],
                                [[w[:, k, :] for k in range(FC)] for w in (wouH, wouL)])
                    i.then_inc(q("returned_summed"), 1)
                    if e + 1 < E0 and j < 3:
                        inp_tr(e + 1, j + 2)

            def front(m):
                a, b_ = tiles_of(m)
                tr4(bk[4], xt[:, a:b_ + 1:2, :], "norm3_done", m + 1, "x3_turned", [("x3_copied", m)])
                pe.wait_ge(q("x3_copied"), m + 1)
                for h in range(2):
                    n = 2 * m + h
                    if n >= 2:
                        pe.wait_ge(q("qu_copied"), n - 1)
                    for k in range(DC):
                        i = pe.matmul(bk[h][:], xsf[m % 2][:, k, h * P:(h + 1) * P], quw[:, k, :], start=k == 0, stop=k == DC - 1)
                    i.then_inc(q("qu_summed"), 1)

            def attend(s, h):
                n = 2 * s + h
                pe.wait_ge(q("products_ready"), n + 1)
                if n >= 2:
                    pe.wait_ge(q("attention_copied"), n - 1)
                parts = (B, B // 2)[h]
                for c in range(DC):
                    for u in range(parts):
                        i = pe.matmul(bk[2 + h][:, c * P:(c + 1) * P], prod[h][:, u, c * P:(c + 1) * P], ident, start=u == 0, stop=u == parts - 1)
                i.then_inc(q("attention_summed"), 1)

            pe.wait_ge(q("returned_copied"), NST)
            for m in range(8):
                front(m)
            pe.wait_ge(q("qu_copied"), 16)
            attend(0, 0)
            for s in range(8 + 3):
                b = s - 1
                seqs = (2 * (b % 4), 2 * (b % 4) + 1)
                if 0 <= b < 8:
                    tr4(bk[4], xs[b % 2], "norm4_done", b + 1, "x4_turned", [("x5_copied", b), ("x3_copied", 8)])
                    scores(1, b, x4f[b % 2], "x4_copied", "probs1_ready", "scores1_summed", seqs)
                if 2 <= s <= 9:
                    d = s - 2
                    pe.wait_ge(q("hyperplane_products_ready"), d + 1)
                    pe.wait_ge(q("probs1_copied"), min(d + 1, 8))
                    for k in range(DC):
                        i = pe.matmul(bk[6][:, 256:256 + 2 * NB6], C["ones"], eh[:, k, :, :].rearrange("p a b -> p (a b)"), start=k == 0, stop=k == DC - 1)
                    i.then_inc(q("hash_summed"), 1)
                if s < 8:
                    attend(s, 1)
                if 0 <= b < 8:
                    if b >= 1:
                        pe.wait_ge(q("hash_copied"), b)
                    probs_tr(b, "probs1_ready", "probs1_copied", "probs1_turned")
                    values(1, b, "probs1_copied", "y5_ready", "attended1_summed", seqs)
                if s >= 3:
                    d = s - 3
                    for h in range(2):
                        n = 2 * d + h
                        pe.wait_ge(q("chunk_weights_ready"), n + 1)
                        if d >= 1:
                            pe.wait_ge(q("y6_ready"), d)
                        for k in range(DC):
                            i = pe.matmul(bk[1][:, h * D:(h + 1) * D], x5f[d % 2][:, k, h * P:(h + 1) * P], ws[n % 2][:, k * D:(k + 1) * D],
                                          start=k == 0, stop=k == DC - 1)
                        i.then_inc(q("ffn_summed"), 1)
                if s < 8:
                    pe.wait_ge(q("biased_residual_ready"), s + 1)
                    if s >= 1:
                        pe.wait_ge(q("norm4_done"), s)
                    for h in range(2):
                        n = 2 * s + h
                        pe.matmul(bk[0][:, h * D:(h + 1) * D], ident, xbs[:, h, :], start=True, stop=False)
                        pe.wait_ge(q("attention_copied"), n + 1)
                        for k in range(DC):
                            i = pe.matmul(bk[0][:, h * D:(h + 1) * D], aof[h][:, k, :], woT[:, k, :], start=False, stop=k == DC - 1)
                        i.then_inc(q("projection_summed"), 1)
                if 0 <= b < 8:
                    tr4(bk[4], x5s[b % 2], "norm5_done", b + 1, "x5_turned", [("x4_copied", b + 1)], strided=True)
                if s < 7:
                    attend(s + 1, 0)

        @block.vector
        def _(v):
            def chain(i):
                link[0] += 1
                i.then_inc(q("vector_written"), 1)
                v.wait_ge(q("vector_written"), link[0])
            link = [0]

            v.wait_ge(q("loaded_value_weight"), 32)
            v.tensor_scalar(bh[:], bdv[:], 0.5, None, ALU.mult).then_inc(q("half_biases_ready"), 1)

            def bias_rows():
                v.wait_ge(q("loaded_constants"), 48)
                v.wait_ge(q("loaded_xattn_weights"), 144)
                for l in range(2):
                    for k in range(DC):
                        i = v.tensor_scalar(bqb[l][:, k, :], C["ones"], bq[l][:, k:k + 1], None, ALU.mult)
                    i.then_inc(q("bias_spread"), 1)

            def stats(k, m, src, ready=None):
                p = m % 2
                if ready:
                    v.wait_ge(q(ready), m + 1)
                for h in range(2):
                    i = v.bn_stats(st[k][:, p, h, :], src(h))
                chain(i)
                if m >= 2:
                    v.wait_ge(q(f"shift{k}_ready"), m - 1)
                for h in range(2):
                    i = v.bn_aggr(mv[k][:, p, h, :], st[k][:, p, h, :])
                i.then_inc(q(f"moments{k}_ready"), 1)

            def row_max(b, ready, done):
                v.wait_ge(q(ready), b + 1)
                v.tensor_reduce(nm[:, b % 2, :], bk[5][:, 0:2 * TK].rearrange("p (h n) -> p h n", h=2), AX.X, ALU.max, negate=True
                                ).then_inc(q(done), 1)

            def attended(b, pv, y, free, k):
                v.wait_ge(q(pv), b + 1)
                if b >= 2:
                    v.wait_ge(q(free), b - 1)
                chain(v.reciprocal(rc[:, b % 2, :], sm[:, b % 2, :]))
                for h in range(2):
                    i = v.scalar_tensor_tensor(out=y2[b % 2][:, h, :], in0=bk[7][:, h * D:(h + 1) * D], scalar=rc[:, b % 2, h:h + 1],
                                               in1=xs[b % 2][:, h, :], op0=ALU.mult, op1=ALU.add)
                i.then_inc(q(y), 1)
                v.wait_ge(q(y), b + 1)
                stats(k, b, lambda h: y2[b % 2][:, h, :])

            for s in range(B + 3):
                if 1 <= s <= B:
                    stats(0, s - 1, lambda h: bk[2][:, h * D:(h + 1) * D], "y1_turned")
                if s < B:
                    v.wait_ge(q("tanh_ready"), s + 1)
                    v.wait_ge(q("half_value_ready"), s + 1)
                    v.scalar_tensor_tensor(out=dv1, in0=th, scalar=1.0, in1=vb[:], op0=ALU.add, op1=ALU.mult
                                    ).then_inc(q("delta_value_ready"), 1)
                    v.wait_ge(q("delta_value_ready"), s + 1)
                    v.wait_ge(q("decay_ready"), s + 1)
                    for c in range(DC):
                        i = v.tensor_tensor_scan(hs[:, c, :], a1[:, c, :], dv1[:, c, :], 0.0, ALU.mult, ALU.add)
                    i.then_inc(q("state_ready"), 1)
                    v.wait_ge(q("state_ready"), s + 1)
                    if s >= 2:
                        v.wait_ge(q("y1_turned"), s - 1)
                    if s < 3:
                        v.wait_ge(q(f"loaded_x{s}"), 16)
                    v.tensor_tensor(y1[s % 2][:], hs, xf[:, :, s * T:(s + 1) * T], ALU.add).then_inc(q("y1_ready"), 1)
                if s == 0:
                    bias_rows()
                if 2 <= s <= B + 1:
                    attended(s - 2, "attended0_summed", "y2_ready", "norm2_done", 1)
                if 1 <= s <= B:
                    row_max(s - 1, "scores0_summed", "max0_ready")

            def R(a):
                return rA[:, a * 128:(a + 1) * 128].rearrange("p (n e) -> p n e", e=E0)
            sc_ = route
            k2 = NT * 2

            def over(x, w=E0):
                return x.unsqueeze(2).to_broadcast([P, x.shape[1], w])
            v.wait_ge(q("logits_summed"), B)
            lg = bk[6][:, 256:384].rearrange("p (n e) -> p n e", e=E0)
            chain(v.tensor_reduce(sc_[:, 0, 0:NT], lg, AX.X, ALU.max))
            v.tensor_tensor(R(0), lg, over(sc_[:, 0, 0:NT]), ALU.subtract).then_inc(q("logits_shifted"), 1)
            v.wait_ge(q("logits_exp_ready"), 1)
            chain(v.tensor_reduce(sc_[:, 1, 0:NT], R(1), AX.X, ALU.add))
            chain(v.reciprocal(sc_[:, 2, 0:NT], sc_[:, 1, 0:NT]))
            chain(v.tensor_tensor(R(2), R(1), over(sc_[:, 2, 0:NT]), ALU.mult))
            w8 = C["w8"].rearrange("p (n e) -> p n e", e=E0)
            M = rA[:, 1024:1280].rearrange("p (n e) -> p n e", e=E0)
            top = sc_[:, 3, 0:k2]
            c8 = sc_[:, 4, 0:k2]
            for k in range(2):
                a, b_ = k * NT, (k + 1) * NT
                chain(v.tensor_reduce(top[:, a:b_], R(2), AX.X, ALU.max))
                chain(v.tensor_tensor(R(3), R(2), over(top[:, a:b_]), ALU.is_equal))
                chain(v.tensor_tensor(R(4), R(3), w8, ALU.mult))
                chain(v.tensor_reduce(c8[:, a:b_], R(4), AX.X, ALU.max))
                chain(v.tensor_tensor(M[:, a:b_, :], w8, over(c8[:, a:b_]), ALU.is_equal))
                if k == 0:
                    chain(v.scalar_tensor_tensor(out=R(2), in0=M[:, 0:NT, :], scalar=-2.0, in1=R(2), op0=ALU.mult, op1=ALU.add))
            v.tensor_copy(rMb, rA[:, 1024:1280]).then_inc(q("choices_ready"), 1)
            v.wait_ge(q("ranks_summed"), 1)
            totE = rA[:, 1280:1536]
            incl = rA[:, 1536:1792]
            chain(v.tensor_copy(totE.rearrange("p (e n) -> p n e", e=E0), bk[0][:, 256:512].rearrange("p (n e) -> p n e", e=E0)))
            chain(v.tensor_tensor_scan(incl, C["smask"], totE, 0.0, ALU.mult, ALU.add))
            chain(v.tensor_tensor(incl, incl, totE, ALU.subtract))
            loc8 = rA[:, 1792:2048].rearrange("p (n e) -> p n e", e=E0)
            chain(v.tensor_tensor(loc8, bk[0][:, 0:256].rearrange("p (n e) -> p n e", e=E0), incl.rearrange("p (e n) -> p n e", e=E0), ALU.add))
            chain(v.tensor_tensor(loc8, loc8, M, ALU.mult))
            loc, hi, lo, keep = (sc_[:, i, 0:k2] for i in (5, 6, 7, 8))
            chain(v.tensor_reduce(loc, loc8, AX.X, ALU.add))
            chain(v.tensor_scalar(hi, loc, float(P), None, ALU.is_ge))
            for j in range(2, ET):
                chain(v.scalar_tensor_tensor(out=hi, in0=loc, scalar=float(P * j), in1=hi, op0=ALU.is_ge, op1=ALU.add))
            chain(v.scalar_tensor_tensor(out=lo, in0=hi, scalar=-float(P), in1=loc, op0=ALU.mult, op1=ALU.add))
            chain(v.scalar_tensor_tensor(out=hi, in0=c8, scalar=-float(ET), in1=hi, op0=ALU.mult, op1=ALU.add))
            chain(v.tensor_scalar(keep, loc, float(CAP), None, ALU.is_lt))
            chain(v.tensor_scalar(hi, hi, float(ET * E0) + 1000.0, None, ALU.add))
            chain(v.scalar_tensor_tensor(out=hi, in0=keep, scalar=-1000.0, in1=hi, op0=ALU.mult, op1=ALU.add))
            ohf = rA[:, 2048:2048 + 1280].rearrange("p (n c) -> p n c", n=k2)
            chain(v.tensor_tensor(ohf, C["iota"][:, 0:NST].unsqueeze(1).to_broadcast([P, k2, NST]), over(hi, NST), ALU.is_equal))
            v.tensor_copy(ohh[:, :, 2 * NST:3 * NST], ohf)
            v.tensor_scalar(ohh[:, :, NST:2 * NST], ohf, C["pcol"], None, ALU.mult)
            v.tensor_tensor(ohh[:, :, 0:NST], ohf, over(C["acon"], NST), ALU.mult)
            for h in range(4):
                r = slice(h * k2 // 4, (h + 1) * k2 // 4)
                v.tensor_tensor(ohl[:, r, :], C["iota"].unsqueeze(1).to_broadcast([P, k2 // 4, P]), over(lo[:, r], P), ALU.is_equal
                                ).then_inc(q("onehots_ready"), 1)
            v.wait_ge(q("slot_table_summed"), 1)
            tb = table
            chain(v.tensor_copy(tb[:, 0:3 * NST], bk[1][:, 0:3 * NST]))
            chain(v.tensor_tensor(tb[:, 120:160], tb[:, 0:40], tb[:, 40:80], ALU.add))
            chain(v.tensor_scalar(tb[:, 160:200], tb[:, 120:160], float(S), -float(S), ALU.is_ge, ALU.mult))
            v.tensor_tensor(idx[:, 0, :], tb[:, 120:160], tb[:, 160:200], ALU.add)
            chain(v.scalar_tensor_tensor(out=tb[:, 200:240], in0=tb[:, 80:120], scalar=-BIG, in1=tb[:, 120:160], op0=ALU.mult, op1=ALU.add))
            v.tensor_scalar(idx[:, 1, :], tb[:, 200:240], BIG, None, ALU.add).then_inc(q("slot_index_ready"), 1)
            g0 = sc_[:, 9, 0:k2]
            den = sc_[:, 10, 0:NT]
            chain(v.tensor_tensor(g0, top, keep, ALU.mult))
            chain(v.tensor_tensor(den, g0[:, 0:NT], g0[:, NT:k2], ALU.add))
            chain(v.tensor_scalar(den, den, 1e-9, None, ALU.max))
            chain(v.reciprocal(sc_[:, 11, 0:NT], den))
            for k in range(2):
                i = v.tensor_tensor(gate[:, k, :], g0[:, k * NT:(k + 1) * NT], sc_[:, 11, 0:NT], ALU.mult)
            chain(i)

            def inp_low(e, j):
                n = e * ET + j
                v.wait_ge(q("inputs_high"), n + 1)
                v.tensor_tensor(inpL[:, :, j * P:(j + 1) * P], bk[6 + n % 2][:, 0:D].rearrange("p (c t) -> p c t", c=DC),
                                inpH4[:, :, j * P:(j + 1) * P], ALU.subtract).then_inc(q("inputs_low"), 1)

            def hid_low(n):
                u = n % 8
                f, hf = u % FC, u // FC
                v.wait_ge(q("hidden_high"), n + 1)
                v.tensor_tensor(hidL[:, f, hf * HALF:(hf + 1) * HALF], hid[n % 2], hidH4[:, f, hf * HALF:(hf + 1) * HALF],
                                ALU.subtract).then_inc(q("hidden_low"), 1)

            def win_low(e, c):
                v.wait_ge(q("w_in_high"), DC * e + c + 1)
                if e == 0:
                    v.wait_ge(q("u_weight_summed"), 1)
                i = v.tensor_tensor(winL[:, c, :], win[:, c, :], winH4[:, c, :], ALU.subtract)
                if c == DC - 1:
                    i.then_inc(q("w_in_low"), 1)

            def back(n):
                v.wait_ge(q("returned_summed"), n + 1)
                if n >= 4:
                    v.wait_ge(q(f"scattered{n % 4}"), 16 * (n // 4))
                v.tensor_copy(oe[n % 4], bk[4 + n % 2][:, 0:D]).then_inc(q("returned_copied"), 1)

            for c in range(DC):
                win_low(0, c)
            for j in range(3):
                inp_low(0, j)
            for e in range(E0):
                for u in range(8):
                    n = 8 * e + u
                    if n == FC:
                        inp_low(0, 3)
                        inp_low(0, 4)
                    v.wait_ge(q("gelu_ready"), n + 1)
                    if n >= 2:
                        v.wait_ge(q("hidden_low"), n - 1)
                    v.tensor_tensor(hid[n % 2], ge[n % 2], bk[2 + n % 2][:, 0:HALF], ALU.mult).then_inc(q("hidden_ready"), 1)
                    if u >= 1:
                        hid_low(n - 1)
                    if u == 2:
                        v.wait_ge(q("w_out_high"), e + 1)
                        v.tensor_tensor(wouL, wou, wouH4, ALU.subtract).then_inc(q("w_out_low"), 1)
                hid_low(8 * e + 7)
                if e + 1 < E0:
                    inp_low(e + 1, 0)
                    inp_low(e + 1, 1)
                for j in range(ET):
                    back(e * ET + j)
                    if e + 1 < E0 and j < 3:
                        inp_low(e + 1, j + 2)
                    if e + 1 < E0 and j in (2, 3):
                        win_low(e + 1, j - 2)

            def returned(m):
                v.wait_ge(q(f"loaded_returned{m % 2}"), 32 * (m // 2 + 1))
                if m >= 2:
                    v.wait_ge(q("norm3_done"), m - 1)
                for h, n in enumerate(tiles_of(m)):
                    i = v.scalar_tensor_tensor(out=y3[m % 2][:, h, :], in0=yb[m % 2][:, h, 0, :], scalar=gate[:, 0, n:n + 1], in1=xt[:, n, :],
                                               op0=ALU.mult, op1=ALU.add)
                chain(i)
                for h, n in enumerate(tiles_of(m)):
                    i = v.scalar_tensor_tensor(out=y3[m % 2][:, h, :], in0=yb[m % 2][:, h, 1, :], scalar=gate[:, 1, n:n + 1], in1=y3[m % 2][:, h, :],
                                               op0=ALU.mult, op1=ALU.add)
                i.then_inc(q("y3_ready"), 1)
                v.wait_ge(q("y3_ready"), m + 1)
                stats(2, m, lambda h: y3[m % 2][:, h, :])

            def distances(m):
                g, i_ = m // 4, m % 4
                Q = (qa, qa2)[g]
                t = 2 * i_ + 1
                v.wait_ge(q("qu_copied"), 2 * m + 2)
                if m >= 2:
                    v.wait_ge(q("distances_ready"), m - 1)
                v.tensor_tensor(dif[m % 2][:, 6 * D:(6 + t) * D].rearrange("p (s n) -> p s n", s=t), Q[:, t:t + 1, :].to_broadcast([P, t, D]), Q[:, 0:t, :],
                                ALU.subtract).then_inc(q("odd_differences_ready"), 1)

            def reduce_distances(m):
                g, i_ = m // 4, m % 4
                v.wait_ge(q("squares_ready"), 7 * g + 2 * i_ + 1)
                if g == 1 and i_ == 0:
                    v.wait_ge(q("kernels_ready"), 7)
                for t in (2 * i_, 2 * i_ + 1):
                    if t:
                        a = t * (t - 1) // 2
                        o = 0 if t % 2 == 0 else 6 * D
                        i = v.tensor_reduce(dsq[:, a:a + t, :], dif[m % 2][:, o:o + t * D].rearrange("p (s h d) -> p s h d", h=NH, d=HD), AX.X, ALU.add)
                i.then_inc(q("distances_ready"), 1)

            def weights(g):
                a = att[g]
                at3 = a.rearrange("p (t s h) -> p t s h", t=B, s=B)
                v.wait_ge(q("kernels_ready"), 7 * g + 7)
                for t in range(B):
                    i = v.memset(at3[:, t, t, :], 1.0)
                    if t:
                        i = v.tensor_copy(at3[:, 0:t, t, :], at3[:, t, 0:t, :])
                chain(i)
                chain(v.tensor_reduce(zz[:], a.rearrange("p (t s h) -> p t h s", t=B, s=B), AX.X, ALU.add))
                chain(v.reciprocal(rz[:], zz[:]))
                chain(v.tensor_tensor(at3, at3, rz[:].unsqueeze(2).to_broadcast([P, B, B, NH]), ALU.mult))

            def weigh(s, h):
                g = s // 4
                n = 2 * s + h
                t = 2 * (s % 4) + h
                if n >= 2:
                    v.wait_ge(q("attention_summed"), n - 1)
                w = att[g].rearrange("p (t s h) -> p t s h", t=B, s=B)[:, t, :, :]
                v.tensor_tensor(prod[n % 2].rearrange("p s (h d) -> p (s h) d", d=HD),
                                (ua, ua2)[g].rearrange("p s (h d) -> p (s h) d", d=HD),
                                w.rearrange("p s h -> p (s h)").unsqueeze(2).to_broadcast([P, B * NH, HD]), ALU.mult
                                                ).then_inc(q(("products_ready", "products_unhalved")[h]), 1)
                if h == 1:
                    v.wait_ge(q("products_unhalved"), s + 1)
                    v.tensor_tensor(prod[h][:, 0:B // 2, :], prod[h][:, 0:B // 2, :], prod[h][:, B // 2:B, :], ALU.add
                                    ).then_inc(q("products_ready"), 1)

            def on_hyperplanes(b):
                v.wait_ge(q("x5_copied"), b + 1)
                if b >= 1:
                    v.wait_ge(q("hash_summed"), b)
                for h in range(2):
                    i = v.tensor_tensor(eh[:, :, h, :], hyp[:], emb[:, :, h:h + 1].to_broadcast([P, DC, NB6]), ALU.mult)
                i.then_inc(q("hyperplane_products_ready"), 1)

            def V6(i):
                return rt[:, i, :].rearrange("p (h n) -> p h n", h=2)

            def projections(b):
                v.wait_ge(q("hash_summed"), b + 1)
                v.tensor_copy(rt[:, 0, :], bk[6][:, 256:256 + 2 * NB6]).then_inc(q("hash_copied"), 1)

            e1, mn, fc, fl, bt, e2 = (rt[:, i, 0:2] for i in (3, 4, 5, 6, 7, 8))

            def hash_bits(b):
                v.wait_ge(q("hash_copied"), b + 1)
                v.scalar_tensor_tensor(out=rt[:, 1, :], in0=rt[:, 0, :], scalar=0.0, in1=C["p6"], op0=ALU.is_gt, op1=ALU.mult)
                chain(v.scalar_tensor_tensor(out=rt[:, 2, :], in0=rt[:, 0, :], scalar=-1.0, in1=rt[:, 0, :], op0=ALU.mult, op1=ALU.max))
                v.tensor_reduce(e1, V6(1), AX.X, ALU.add)
                chain(v.tensor_reduce(mn, V6(2), AX.X, ALU.min))

            def hash_flip(b):
                chain(v.tensor_tensor(V6(9), V6(2), over(mn, NB6), ALU.is_equal))
                chain(v.tensor_tensor(rt[:, 9, :], rt[:, 9, :], C["w6"], ALU.mult))
                chain(v.tensor_reduce(fc, V6(9), AX.X, ALU.max))
                chain(v.tensor_tensor(V6(9), C["w6"].rearrange("p (h n) -> p h n", h=2), over(fc, NB6), ALU.is_equal))
                v.tensor_tensor(rt[:, 10, :], rt[:, 9, :], C["p6"], ALU.mult)
                chain(v.tensor_tensor(rt[:, 11, :], rt[:, 9, :], rt[:, 1, :], ALU.mult))
                v.tensor_reduce(fl, V6(10), AX.X, ALU.add)
                chain(v.tensor_reduce(bt, V6(11), AX.X, ALU.add))
                chain(v.tensor_tensor(e2, e1, fl, ALU.add))
                chain(v.scalar_tensor_tensor(out=e2, in0=bt, scalar=-2.0, in1=e2, op0=ALU.mult, op1=ALU.add))
                if b >= 2:
                    v.wait_ge(q("gathered_chunk_weights0"), 32 * (b - 1))
                    v.wait_ge(q("gathered_chunk_weights1"), 32 * (b - 1))
                wi = widx[b % 2][:].rearrange("p (h k) -> p h k", k=2)
                v.tensor_scalar(wi[:, :, 0], e1, float(P), C["pcol"], ALU.mult, ALU.add)
                v.tensor_scalar(wi[:, :, 1], e2, float(P), C["pcol"], ALU.mult, ALU.add).then_inc(q("chunk_index_ready"), 1)

            returned(0)
            returned(1)
            for f in range(8):
                if f < 6:
                    returned(f + 2)
                if f == 7:
                    weights(0)
                if 1 <= f:
                    distances(f - 1)
                if 2 <= f:
                    reduce_distances(f - 2)
            weigh(0, 0)
            for s in range(8 + 3):
                b = s - 1
                if 2 <= s <= 9:
                    on_hyperplanes(s - 2)
                if s < 8:
                    weigh(s, 1)
                if 2 <= s <= 9:
                    projections(s - 2)
                if 0 <= b < 8:
                    row_max(b, "scores1_summed", "max1_ready")
                if 8 <= s <= 9:
                    hash_bits(s - 2)
                    hash_flip(s - 2)
                if s < 7:
                    weigh(s + 1, 0)
                if s == 0:
                    distances(7)
                if 0 <= b < 8:
                    attended(b, "attended1_summed", "y5_ready", "norm5_done", 4)
                if s < 2:
                    reduce_distances(s + 6)
                if s >= 3:
                    d = s - 3
                    v.wait_ge(q("ffn_summed"), 2 * d + 2)
                    if d >= 2:
                        v.wait_ge(q("norm6_done"), d - 1)
                    v.scalar_tensor_tensor(out=y6b[d % 2][:].rearrange("p h n -> p (h n)"), in0=bk[1][:], scalar=0.5,
                                           in1=x5s[d % 2][:].rearrange("p h n -> p (h n)"), op0=ALU.mult, op1=ALU.add
                                                           ).then_inc(q("y6_ready"), 1)
                    v.wait_ge(q("y6_ready"), d + 1)
                    stats(5, d, lambda h: y6b[d % 2][:, h, :])
                if 2 <= s < 8:
                    hash_bits(s - 2)
                if s < 8:
                    v.wait_ge(q("projection_summed"), 2 * s + 2)
                    stats(3, s, lambda h: bk[0][:, h * D:(h + 1) * D])
                if 2 <= s < 8:
                    hash_flip(s - 2)
                if s == 2:
                    weights(1)


def kernel(x, ctx_768, L0_attn_W_delta, L0_attn_b_delta, L0_attn_W_value, L0_attn_b_value, L0_xattn_Wq, L0_xattn_bq, L0_xattn_Wk,
           L0_xattn_bk, L0_xattn_Wv, L0_xattn_bv, L0_ffn_Wg, L0_ffn_W_in, L0_ffn_W_out, L1_attn_q_weight, L1_attn_v_weight, L1_attn_out_w,
           L1_attn_out_b, L1_xattn_Wq, L1_xattn_bq, L1_xattn_Wk, L1_xattn_bk, L1_xattn_Wv, L1_xattn_bv, L1_ffn_expert_weights,
           L1_ffn_hyperplanes):
    import concourse.bacc as bacc
    from concourse.bass_utils import run_bass_kernel_spmd
    import ml_dtypes

    c = np.ascontiguousarray
    n = np.asarray
    arrays = {
        "xT": c(n(x).reshape(S, D).T), "ctxT": c(n(ctx_768).reshape(B * TK, CD).T),
        "Wd": c(n(L0_attn_W_delta).T), "Wv": c(n(L0_attn_W_value).T),
        "bdv": c(np.stack([n(L0_attn_b_delta), n(L0_attn_b_value)]).reshape(2, DC, P).transpose(2, 0, 1)),
        "Wq0": c(n(L0_xattn_Wq)), "bq0": c(n(L0_xattn_bq).reshape(DC, P).T), "Wk0": c(n(L0_xattn_Wk).T), "bk0": c(n(L0_xattn_bk)[None]),
        "Wvx0": c(n(L0_xattn_Wv).T), "bvx0": c(n(L0_xattn_bv)[None]),
        "Wq1": c(n(L1_xattn_Wq).T), "bq1": c(n(L1_xattn_bq).reshape(DC, P).T), "Wk1": c(n(L1_xattn_Wk)), "bk1": c(n(L1_xattn_bk)[None]),
        "Wvx1": c(n(L1_xattn_Wv)), "bvx1": c(n(L1_xattn_bv)[None]),
        "Wg": c(n(L0_ffn_Wg)), "W_in": c(n(L0_ffn_W_in)), "W_out": c(n(L0_ffn_W_out)),
        "qw": c(n(L1_attn_q_weight).reshape(D, D)), "qwT": c(n(L1_attn_q_weight).reshape(D, D).T),
        "vw": c(n(L1_attn_v_weight).reshape(D, D)), "woT": c(n(L1_attn_out_w).T),
        "obr": c(np.broadcast_to(n(L1_attn_out_b), (P, D))), "hyp": c(n(L1_ffn_hyperplanes)),
        "EW": c(n(L1_ffn_expert_weights).reshape(64 * P, 2 * D)),
        "cf": shape_constants(), "ones1": np.ones((1, B * TK), np.float32),
        "ltri": np.triu(np.ones((P, P), np.float32), 1).astype(ml_dtypes.bfloat16),
        "onesb": np.ones((P, P), ml_dtypes.bfloat16),
    }
    nc = bacc.Bacc("TRN2", target_bir_lowering=False, num_devices=1)
    A = {k: nc.dram_tensor(k, a.shape, mybir.dt.from_np(a.dtype), kind="ExternalInput").ap() for k, a in arrays.items()}
    out = nc.dram_tensor("out", (B, T, D), F32, kind="ExternalOutput").ap()
    Y = nc.dram_tensor("expert_rows", (2 * S, D), F32, kind="Internal").ap()
    X2 = nc.dram_tensor("x2_rows", (S, D), F32, kind="Internal").ap()
    program(nc, A, out, Y, X2)
    r = run_bass_kernel_spmd(nc, [arrays], core_ids=[0])
    return r.results[0]["out"]
```
